# Optimizing a Trainium2 kernel written in Bass

```python
import numpy as np
import jax
import jax.numpy as jnp

def _softmax(x, axis=-1):
    return jax.nn.softmax(x, axis=axis)

def _gelu(x):
    return jax.nn.gelu(x, approximate=True)

def _silu(x):
    return jax.nn.silu(x)

def _sigmoid(x):
    return jax.nn.sigmoid(x)

def _layernorm(x, axis=-1, eps=1e-05):
    m = jnp.mean(x, axis=axis, keepdims=True)
    v = jnp.var(x, axis=axis, keepdims=True)
    return (x - m) / jnp.sqrt(v + eps)

def _scatter_add(tgt, idx, src, axis=0):
    return tgt.at[idx].add(src)

def _segment_sum(src, seg, n):
    return jax.ops.segment_sum(src, seg, n)
kernel_name = 'mk_vit_tower_d1_tok_img256_r4_bb9d0c'

def setup_inputs(seed: int=0):
    np.random.seed(seed)
    _w = jnp.asarray

    def _rec_inputs():
        import jax
        import jax.numpy as jnp
        _rk = jax.random.key(seed)
        x = -0.000798584 + 1.00089 * jax.random.normal(jax.random.fold_in(_rk, 1), (32, 64, 75, 3), jnp.float32)
        return x
    x = _rec_inputs()

    def _L0_tok_setup():
        import jax, jax.numpy as jnp
        import numpy as np
        EPS = 1e-05
        B, T, V = (32, 64, 75)
        DIMS = [3, 128, 128, 64]

        def _layer(x, A, W, b, g, be, m, v, relu):
            x = jnp.einsum('btvc,co->btvo', x, W)
            x = jnp.einsum('uv,btvo->btuo', A, x)
            x = x + b
            x = (x - m) * (g * jax.lax.rsqrt(v + EPS)) + be
            if relu:
                x = jax.nn.relu(x)
            return x
        key = jax.random.key(seed)
        ks = jax.random.split(key, 32)
        inp = {'x': jax.random.normal(ks[0], (B, T, V, DIMS[0]), dtype=jnp.float32), 'A': jax.random.uniform(ks[1], (V, V), dtype=jnp.float32) / V}
        ki = 2
        for i in range(3):
            cin, cout = (DIMS[i], DIMS[i + 1])
            bound = float(np.sqrt(6.0 / (cin + cout)))
            inp[f'W{i}'] = jax.random.uniform(ks[ki], (cin, cout), minval=-bound, maxval=bound, dtype=jnp.float32)
            ki += 1
            inp[f'b{i}'] = jnp.zeros((cout,), dtype=jnp.float32)
            inp[f'g{i}'] = jnp.ones((cout,), dtype=jnp.float32)
            inp[f'be{i}'] = jnp.zeros((cout,), dtype=jnp.float32)
            inp[f'm{i}'] = 0.1 * jax.random.normal(ks[ki], (cout,), dtype=jnp.float32)
            ki += 1
            inp[f'v{i}'] = jax.random.uniform(ks[ki], (cout,), minval=0.5, maxval=1.5, dtype=jnp.float32)
            ki += 1
        return inp
    _L0_tok_all = _L0_tok_setup()
    _L0_tok_in = {k: v for k, v in _L0_tok_all.items() if k in ('A', 'W0', 'b0', 'g0', 'be0', 'm0', 'v0', 'W1', 'b1', 'g1', 'be1', 'm1', 'v1', 'W2', 'b2', 'g2', 'be2', 'm2', 'v2')}
    del _L0_tok_all

    def _L0_attn_setup():
        import jax, jax.numpy as jnp
        import numpy as np
        LN_EPS = 1e-05

        def _layernorm(x, w, b):
            mu = jnp.mean(x, axis=-1, keepdims=True)
            var = jnp.mean(jnp.square(x - mu), axis=-1, keepdims=True)
            return (x - mu) * jax.lax.rsqrt(var + LN_EPS) * w + b

        def _mamba_mixer(h, in_proj_w, conv_w, conv_b, ssm_B, ssm_C, ssm_D, out_proj_w):
            B, L, D = h.shape
            xz = jnp.einsum('bld,ed->ble', h, in_proj_w)
            xc, z = jnp.split(xz, 2, axis=-1)
            xc_t = jnp.transpose(xc, (0, 2, 1))
            xc_t = jax.lax.conv_general_dilated(xc_t, conv_w, window_strides=(1,), padding=[(conv_w.shape[-1] - 1, 0)], feature_group_count=D, dimension_numbers=('NCH', 'OIH', 'NCH'))
            xc_t = xc_t + conv_b[None, :, None]
            xc = jax.nn.silu(jnp.transpose(xc_t, (0, 2, 1)))
            z = jax.nn.silu(z)
            bc = jnp.sum(ssm_B * ssm_C, axis=-1)
            y = jnp.cumsum(xc, axis=1) * bc + xc * ssm_D
            out = jnp.einsum('bld,ed->ble', y * z, out_proj_w)
            return out
        key = jax.random.key(seed)
        ks = jax.random.split(key, 10)
        B, L, D = (8, 1024, 64)
        Dff, S, K = (256, 8, 3)
        s = 0.02
        return {'x': jax.random.normal(ks[0], (B, L, D), jnp.float32), 'ln1_w': jnp.ones((D,), jnp.float32), 'ln1_b': jnp.zeros((D,), jnp.float32), 'in_proj_w': jax.random.normal(ks[1], (2 * D, D), jnp.float32) * s, 'conv_w': jax.random.normal(ks[2], (D, 1, K), jnp.float32) * s, 'conv_b': jax.random.normal(ks[3], (D,), jnp.float32) * s, 'ssm_B': jax.random.normal(ks[4], (D, S), jnp.float32) * s, 'ssm_C': jax.random.normal(ks[5], (D, S), jnp.float32) * s, 'ssm_D': jnp.ones((D,), jnp.float32), 'out_proj_w': jax.random.normal(ks[6], (D, D), jnp.float32) * s, 'ln2_w': jnp.ones((D,), jnp.float32), 'ln2_b': jnp.zeros((D,), jnp.float32), 'fc1_w': jax.random.normal(ks[7], (Dff, D), jnp.float32) * s, 'fc1_b': jnp.zeros((Dff,), jnp.float32), 'fc2_w': jax.random.normal(ks[8], (D, Dff), jnp.float32) * s, 'fc2_b': jnp.zeros((D,), jnp.float32)}
    _L0_attn_all = _L0_attn_setup()
    _L0_attn_in = {k: v for k, v in _L0_attn_all.items() if k in ('ln1_w', 'ln1_b', 'in_proj_w', 'conv_w', 'conv_b', 'ssm_B', 'ssm_C', 'ssm_D', 'out_proj_w', 'ln2_w', 'ln2_b', 'fc1_w', 'fc1_b', 'fc2_w', 'fc2_b')}
    del _L0_attn_all

    def _L0_ffn_setup():
        import jax, jax.numpy as jnp
        import numpy as np
        B, T, C = (64, 96, 64)
        NH, NKV = (4, 2)
        HD = C // NH
        NREP = NH // NKV
        NE, TOPK = (8, 2)
        HID = int(8 / 3 * C)
        EPS_RMS = 1e-06

        def _rope_tables(t_len):
            inv_freq = 1.0 / 10000.0 ** (np.arange(0, HD, 2, dtype=np.float32) / HD)
            t = np.arange(t_len, dtype=np.float32)
            freqs = np.outer(t, inv_freq)
            emb = np.concatenate([freqs, freqs], axis=-1)
            return (jnp.asarray(np.cos(emb)), jnp.asarray(np.sin(emb)))

        def _rotate_half(x):
            h = x.shape[-1] // 2
            return jnp.concatenate([-x[..., h:], x[..., :h]], axis=-1)

        def _rmsnorm(v, w):
            return v * jax.lax.rsqrt(jnp.mean(v * v, axis=-1, keepdims=True) + EPS_RMS) * w
        key = jax.random.key(seed)
        ks = jax.random.split(key, 10)
        s = lambda k, shape: jax.random.normal(k, shape, jnp.float32) * 0.02
        return {'x': jax.random.normal(ks[0], (B, T, C), jnp.float32), 'ln1_w': jnp.ones((C,), jnp.float32), 'ln2_w': jnp.ones((C,), jnp.float32), 'wq': s(ks[1], (NH * HD, C)), 'wk': s(ks[2], (NKV * HD, C)), 'wv': s(ks[3], (NKV * HD, C)), 'wo': s(ks[4], (C, C)), 'router_w': s(ks[5], (NE, C)), 'w1': s(ks[6], (NE, HID, C)), 'w2': s(ks[7], (NE, C, HID)), 'w3': s(ks[8], (NE, HID, C))}
    _L0_ffn_all = _L0_ffn_setup()
    _L0_ffn_in = {k: v for k, v in _L0_ffn_all.items() if k in ('ln1_w', 'ln2_w', 'wq', 'wk', 'wv', 'wo', 'router_w', 'w1', 'w2', 'w3')}
    del _L0_ffn_all
    return {'x': x, 'L0_tok_A': _L0_tok_in['A'], 'L0_tok_W0': _L0_tok_in['W0'], 'L0_tok_b0': _L0_tok_in['b0'], 'L0_tok_g0': _L0_tok_in['g0'], 'L0_tok_be0': _L0_tok_in['be0'], 'L0_tok_m0': _L0_tok_in['m0'], 'L0_tok_v0': _L0_tok_in['v0'], 'L0_tok_W1': _L0_tok_in['W1'], 'L0_tok_b1': _L0_tok_in['b1'], 'L0_tok_g1': _L0_tok_in['g1'], 'L0_tok_be1': _L0_tok_in['be1'], 'L0_tok_m1': _L0_tok_in['m1'], 'L0_tok_v1': _L0_tok_in['v1'], 'L0_tok_W2': _L0_tok_in['W2'], 'L0_tok_b2': _L0_tok_in['b2'], 'L0_tok_g2': _L0_tok_in['g2'], 'L0_tok_be2': _L0_tok_in['be2'], 'L0_tok_m2': _L0_tok_in['m2'], 'L0_tok_v2': _L0_tok_in['v2'], 'L0_attn_ln1_w': _L0_attn_in['ln1_w'], 'L0_attn_ln1_b': _L0_attn_in['ln1_b'], 'L0_attn_in_proj_w': _L0_attn_in['in_proj_w'], 'L0_attn_conv_w': _L0_attn_in['conv_w'], 'L0_attn_conv_b': _L0_attn_in['conv_b'], 'L0_attn_ssm_B': _L0_attn_in['ssm_B'], 'L0_attn_ssm_C': _L0_attn_in['ssm_C'], 'L0_attn_ssm_D': _L0_attn_in['ssm_D'], 'L0_attn_out_proj_w': _L0_attn_in['out_proj_w'], 'L0_attn_ln2_w': _L0_attn_in['ln2_w'], 'L0_attn_ln2_b': _L0_attn_in['ln2_b'], 'L0_attn_fc1_w': _L0_attn_in['fc1_w'], 'L0_attn_fc1_b': _L0_attn_in['fc1_b'], 'L0_attn_fc2_w': _L0_attn_in['fc2_w'], 'L0_attn_fc2_b': _L0_attn_in['fc2_b'], 'L0_ffn_ln1_w': _L0_ffn_in['ln1_w'], 'L0_ffn_ln2_w': _L0_ffn_in['ln2_w'], 'L0_ffn_wq': _L0_ffn_in['wq'], 'L0_ffn_wk': _L0_ffn_in['wk'], 'L0_ffn_wv': _L0_ffn_in['wv'], 'L0_ffn_wo': _L0_ffn_in['wo'], 'L0_ffn_router_w': _L0_ffn_in['router_w'], 'L0_ffn_w1': _L0_ffn_in['w1'], 'L0_ffn_w2': _L0_ffn_in['w2'], 'L0_ffn_w3': _L0_ffn_in['w3']}

def reference(x, L0_tok_A, L0_tok_W0, L0_tok_b0, L0_tok_g0, L0_tok_be0, L0_tok_m0, L0_tok_v0, L0_tok_W1, L0_tok_b1, L0_tok_g1, L0_tok_be1, L0_tok_m1, L0_tok_v1, L0_tok_W2, L0_tok_b2, L0_tok_g2, L0_tok_be2, L0_tok_m2, L0_tok_v2, L0_attn_ln1_w, L0_attn_ln1_b, L0_attn_in_proj_w, L0_attn_conv_w, L0_attn_conv_b, L0_attn_ssm_B, L0_attn_ssm_C, L0_attn_ssm_D, L0_attn_out_proj_w, L0_attn_ln2_w, L0_attn_ln2_b, L0_attn_fc1_w, L0_attn_fc1_b, L0_attn_fc2_w, L0_attn_fc2_b, L0_ffn_ln1_w, L0_ffn_ln2_w, L0_ffn_wq, L0_ffn_wk, L0_ffn_wv, L0_ffn_wo, L0_ffn_router_w, L0_ffn_w1, L0_ffn_w2, L0_ffn_w3):
    import jax
    import jax.numpy as jnp

    def _L0_tok_ref(x, A, W0, b0, g0, be0, m0, v0, W1, b1, g1, be1, m1, v1, W2, b2, g2, be2, m2, v2):
        import jax, jax.numpy as jnp
        import numpy as np
        EPS = 1e-05
        B, T, V = (32, 64, 75)
        DIMS = [3, 128, 128, 64]

        def _layer(x, A, W, b, g, be, m, v, relu):
            x = jnp.einsum('btvc,co->btvo', x, W)
            x = jnp.einsum('uv,btvo->btuo', A, x)
            x = x + b
            x = (x - m) * (g * jax.lax.rsqrt(v + EPS)) + be
            if relu:
                x = jax.nn.relu(x)
            return x
        x = _layer(x, A, W0, b0, g0, be0, m0, v0, relu=True)
        x = _layer(x, A, W1, b1, g1, be1, m1, v1, relu=True)
        x = _layer(x, A, W2, b2, g2, be2, m2, v2, relu=False)
        return x.mean(axis=2)

    def _L0_attn_ref(x, ln1_w, ln1_b, in_proj_w, conv_w, conv_b, ssm_B, ssm_C, ssm_D, out_proj_w, ln2_w, ln2_b, fc1_w, fc1_b, fc2_w, fc2_b):
        import jax, jax.numpy as jnp
        import numpy as np
        LN_EPS = 1e-05

        def _layernorm(x, w, b):
            mu = jnp.mean(x, axis=-1, keepdims=True)
            var = jnp.mean(jnp.square(x - mu), axis=-1, keepdims=True)
            return (x - mu) * jax.lax.rsqrt(var + LN_EPS) * w + b

        def _mamba_mixer(h, in_proj_w, conv_w, conv_b, ssm_B, ssm_C, ssm_D, out_proj_w):
            B, L, D = h.shape
            xz = jnp.einsum('bld,ed->ble', h, in_proj_w)
            xc, z = jnp.split(xz, 2, axis=-1)
            xc_t = jnp.transpose(xc, (0, 2, 1))
            xc_t = jax.lax.conv_general_dilated(xc_t, conv_w, window_strides=(1,), padding=[(conv_w.shape[-1] - 1, 0)], feature_group_count=D, dimension_numbers=('NCH', 'OIH', 'NCH'))
            xc_t = xc_t + conv_b[None, :, None]
            xc = jax.nn.silu(jnp.transpose(xc_t, (0, 2, 1)))
            z = jax.nn.silu(z)
            bc = jnp.sum(ssm_B * ssm_C, axis=-1)
            y = jnp.cumsum(xc, axis=1) * bc + xc * ssm_D
            out = jnp.einsum('bld,ed->ble', y * z, out_proj_w)
            return out
        h = _layernorm(x, ln1_w, ln1_b)
        x = x + _mamba_mixer(h, in_proj_w, conv_w, conv_b, ssm_B, ssm_C, ssm_D, out_proj_w)
        h = _layernorm(x, ln2_w, ln2_b)
        h = jax.nn.gelu(jnp.einsum('bld,fd->blf', h, fc1_w) + fc1_b, approximate=False)
        x = x + jnp.einsum('blf,df->bld', h, fc2_w) + fc2_b
        return x

    def _L0_ffn_ref(x, ln1_w, ln2_w, wq, wk, wv, wo, router_w, w1, w2, w3):
        import jax, jax.numpy as jnp
        import numpy as np
        B, T, C = (64, 96, 64)
        NH, NKV = (4, 2)
        HD = C // NH
        NREP = NH // NKV
        NE, TOPK = (8, 2)
        HID = int(8 / 3 * C)
        EPS_RMS = 1e-06

        def _rope_tables(t_len):
            inv_freq = 1.0 / 10000.0 ** (np.arange(0, HD, 2, dtype=np.float32) / HD)
            t = np.arange(t_len, dtype=np.float32)
            freqs = np.outer(t, inv_freq)
            emb = np.concatenate([freqs, freqs], axis=-1)
            return (jnp.asarray(np.cos(emb)), jnp.asarray(np.sin(emb)))

        def _rotate_half(x):
            h = x.shape[-1] // 2
            return jnp.concatenate([-x[..., h:], x[..., :h]], axis=-1)

        def _rmsnorm(v, w):
            return v * jax.lax.rsqrt(jnp.mean(v * v, axis=-1, keepdims=True) + EPS_RMS) * w
        Bx, Tx, Cx = x.shape
        h = _rmsnorm(x, ln1_w)
        q = (h @ wq.T).reshape(Bx, Tx, NH, HD).transpose(0, 2, 1, 3)
        k = (h @ wk.T).reshape(Bx, Tx, NKV, HD).transpose(0, 2, 1, 3)
        v = (h @ wv.T).reshape(Bx, Tx, NKV, HD).transpose(0, 2, 1, 3)
        cos, sin = _rope_tables(Tx)
        cos, sin = (cos[None, None], sin[None, None])
        q = q * cos + _rotate_half(q) * sin
        k = k * cos + _rotate_half(k) * sin
        k = jnp.repeat(k, NREP, axis=1)
        v = jnp.repeat(v, NREP, axis=1)
        scores = jnp.einsum('bhtd,bhsd->bhts', q, k) / jnp.sqrt(jnp.float32(HD))
        causal = jnp.tril(jnp.ones((Tx, Tx), dtype=bool))
        scores = jnp.where(causal[None, None], scores, jnp.float32(-1e+30))
        att = jax.nn.softmax(scores, axis=-1)
        y = jnp.einsum('bhts,bhsd->bhtd', att, v).transpose(0, 2, 1, 3).reshape(Bx, Tx, Cx)
        x = x + y @ wo.T
        flat = _rmsnorm(x, ln2_w).reshape(-1, Cx)
        probs = jax.nn.softmax(flat @ router_w.T, axis=-1)
        tp, ti = jax.lax.top_k(probs, TOPK)
        tp = tp / (jnp.sum(tp, axis=-1, keepdims=True) + 1e-09)
        weights = jnp.sum(tp[..., None] * jax.nn.one_hot(ti, NE, dtype=flat.dtype), axis=1)
        out = jnp.zeros_like(flat)
        for e in range(NE):
            hh = jax.nn.silu(flat @ w1[e].T) * (flat @ w3[e].T)
            out = out + weights[:, e:e + 1] * (hh @ w2[e].T)
        return x + out.reshape(Bx, Tx, Cx)
    h = _L0_tok_ref(x, L0_tok_A, L0_tok_W0, L0_tok_b0, L0_tok_g0, L0_tok_be0, L0_tok_m0, L0_tok_v0, L0_tok_W1, L0_tok_b1, L0_tok_g1, L0_tok_be1, L0_tok_m1, L0_tok_v1, L0_tok_W2, L0_tok_b2, L0_tok_g2, L0_tok_be2, L0_tok_m2, L0_tok_v2)
    h = h + _L0_attn_ref(_layernorm(h, axis=-1), L0_attn_ln1_w, L0_attn_ln1_b, L0_attn_in_proj_w, L0_attn_conv_w, L0_attn_conv_b, L0_attn_ssm_B, L0_attn_ssm_C, L0_attn_ssm_D, L0_attn_out_proj_w, L0_attn_ln2_w, L0_attn_ln2_b, L0_attn_fc1_w, L0_attn_fc1_b, L0_attn_fc2_w, L0_attn_fc2_b)
    h = h + _L0_ffn_ref(_layernorm(h, axis=-1), L0_ffn_ln1_w, L0_ffn_ln2_w, L0_ffn_wq, L0_ffn_wk, L0_ffn_wv, L0_ffn_wo, L0_ffn_router_w, L0_ffn_w1, L0_ffn_w2, L0_ffn_w3)
    return h

_drawn_inputs = setup_inputs


def setup_inputs(seed=0):
    import zlib

    import numpy as np

    out = dict(_drawn_inputs(seed))
    spreads = {'L0_tok_b0': (0.0, 0.1),
     'L0_tok_g0': (1.0, 0.6),
     'L0_tok_be0': (0.0, 0.1),
     'L0_tok_b1': (0.0, 0.267),
     'L0_tok_g1': (1.0, 0.2),
     'L0_tok_be1': (0.0, 0.356),
     'L0_tok_b2': (0.0, 0.8),
     'L0_tok_g2': (1.0, 0.2),
     'L0_tok_be2': (0.0, 0.8),
     'L0_attn_ln1_w': (1.0, 0.6),
     'L0_attn_ln1_b': (0.0, 0.8),
     'L0_attn_ssm_D': (1.0, 0.6),
     'L0_attn_ln2_w': (1.0, 0.6),
     'L0_attn_ln2_b': (0.0, 2.0),
     'L0_attn_fc1_b': (0.0, 2.0),
     'L0_attn_fc2_b': (0.0, 0.8),
     'L0_ffn_ln1_w': (1.0, 0.6),
     'L0_ffn_ln2_w': (1.0, 0.6)}
    factors = {'x': 5.182,
     'L0_tok_A': 8.0,
     'L0_tok_W0': 4.284,
     'L0_tok_v0': 2.979,
     'L0_attn_in_proj_w': 8.0,
     'L0_attn_conv_w': 8.0,
     'L0_attn_conv_b': 8.0,
     'L0_attn_ssm_B': 8.0,
     'L0_attn_ssm_C': 8.0,
     'L0_attn_out_proj_w': 8.0,
     'L0_attn_fc1_w': 13.737,
     'L0_ffn_wq': 8.0,
     'L0_ffn_wk': 8.0,
     'L0_ffn_wv': 5.366,
     'L0_ffn_wo': 4.169,
     'L0_ffn_router_w': 8.0,
     'L0_ffn_w1': 8.0,
     'L0_ffn_w2': 8.0,
     'L0_ffn_w3': 8.0,
     'L0_tok_m2': 5.108,
     'L0_attn_fc2_w': 3.77}
    for name, (base, spread) in spreads.items():
        noise = np.random.default_rng([zlib.crc32(name.encode()), seed]).standard_normal(out[name].shape)
        drawn = base * np.exp(spread * noise) if base else spread * noise
        out[name] = jnp.asarray(drawn.astype(out[name].dtype))
    for name, factor in factors.items():
        out[name] = (out[name] * factor).astype(out[name].dtype)
    return out
```

```python
from contextlib import ExitStack

import numpy as np

import concourse.bass as bass
from concourse import mybir

F32 = mybir.dt.float32
F32R = mybir.dt.float32r
ALU = mybir.AluOpType
ACT = mybir.ActivationFunctionType
AX = mybir.AxisListType

P = 128
SEQS, T, V, CIN, C1, C = 32, 64, 75, 3, 128, 64
FRAMES = SEQS * T
TILES = FRAMES // P
PAIRS = TILES // 2
SF = 8
STEPS = P // SF
NSTEP = FRAMES // SF
HALF = SF // 2 * V
PARTS = 4
GROUP = 32
BATCH = 4
NBATCH = STEPS // BATCH
FFB = 4
NH, HD, NKV, NE = 4, 16, 2, 8
HID = int(8 / 3 * C)
HB = HID // 2
NHB = 2 * NE
MASKED = -1e30
CHUNK = 4
NCHUNK = TILES // CHUNK


def offsets(parts):
    at, out = 0, {}
    for name, n in parts:
        out[name] = (at, n)
        at += n
    return out, at


GCN_PARTS = [("at", V), ("a", V), ("w1", C1), ("w2", C), ("w0", C1), ("bn0", 5 * C1), ("bn1", 5),
             ("bn2", 5 * C), ("bias_row", 1), ("own_frame", SF), ("ident", P),
             ("mean_v", P), ("xt0", STEPS * PARTS * GROUP)]
TAIL_PARTS = [("bd_xc", P), ("bd_z", P), ("bd_out", P), ("bd_fc1", FFB * P), ("bd_fc2", FFB * P),
              ("bd_wo", P), ("wq", P), ("wk", P), ("wv", 2 * NKV * HD), ("router", NE),
              ("fc2_b", C), ("ln1_w", 1), ("ln1_b", 1), ("conv_w", 3), ("conv_b", 1), ("ssm_b", 8),
              ("ssm_c", 8), ("ssm_d", 1), ("ln2_w", 1), ("ln2_b", 1), ("fc1_b", FFB), ("rms1_w", 1),
              ("rms2_w", 1), ("tri", P), ("causal", P), ("rope", P), ("fold", P),
              ("head", NH), ("expert", TILES * NE)]
MOE_PARTS = [("w1", NHB * HB), ("w3", NHB * HB), ("w2", NHB * C)]
GCN_AT, GCN_N = offsets(GCN_PARTS)
TAIL_AT, TAIL_N = offsets(TAIL_PARTS)
MOE_AT, MOE_N = offsets(MOE_PARTS)


def program(nc, x, gcn, tail, moe, out):
    ctx = ExitStack()
    with ctx:
        def sb(name, shape, dt=F32):
            return ctx.enter_context(nc.sbuf_tensor(name, shape, dt))

        def sem(name):
            return ctx.enter_context(nc.semaphore(name))

        gcn_sb = sb("gcn_sb", [P, GCN_AT["xt0"][0]])
        tail_sb = sb("tail_sb", [P, TAIL_N])
        moe_sb = sb("moe_sb", [P, MOE_N])

        def g(name, rows=P):
            at, n = GCN_AT[name]
            return gcn_sb[0:rows, at:at + n]

        def w(name, r0=0, r1=P):
            at, n = TAIL_AT[name]
            return tail_sb[r0:r1, at:at + n]

        def m(name, rows=P):
            at, n = MOE_AT[name]
            return moe_sb[0:rows, at:at + n]

        x_tile = sb("x_tile", [P, V * CIN])
        xt = sb("xt", [V + 1, STEPS, PARTS * GROUP])
        gx = sb("gx", [PARTS * GROUP, STEPS, V], F32R)
        buf_s = sb("buf_s", [P, 2, NH * P])
        buf_p = sb("buf_p", [P, 2, NH * P])
        buf_t = sb("buf_t", [P, 2, NH * P])
        buf_ch = sb("buf_ch", [P, 4, PAIRS * P])
        buf_ff = sb("buf_ff", [P, FFB, PAIRS * P])
        buf_1 = sb("buf_1", [P, NHB * CHUNK * P])
        w0_exp = buf_s[0:PARTS * GROUP, :, :]
        w0_r = sb("w0_r", [PARTS * GROUP, 2, 512], F32R)
        at = 2 * SF * C1
        h1 = buf_1[0:V, 0:at].rearrange("v (b f c) -> v b f c", b=2, f=SF)
        gt, h2, h2w = (buf_1[:, at + n * 4 * HALF:at + (n + 1) * 4 * HALF].rearrange("p (b n) -> p b n", b=2)
                       for n in range(3))
        sums = buf_1[:, at + 12 * HALF:at + 12 * HALF + FRAMES]
        mean_a = sb("mean_a", [P, V])
        half = sb("half", [P, C1])
        s0 = sb("s0", [PARTS * GROUP, C1])
        c0 = sb("c0", [PARTS * GROUP, C1])
        w0s = sb("w0s", [PARTS * GROUP, C1])
        s1 = sb("s1", [P, 1])
        c1 = sb("c1", [P, 1])
        s2 = sb("s2", [P, C])
        c2 = sb("c2", [P, C])
        bn_e = sb("bn_e", [P, C1 + 1 + C])

        h_tok = sb("h_tok", [P, TILES, C])
        h_new = sb("h_new", [P, TILES, C])
        x_tok = sb("x_tok", [P, TILES, C])
        x_new = sb("x_new", [P, TILES, C])
        n_tok = sb("n_tok", [P, TILES, C])
        d_tok = sb("d_tok", [P, TILES, C])
        y_tok = sb("y_tok", [P, TILES, C])
        q_tok = y_tok
        row_a = sb("row_a", [P, TILES])
        row_v = sb("row_v", [P, TILES])
        row_r = sb("row_r", [P, TILES])
        n_ch = sb("n_ch", [P, PAIRS * P])
        xc_pad = sb("xc_pad", [P, SEQS // 2, T + 2])
        xc_ch, cv_ch, cw_ch, z_ch = (buf_ch[:, n, :] for n in range(4))
        xc_tok = sb("xc_tok", [P, PAIRS, P])
        bc = sb("bc", [P, 8])
        bcs = sb("bcs", [P, 1])
        ff = buf_ff
        qq, kk = buf_ff[:, 0:2, :], buf_ff[:, 2:4, :]
        n_twice = buf_ff[:, 0:2, :].rearrange("p b n -> p (b n)").rearrange("p (j a c) -> p j a c", j=TILES, a=2)
        kb = buf_ch[:].rearrange("p b n -> p (b n)").rearrange("p (b k h s) -> p b k h s", b=2, k=4, h=NH)
        v_tok = sb("v_tok", [P, TILES, NKV * HD])
        sm, pr, pt = (b[:].rearrange("p b (h s) -> p b h s", h=NH) for b in (buf_s, buf_p, buf_t))
        mx = sb("mx", [P, TILES * NH])
        nmx = sb("nmx", [P, TILES * NH])
        den = sb("den", [P, TILES * NH])
        rden = sb("rden", [P, TILES * NH])
        f_r = sb("f_r", [P, TILES * P], F32R)
        w1_h = sb("w1_h", [P, NHB * HB], F32R)
        w3_h = sb("w3_h", [P, NHB * HB], F32R)
        w1_l = sb("w1_l", [P, NHB * HB], F32R)
        w3_l = sb("w3_l", [P, NHB * HB], F32R)
        lg = sb("lg", [P, TILES, NE])
        ep = sb("ep", [P, TILES, NE])
        oh1 = sb("oh1", [P, TILES, NE])
        oh2 = sb("oh2", [P, TILES, NE])
        tmp8 = sb("tmp8", [P, TILES, NE])
        gate = sb("gate", [P, TILES, NE])
        r_a = sb("r_a", [P, TILES])
        r_b = sb("r_b", [P, TILES])
        r_c = sb("r_c", [P, TILES])
        r_d = sb("r_d", [P, TILES])
        act_h = buf_p[0:HB, :, :]
        hh = buf_1[0:HB, :].rearrange("p (b n) -> p b n", b=NHB)
        eo = buf_t[:].rearrange("p b (e c) -> p b e c", e=NE)
        ps = ctx.enter_context(nc.psum_tensor("ps", [P, 8, 512], F32))

        gcn_loaded, tail_loaded, moe_loaded = sem("gcn_loaded"), sem("tail_loaded"), sem("moe_loaded")
        xt0_loaded = sem("xt0_loaded")
        x_loaded, x_taken = sem("x_loaded"), sem("x_taken")
        xt_ready = sem("xt_ready")
        gx_summed, gx_high, gx_ready = sem("gx_summed"), sem("gx_high"), sem("gx_ready")
        mean_summed, mean_ready = sem("mean_summed"), sem("mean_ready")
        bn_eps, bn_rsqrt, c0_ready, w0_ready, w0_high, bn1_ready, bn2_ready = (
            sem("bn_eps"), sem("bn_rsqrt"), sem("c0_ready"), sem("w0_ready"), sem("w0_high"),
            sem("bn1_ready"), sem("bn2_ready"))
        w0_low = sem("w0_low")
        h1_summed, h1_ready = sem("h1_summed"), sem("h1_ready")
        g_summed, g_ready = sem("g_summed"), sem("g_ready")
        h2_summed, h2_ready = sem("h2_summed"), sem("h2_ready")
        h2_free, h2w_free, h2w_ready = sem("h2_free"), sem("h2w_free"), sem("h2w_ready")
        h_summed = sem("h_summed")
        var_ready, rsqrt_ready, norm_ready, norm_turned, norm_ch = (
            sem("var_ready"), sem("rsqrt_ready"), sem("norm_ready"), sem("norm_turned"), sem("norm_ch"))
        pow_ready = sem("pow_ready")
        pad_zero, xz_summed, xc_copied, conv_ready, xc_silu, z_silu = (
            sem("pad_zero"), sem("xz_summed"), sem("xc_copied"), sem("conv_ready"), sem("xc_silu"),
            sem("z_silu"))
        xc_turned, xc_tok_ready, cum_summed, yz_ready, mix_summed, x2_ready, hx_ready = (
            sem("xc_turned"), sem("xc_tok_ready"), sem("cum_summed"), sem("yz_ready"),
            sem("mix_summed"), sem("x2_ready"), sem("hx_ready"))
        hb_ready = sem("hb_ready")
        fc1_summed, gelu_ready, fc2_summed = sem("fc1_summed"), sem("gelu_ready"), sem("fc2_summed")
        q_summed, q_ready, k_summed, k_ready, v_summed, v_ready = (
            sem("q_summed"), sem("q_ready"), sem("k_summed"), sem("k_ready"), sem("v_summed"),
            sem("v_ready"))
        kf_summed, kb_ready, s_summed, s_masked, max_ready, exp_ready, pt_turned, pt_ready = (
            sem("kf_summed"), sem("kb_ready"), sem("s_summed"), sem("s_masked"), sem("max_ready"),
            sem("exp_ready"), sem("pt_turned"), sem("pt_ready"))
        pv_summed, y_ready, y_turned, y_ch, wo_summed, x4_ready = (
            sem("pv_summed"), sem("y_ready"), sem("y_turned"), sem("y_ch"), sem("wo_summed"),
            sem("x4_ready"))
        f_turned, f_high, f_ready, wh_ready, wl_ready = (
            sem("f_turned"), sem("f_high"), sem("f_ready"), sem("wh_ready"), sem("wl_ready"))
        lg_summed, lg_ready, lexp_ready, gate_ready = (
            sem("lg_summed"), sem("lg_ready"), sem("lexp_ready"), sem("gate_ready"))
        e1_summed, e3_summed, silu_ready, hh_ready, eo_summed, eo_weighted, out_ready, stored = (
            sem("e1_summed"), sem("e3_summed"), sem("silu_ready"), sem("hh_ready"),
            sem("eo_summed"), sem("eo_weighted"), sem("out_ready"), sem("stored"))
        dve_chain = sem("dve_chain")

        h1_ps = ps[0:V, 0:2, :]
        g_ps = ps[:, 2:4, 0:HALF]
        h2_ps = ps[:, 4:6, 0:HALF]
        xt_ps = ps[0:V, 6, 0:CIN * P]
        gx_ps = ps[0:PARTS * GROUP, 7, 0:BATCH * V]

        def banks(a, n):
            return ps[:, a:a + n, :].rearrange("p b n -> p (b n)")

        def split(ap, a):
            return ap.rearrange("p (a b) -> p a b", a=a)

        ident = g("ident")
        GX_STEPS = [6, 9, 12, 14]

        block = ctx.enter_context(nc.Block())

        @block.sync
        def _(sp):
            sp.dma_start(gcn_sb[:], gcn[:, 0:GCN_AT["xt0"][0]]).then_inc(gcn_loaded, 16)
            at, n = GCN_AT["xt0"]
            sp.dma_start(xt[:].rearrange("v s g -> v (s g)"), gcn[0:V + 1, at:at + n]).then_inc(xt0_loaded, 16)
            sp.dma_start(x_tile[:], x[0:P, :]).then_inc(x_loaded, 16)
            sp.dma_start(tail_sb[:], tail).then_inc(tail_loaded, 16)
            sp.dma_start(moe_sb[:], moe).then_inc(moe_loaded, 16)
            for j in range(1, TILES):
                sp.wait_ge(x_taken, j)
                sp.dma_start(x_tile[:], x[j * P:(j + 1) * P, :]).then_inc(x_loaded, 16)
            sp.wait_ge(out_ready, 1)
            sp.dma_start(out.rearrange("(j p) c -> p j c", p=P), y_tok[:]).then_inc(stored, 16)
            sp.wait_ge(stored, 16)

        @block.tensor
        def _(pe):
            def turn_x(j):
                pe.wait_ge(x_loaded, 16 * (j + 1))
                for i in range(CIN):
                    mm = pe.transpose(xt_ps[:, i * P:(i + 1) * P], x_tile[:, i::CIN], ident)
                mm.then_inc(x_taken, 1)

            def gx_batch(j, b):
                pe.wait_ge(xt_ready, PARTS * (j + 1))
                for k in range(BATCH):
                    slot = BATCH * b + k
                    mm = pe.matmul(gx_ps[:, k * V:(k + 1) * V],
                                   xt[:, slot, :],
                                   g("at", V + 1), start=True, stop=True)
                mm.then_inc(gx_summed, 1)

            def layer0(slot):
                for v in range(2):
                    mm = pe.matmul(h1_ps[:, v, :], gx[:, slot, :], w0_r[:, v, :], start=True, stop=True)
                mm.then_inc(h1_summed, 1)

            def mix(par):
                for f in range(SF):
                    v, k = divmod(f, SF // 2)
                    mm = pe.matmul(g_ps[:, v, k * V:(k + 1) * V], h1[:, par, f, :], g("at", V),
                                   start=True, stop=True)
                mm.then_inc(g_summed, 1)

            def layer1(par):
                for v in range(2):
                    mm = pe.matmul(h2_ps[:, v, :], g("w1"), gt[:, par, v * HALF:(v + 1) * HALF],
                                   start=True, stop=True)
                mm.then_inc(h2_summed, 1)

            pe.wait_ge(gcn_loaded, 16)
            pe.matmul(ps[:, 0, 0:V], g("mean_v", V), g("a", V), start=True, stop=True).then_inc(mean_summed, 1)
            turn_x(0)
            for b in range(NBATCH):
                if b:
                    pe.wait_ge(gx_ready, b)
                gx_batch(0, b)
            pe.wait_ge(w0_low, 2)
            pe.wait_ge(mean_ready, 1)
            pe.wait_ge(gx_ready, NBATCH)
            layer0(0)
            pe.wait_ge(h1_ready, 1)
            mix(0)
            layer0(1)

            def tile(i, last):
                at = i * STEPS
                for s in range(STEPS):
                    if not (last and s + 2 >= STEPS):
                        pe.wait_ge(h1_ready, at + s + 2)
                        if (s + 2) % BATCH == 0:
                            pe.wait_ge(gx_ready, i * NBATCH + (s + 2) // BATCH + 1)
                        layer0((s + 2) % STEPS)
                    if not (last and s + 1 >= STEPS):
                        if last and s + 2 >= STEPS:
                            pe.wait_ge(h1_ready, at + s + 2)
                        pe.wait_ge(g_ready, at + s + 1)
                        mix((s + 1) % 2)
                    if last and s + 1 >= STEPS:
                        pe.wait_ge(g_ready, at + s + 1)
                    pe.wait_ge(h2_ready, at + s)
                    layer1(s % 2)
                    if not last:
                        if s == 1:
                            turn_x(i + 1)
                        if s in GX_STEPS:
                            b = GX_STEPS.index(s)
                            pe.wait_ge(gx_ready, (i + 1) * NBATCH + b)
                            gx_batch(i + 1, b)

            with pe.Fori(0, TILES - 1) as i:
                tile(i, False)
            tile(TILES - 1, True)

            pe.wait_ge(h2w_free, 2 + NSTEP)
            pe.wait_ge(h1_ready, NSTEP)
            for j in range(TILES):
                mm = pe.matmul(banks(0, 2)[:, j * C:(j + 1) * C], sums[:, j * P:(j + 1) * P], g("w2"),
                               start=True, stop=True)
            mm.then_inc(h_summed, 1)

            def turn_pairs(src, dst, done):
                for p in range(PAIRS):
                    mm = pe.transpose(dst[:, p * P:(p + 1) * P], src[:, 2 * p:2 * p + 2, :], ident)
                mm.then_inc(done, 1)

            pe.wait_ge(tail_loaded, 16)
            pe.wait_ge(g_ready, NSTEP)
            pe.wait_ge(h2_ready, NSTEP)
            pe.wait_ge(norm_ready, 1)
            turn_pairs(n_tok, banks(2, 2), norm_turned)
            pe.wait_ge(norm_ch, 1)
            for bank, wn in ((4, "bd_xc"), (6, "bd_z")):
                for v in range(2):
                    mm = pe.matmul(ps[:, bank + v, :], w(wn), n_ch[:, v * 512:(v + 1) * 512],
                                   start=True, stop=True)
                mm.then_inc(xz_summed, 1)
            pe.wait_ge(xc_silu, 1)
            for p in range(PAIRS):
                mm = pe.transpose(banks(2, 2)[:, p * P:(p + 1) * P], xc_ch[:, p * P:(p + 1) * P], ident)
            mm.then_inc(xc_turned, 1)
            pe.wait_ge(xc_tok_ready, 1)
            for p in range(PAIRS):
                mm = pe.matmul(banks(4, 2)[:, p * P:(p + 1) * P], xc_tok[:, p, :], w("tri"),
                               start=True, stop=True)
            mm.then_inc(cum_summed, 1)
            pe.wait_ge(yz_ready, 1)
            for p in range(PAIRS):
                mm = pe.matmul(banks(2, 2)[:, p * P:(p + 1) * P], cw_ch[:, p * P:(p + 1) * P], w("bd_out"),
                               start=True, stop=True)
            mm.then_inc(mix_summed, 1)
            pe.wait_ge(norm_ready, 2)
            turn_pairs(n_tok, banks(4, 2), norm_turned)
            pe.wait_ge(norm_ch, 2)
            for fb in range(FFB):
                if fb >= 2:
                    pe.wait_ge(gelu_ready, fb - 1)
                for v in range(2):
                    mm = pe.matmul(ps[:, 2 * (fb % 2) + v, :], w("bd_fc1")[:, fb * P:(fb + 1) * P],
                                   n_ch[:, v * 512:(v + 1) * 512], start=True, stop=True)
                mm.then_inc(fc1_summed, 1)
            pe.wait_ge(gelu_ready, FFB)
            for p in range(PAIRS):
                for fb in range(FFB):
                    mm = pe.matmul(banks(6, 2)[:, p * P:(p + 1) * P], ff[:, fb, p * P:(p + 1) * P],
                                   w("bd_fc2")[:, fb * P:(fb + 1) * P],
                                   start=(fb == 0), stop=(fb == FFB - 1))
            mm.then_inc(fc2_summed, 1)

            pe.wait_ge(norm_ready, 3)
            turn_pairs(n_tok, banks(0, 2), norm_turned)
            pe.wait_ge(norm_ch, 3)
            for par in range(2):
                rows = slice(par * C, (par + 1) * C)
                for v in range(2):
                    mm = pe.matmul(ps[:, 2 + v, :], w("wq", par * C, par * C + C),
                                   n_ch[rows, v * 512:(v + 1) * 512], start=True, stop=True)
                mm.then_inc(q_summed, 1)
                for v in range(2):
                    mm = pe.matmul(ps[:, 4 + v, :], w("wk", par * C, par * C + C),
                                   n_ch[rows, v * 512:(v + 1) * 512], start=True, stop=True)
                mm.then_inc(k_summed, 1)
                if par == 0:
                    pe.wait_ge(k_ready, 1)
            pe.wait_ge(hx_ready, 2)
            for p in range(PAIRS):
                mm = pe.matmul(ps[:, 6, p * 2 * NKV * HD:(p + 1) * 2 * NKV * HD], n_ch[:, p * P:(p + 1) * P],
                               w("wv"), start=True, stop=True)
            mm.then_inc(v_summed, 1)
            pe.wait_ge(k_ready, 2)
            pe.wait_ge(v_ready, 1)

            def fold_keys(n):
                par, v = n % 2, n // 2
                if n:
                    pe.wait_ge(kb_ready, n)
                pe.matmul(ps[:, 7, :], w("fold"), kk[:, par, v * 512:(v + 1) * 512],
                          start=True, stop=True).then_inc(kf_summed, 1)

            def scores(n, k):
                a = 4 * n + k
                par, v = n % 2, n // 2
                pe.wait_ge(kb_ready, n + 1)
                if a >= 2:
                    pe.wait_ge(s_masked, a - 1)
                pe.matmul(ps[:, 2 + a % 2, :], qq[:, par, v * 512 + k * P:v * 512 + (k + 1) * P],
                          kb[:, n % 2, k, :, :].rearrange("p h s -> p (h s)"),
                          start=True, stop=True).then_inc(s_summed, 1)

            def turn_probs(a):
                pe.wait_ge(exp_ready, a + 1)
                if a >= 2:
                    pe.wait_ge(pt_ready, a - 1)
                for h in range(NH):
                    mm = pe.transpose(ps[:, 4 + a % 2, h * P:(h + 1) * P], pr[:, a % 2, h, :], ident)
                mm.then_inc(pt_turned, 1)

            def values(a):
                n, k = divmod(a, 4)
                j = 2 * (4 * (n // 2) + k) + n % 2
                pe.wait_ge(pt_ready, a + 1)
                for h in range(NH):
                    kv = h * NKV // NH
                    mm = pe.matmul(banks(0, 2)[:, j * C + h * HD:j * C + (h + 1) * HD], pt[:, a % 2, h, :],
                                   v_tok[:, j, kv * HD:(kv + 1) * HD], start=True, stop=True)
                mm.then_inc(pv_summed, 1)

            fold_keys(0)
            for a in range(TILES + 2):
                if a < TILES:
                    if a % 4 == 0 and a // 4 + 1 < TILES // 4:
                        fold_keys(a // 4 + 1)
                    scores(a // 4, a % 4)
                if 1 <= a <= TILES:
                    turn_probs(a - 1)
                if a >= 2:
                    values(a - 2)
            pe.wait_ge(y_ready, 1)
            turn_pairs(y_tok, banks(2, 2), y_turned)
            pe.wait_ge(y_ch, 1)
            for p in range(PAIRS):
                mm = pe.matmul(banks(4, 2)[:, p * P:(p + 1) * P], n_ch[:, p * P:(p + 1) * P], w("bd_wo"),
                               start=True, stop=True)
            mm.then_inc(wo_summed, 1)

            pe.wait_ge(norm_ready, 4)
            for n in range(NCHUNK):
                for k in range(CHUNK):
                    j = CHUNK * n + k
                    mm = pe.transpose(ps[:, n, k * P:(k + 1) * P],
                                      n_twice[:, j, :, :].rearrange("p a c -> p (a c)"), ident)
                mm.then_inc(f_turned, 1)
            pe.wait_ge(f_ready, NCHUNK)
            for j in range(TILES):
                mm = pe.matmul(ps[:, 4, j * NE:(j + 1) * NE], f_r[:, j * P:(j + 1) * P].bitcast(F32),
                               w("router"), start=True, stop=True)
            mm.then_inc(lg_summed, 1)
            pe.wait_ge(wl_ready, 2)
            pe.wait_ge(lg_ready, 1)

            def up(n, b):
                k = NHB * n + b
                cols = slice(b * HB, (b + 1) * HB)
                f = f_r[:, n * CHUNK * P:(n + 1) * CHUNK * P]
                for bank, hi, lo, done, free in ((0, w1_h, w1_l, e1_summed, silu_ready),
                                                 (2, w3_h, w3_l, e3_summed, hh_ready)):
                    if k >= 2:
                        pe.wait_ge(free, k - 1)
                    o = ps[0:HB, bank + k % 2, :]
                    pe.matmul(o, hi[:, cols], f, start=True, stop=False)
                    pe.matmul(o, lo[:, cols], f, start=False, stop=True).then_inc(done, 1)

            def down(n, k):
                a = CHUNK * n + k
                if a >= 2:
                    pe.wait_ge(eo_weighted, a - 1)
                for e in range(NE):
                    for q in range(2):
                        b = 2 * e + q
                        mm = pe.matmul(ps[:, 4 + a % 2, e * C:(e + 1) * C], hh[:, b, k * P:(k + 1) * P],
                                       m("w2", HB)[:, b * C:(b + 1) * C], start=(q == 0), stop=(q == 1))
                mm.then_inc(eo_summed, 1)

            for n in range(NCHUNK):
                for b in range(NHB):
                    up(n, b)
                pe.wait_ge(hh_ready, NHB * (n + 1))
                for k in range(CHUNK):
                    down(n, k)

        @block.scalar
        def _(act):
            def xt_copy(j, part):
                act.wait_ge(x_taken, j + 1)
                act.activation(xt[0:V, :, part * GROUP:part * GROUP + CIN * SF].rearrange("v s (i f) -> v s i f", f=SF),
                               xt_ps.rearrange("v (i s f) -> v s i f", i=CIN, f=SF),
                               ACT.Copy).then_inc(xt_ready, 1)

            def gx_copy(j, b):
                act.wait_ge(gx_summed, j * NBATCH + b + 1)
                act.activation(gx[:, BATCH * b:BATCH * (b + 1), :],
                               gx_ps.rearrange("p (s v) -> p s v", v=V), ACT.Copy).then_inc(gx_high, 1)

            def h1_relu(k, par):
                act.wait_ge(h1_summed, k + 1)
                act.activation(h1[:, par, :, :].rearrange("v f c -> v (f c)"),
                               h1_ps.rearrange("v b n -> v (b n)"), ACT.Relu).then_inc(h1_ready, 1)

            def h2_relu(k, par):
                act.wait_ge(h2_summed, k + 1)
                act.wait_ge(h2_free, k + 1)
                act.activation(split(h2[:, par, :], 2), h2_ps, ACT.Relu, bias=c1[:, 0:1],
                               scale=s1[:, 0:1]).then_inc(h2_ready, 1)

            act.wait_ge(w0_ready, 2)
            act.activation(w0_r[:], w0_exp, ACT.Copy).then_inc(w0_high, 1)
            act.wait_ge(xt0_loaded, 16)
            for part in range(PARTS):
                xt_copy(0, part)
            for b in range(NBATCH):
                gx_copy(0, b)
            h1_relu(0, 0)
            h1_relu(1, 1)
            act.wait_ge(bn1_ready, 1)

            def tile(i, last):
                at = i * STEPS
                for s in range(STEPS):
                    if not (last and s + 2 >= STEPS):
                        h1_relu(at + s + 2, s % 2)
                    h2_relu(at + s, s % 2)
                    if not last:
                        if 1 <= s <= PARTS:
                            xt_copy(i + 1, s - 1)
                        if s in GX_STEPS:
                            gx_copy(i + 1, GX_STEPS.index(s))

            with act.Fori(0, TILES - 1) as i:
                tile(i, False)
            tile(TILES - 1, True)

            def norm_scale(n, src, scale, bias=None):
                act.wait_ge(norm_turned, n)
                if bias is None:
                    act.activation(n_ch[:], src, ACT.Copy, scale=scale).then_inc(norm_ch, 1)
                else:
                    act.activation(n_ch[:], src, ACT.Identity, bias=bias, scale=scale).then_inc(norm_ch, 1)

            act.wait_ge(tail_loaded, 16)
            norm_scale(1, banks(2, 2), w("ln1_w"), w("ln1_b"))
            act.wait_ge(xz_summed, 1)
            act.wait_ge(pad_zero, 1)
            act.activation(xc_pad[:, :, 2:T + 2], banks(4, 2).rearrange("p (q t) -> p q t", t=T),
                           ACT.Copy).then_inc(xc_copied, 1)
            act.wait_ge(xz_summed, 2)
            act.activation(z_ch, banks(6, 2), ACT.Silu).then_inc(z_silu, 1)
            act.wait_ge(conv_ready, 1)
            act.activation(xc_ch, cv_ch, ACT.Silu).then_inc(xc_silu, 1)
            act.wait_ge(xc_turned, 1)
            act.activation(xc_tok[:].rearrange("p a b -> p (a b)"), banks(2, 2),
                           ACT.Copy).then_inc(xc_tok_ready, 1)
            norm_scale(2, banks(4, 2), w("ln2_w"), w("ln2_b"))
            for fb in range(FFB):
                act.wait_ge(fc1_summed, fb + 1)
                act.activation(ff[:, fb, :], banks(2 * (fb % 2), 2), ACT.Gelu,
                               bias=w("fc1_b")[:, fb:fb + 1]).then_inc(gelu_ready, 1)
            norm_scale(3, banks(0, 2), w("rms1_w"))
            act.wait_ge(v_summed, 1)
            act.activation(v_tok[:].rearrange("p a b -> p (a b)"), ps[:, 6, :], ACT.Copy).then_inc(v_ready, 1)

            def key_blocks(n):
                act.wait_ge(kf_summed, n + 1)
                if n >= 2:
                    act.wait_ge(s_summed, 4 * (n - 1))
                for h in range(NH):
                    a = act.activation(kb[:, n % 2, :, h, :], split(ps[:, 7, :], 4), ACT.Copy,
                                       scale=w("head")[:, h:h + 1])
                a.then_inc(kb_ready, 1)

            key_blocks(0)
            for a in range(TILES + 1):
                if a % 4 == 0 and a // 4 + 1 < TILES // 4:
                    key_blocks(a // 4 + 1)
                if a < TILES:
                    act.wait_ge(max_ready, a + 1)
                    if a >= 2:
                        act.wait_ge(pt_turned, a - 1)
                    for h in range(NH):
                        e = act.activation(pr[:, a % 2, h, :], sm[:, a % 2, h, :], ACT.Exp,
                                           bias=nmx[:, a * NH + h:a * NH + h + 1], scale=HD ** -0.5,
                                           accum_out=den[:, a * NH + h:a * NH + h + 1])
                    e.then_inc(exp_ready, 1)
                if a >= 1:
                    act.wait_ge(pt_turned, a)
                    if a >= 3:
                        act.wait_ge(pv_summed, a - 2)
                    act.activation(pt[:, (a - 1) % 2, :, :].rearrange("p h s -> p (h s)"),
                                   ps[:, 4 + (a - 1) % 2, :], ACT.Copy).then_inc(pt_ready, 1)
            act.wait_ge(y_turned, 1)
            act.activation(n_ch[:], banks(2, 2), ACT.Copy).then_inc(y_ch, 1)

            act.wait_ge(moe_loaded, 16)
            act.activation(w1_h[:], m("w1"), ACT.Copy).then_inc(wh_ready, 1)
            act.activation(w3_h[:], m("w3"), ACT.Copy).then_inc(wh_ready, 1)
            for n in range(NCHUNK):
                act.wait_ge(f_turned, n + 1)
                act.activation(f_r[:, n * CHUNK * P:(n + 1) * CHUNK * P], ps[:, n, :], ACT.Copy,
                               scale=w("rms2_w")).then_inc(f_high, 1)
            act.wait_ge(lg_ready, 2)
            act.activation(ep[:], lg[:], ACT.Exp).then_inc(lexp_ready, 1)
            for k in range(NCHUNK * NHB):
                act.wait_ge(e1_summed, k + 1)
                if k >= 2:
                    act.wait_ge(hh_ready, k - 1)
                act.activation(act_h[:, k % 2, :], ps[0:HB, k % 2, :], ACT.Silu).then_inc(silu_ready, 1)

        @block.gpsimd
        def _(pool):
            pool.memset(xc_pad[:, :, 0:2], 0.0).then_inc(pad_zero, 1)
            pool.memset(half[:], -0.5).then_inc(pow_ready, 1)
            pool.wait_ge(pow_ready, 1)
            pool.wait_ge(bn_eps, 3)
            pool.tensor_tensor(s0[:], bn_e[0:PARTS * GROUP, 0:C1], half[0:PARTS * GROUP, :], ALU.pow).then_inc(bn_rsqrt, 1)
            pool.tensor_tensor(s1[:], bn_e[:, C1:C1 + 1], half[:, 0:1], ALU.pow).then_inc(bn_rsqrt, 1)
            pool.tensor_tensor(s2[:], bn_e[:, C1 + 1:], half[:, 0:C], ALU.pow).then_inc(bn_rsqrt, 1)
            pool.wait_ge(mean_ready, 1)

            def tile(i):
                for s in range(STEPS):
                    k = i * STEPS + s
                    pool.wait_ge(h2_ready, k + 1)
                    pool.wait_ge(h2w_free, k + 1)
                    pool.tensor_tensor(split(h2w[:, s % 2, :], SF), split(h2[:, s % 2, :], SF),
                                       mean_a[:].rearrange("p (a v) -> p a v", a=1).to_broadcast([P, SF, V]),
                                       ALU.mult).then_inc(h2_free, 1)

            pool.nop().then_inc(h2_free, 2)
            with pool.Fori(0, TILES) as i:
                tile(i)

            for n in range(6):
                pool.wait_ge(var_ready, n + 1)
                pool.tensor_tensor(row_r[:], row_v[:], half[:, 0:TILES], ALU.pow).then_inc(rsqrt_ready, 1)

        @block.vector
        def _(dve):
            chain = [0]

            def link(ins):
                chain[0] += 1
                ins.then_inc(dve_chain, 1)
                dve.wait_ge(dve_chain, chain[0])

            def bcast(ap, n):
                return ap.rearrange("p (a o) -> p a o", o=1).to_broadcast([ap.shape[0], ap.shape[1], n])

            dve.wait_ge(gcn_loaded, 16)
            G0 = PARTS * GROUP
            bn0, bn1, bn2 = g("bn0", G0), g("bn1"), g("bn2")
            dve.tensor_scalar(bn_e[0:G0, 0:C1], bn0[:, C1:2 * C1], 1e-5, None, ALU.add).then_inc(bn_eps, 1)
            dve.tensor_scalar(bn_e[:, C1:C1 + 1], bn1[:, 1:2], 1e-5, None, ALU.add).then_inc(bn_eps, 1)
            dve.tensor_scalar(bn_e[:, C1 + 1:], bn2[:, C:2 * C], 1e-5, None, ALU.add).then_inc(bn_eps, 1)

            def bn_shift(s, c, bn, n):
                link(dve.tensor_tensor(s, s, bn[:, 0:n], ALU.mult))
                link(dve.tensor_tensor(c, bn[:, 2 * n:3 * n], bn[:, 3 * n:4 * n], ALU.subtract))
                link(dve.tensor_tensor(c, c, s, ALU.mult))
                return dve.tensor_tensor(c, c, bn[:, 4 * n:5 * n], ALU.add)

            dve.wait_ge(bn_rsqrt, 3)
            link(bn_shift(s0[:], c0[:], bn0, C1))
            link(dve.tensor_tensor(w0s[:], g("w0", G0), s0[:], ALU.mult))
            link(dve.scalar_tensor_tensor(out=w0s[:], in0=c0[:], scalar=g("bias_row", G0), in1=w0s[:],
                                          op0=ALU.mult, op1=ALU.add))
            for v in range(2):
                dve.tensor_tensor(w0_exp[:, v, :].rearrange("p (f c) -> p f c", c=C1),
                                  w0s[:].rearrange("p (a c) -> p a c", a=1).to_broadcast([G0, SF // 2, C1]),
                                  bcast(g("own_frame", G0)[:, v * SF // 2:(v + 1) * SF // 2], C1),
                                  ALU.mult).then_inc(w0_ready, 1)
            bn_shift(s1[:], c1[:], bn1, 1).then_inc(bn1_ready, 1)
            link(bn_shift(s2[:], c2[:], bn2, C))
            dve.wait_ge(w0_high, 1)
            dve.wait_ge(w0_ready, 2)
            for part in (1, 3):
                rows = slice(part * GROUP, (part + 1) * GROUP)
                dve.tensor_tensor(w0_r[rows, :, :], w0_exp[rows, :, :], w0_r[rows, :, :].bitcast(F32),
                                  ALU.subtract).then_inc(w0_low, 1)
            dve.wait_ge(mean_summed, 1)
            dve.tensor_copy(mean_a[:], ps[:, 0, 0:V]).then_inc(mean_ready, 1)
            dve.nop().then_inc(h2w_free, 2)

            def gx_low(n, b):
                rows = slice(2 * GROUP, PARTS * GROUP)
                o = gx[rows, BATCH * b:BATCH * (b + 1), :]
                dve.wait_ge(gx_high, n)
                dve.tensor_tensor(o, gx_ps[rows, :].rearrange("p (s v) -> p s v", v=V), o.bitcast(F32),
                                  ALU.subtract).then_inc(gx_ready, 1)

            def g_copy(k, par):
                dve.wait_ge(g_summed, k + 1)
                dve.tensor_copy(split(gt[:, par, :], 2), g_ps).then_inc(g_ready, 1)

            def vertex_sum(k, par, col):
                dve.wait_ge(h2_free, k + 3)
                dve.tensor_reduce(sums[:, col], split(h2w[:, par, :], SF), AX.X, ALU.add).then_inc(h2w_free, 1)

            for b in range(NBATCH):
                gx_low(b + 1, b)
            for k in range(3):
                g_copy(k, k % 2)

            def tile(i, last):
                at = i * STEPS
                for s in range(STEPS):
                    col = slice(i * P + s * SF, i * P + s * SF + SF) if last else bass.ds(i * P + s * SF, SF)
                    vertex_sum(at + s, s % 2, col)
                    if not (last and s + 3 >= STEPS):
                        g_copy(at + s + 3, (s + 3) % 2)
                    if not last and s + 2 in GX_STEPS:
                        b = GX_STEPS.index(s + 2)
                        gx_low((i + 1) * NBATCH + b + 1, b)

            with dve.Fori(0, TILES - 1) as i:
                tile(i, False)
            tile(TILES - 1, True)

            dve.wait_ge(h_summed, 1)
            h2d = h_tok[:]
            row = lambda ap: ap.rearrange("p (a c) -> p a c", a=1).to_broadcast([P, TILES, C])
            link(dve.tensor_tensor(h2d, banks(0, 2).rearrange("p (j c) -> p j c", c=C), row(s2[:]), ALU.mult))
            link(dve.tensor_tensor(h2d, h2d, row(c2[:]), ALU.add))

            norms = [0]

            def rsqrt_scale(src, dst, eps, twice=False):
                link(dve.tensor_tensor(q_tok[:], src, src, ALU.mult))
                link(dve.tensor_reduce(row_v[:], q_tok[:], AX.X, ALU.add))
                norms[0] += 1
                dve.tensor_scalar(row_v[:], row_v[:], 1.0 / C, eps, ALU.mult, ALU.add).then_inc(var_ready, 1)
                dve.wait_ge(rsqrt_ready, norms[0])
                if twice:
                    src = src.rearrange("p j (a c) -> p j a c", a=1).to_broadcast([P, TILES, 2, C])
                    return dve.tensor_tensor(dst, src, row_r[:].rearrange("p (j a c) -> p j a c", a=1, c=1)
                                             .to_broadcast([P, TILES, 2, C]), ALU.mult)
                return dve.tensor_tensor(dst, src, bcast(row_r[:], C), ALU.mult)

            def layer_norm(src, dst):
                link(dve.tensor_reduce(row_a[:], src, AX.X, ALU.add))
                link(dve.tensor_scalar(row_a[:], row_a[:], -1.0 / C, None, ALU.mult))
                link(dve.tensor_tensor(d_tok[:], src, bcast(row_a[:], C), ALU.add))
                return rsqrt_scale(d_tok[:], dst, 1e-5)

            link(layer_norm(h_tok[:], x_tok[:]))
            layer_norm(x_tok[:], n_tok[:]).then_inc(norm_ready, 1)
            dve.wait_ge(tail_loaded, 16)
            link(dve.tensor_tensor(bc[:], w("ssm_b"), w("ssm_c"), ALU.mult))
            link(dve.tensor_reduce(bcs[:], bc[:], AX.X, ALU.add))
            link(dve.tensor_tensor(h_tok[:], h_tok[:], row(w("fc2_b")), ALU.add))
            seq = lambda ap: ap.rearrange("p (q t) -> p q t", t=T)
            cw = w("conv_w")
            dve.wait_ge(xc_copied, 1)
            link(dve.tensor_scalar(seq(cv_ch), xc_pad[:, :, 2:T + 2], cw[:, 2:3], w("conv_b"),
                                   ALU.mult, ALU.add))
            link(dve.scalar_tensor_tensor(out=seq(cw_ch), in0=xc_pad[:, :, 1:T + 1], scalar=cw[:, 1:2],
                                          in1=seq(cv_ch), op0=ALU.mult, op1=ALU.add))
            dve.scalar_tensor_tensor(out=seq(cv_ch), in0=xc_pad[:, :, 0:T], scalar=cw[:, 0:1],
                                     in1=seq(cw_ch), op0=ALU.mult, op1=ALU.add).then_inc(conv_ready, 1)
            dve.wait_ge(xc_silu, 1)
            link(dve.tensor_scalar(cv_ch, xc_ch, w("ssm_d"), None, ALU.mult))
            dve.wait_ge(cum_summed, 1)
            link(dve.scalar_tensor_tensor(out=cv_ch, in0=banks(4, 2), scalar=bcs[:, 0:1], in1=cv_ch,
                                          op0=ALU.mult, op1=ALU.add))
            dve.wait_ge(z_silu, 1)
            dve.tensor_tensor(cw_ch, cv_ch, z_ch, ALU.mult).then_inc(yz_ready, 1)
            dve.wait_ge(mix_summed, 1)
            flat = lambda t: t[:].rearrange("p j c -> p (j c)")
            link(dve.tensor_tensor(flat(x_new), flat(x_tok), banks(2, 2), ALU.add))
            layer_norm(x_new[:], n_tok[:]).then_inc(norm_ready, 1)
            link(dve.tensor_tensor(h_tok[:], h_tok[:], x_new[:], ALU.add))
            dve.wait_ge(fc2_summed, 1)
            dve.tensor_tensor(flat(h_new), flat(h_tok), banks(6, 2), ALU.add).then_inc(hx_ready, 2)
            dve.wait_ge(hx_ready, 2)

            link(layer_norm(h_new[:], x_tok[:]))
            rsqrt_scale(x_tok[:], n_tok[:], 1e-6).then_inc(norm_ready, 1)
            rope = w("rope").rearrange("p (a t) -> p a t", a=1).to_broadcast([P, PAIRS, P])
            tok = lambda ap: ap.rearrange("p (a t) -> p a t", t=P)
            for par in range(2):
                dve.wait_ge(q_summed, par + 1)
                dve.tensor_tensor(tok(qq[:, par, :]), tok(banks(2, 2)), rope, ALU.mult).then_inc(q_ready, 1)
                dve.wait_ge(k_summed, par + 1)
                dve.tensor_tensor(tok(kk[:, par, :]), tok(banks(4, 2)), rope, ALU.mult).then_inc(k_ready, 1)
            causal = w("causal").rearrange("p (a s) -> p a s", a=1).to_broadcast([P, NH, P])
            for a in range(TILES):
                dve.wait_ge(s_summed, a + 1)
                if a >= 2:
                    dve.wait_ge(exp_ready, a - 1)
                dve.tensor_tensor(sm[:, a % 2, :, :], split(ps[:, 2 + a % 2, :], NH), causal,
                                  ALU.add).then_inc(s_masked, 1)
                dve.wait_ge(s_masked, a + 1)
                cols = slice(a * NH, (a + 1) * NH)
                link(dve.tensor_reduce(mx[:, cols], sm[:, a % 2, :, :], AX.X, ALU.max))
                dve.tensor_scalar(nmx[:, cols], mx[:, cols], -HD ** -0.5, None, ALU.mult).then_inc(max_ready, 1)
            dve.wait_ge(exp_ready, TILES)
            link(dve.reciprocal(rden[:], den[:]))
            dve.wait_ge(pv_summed, TILES)
            order = rden[:].rearrange("p (v q k h) -> p v q k h", v=2, q=2, k=4)
            for par in range(2):
                for v in range(2):
                    o = y_tok[:, 8 * v + par:8 * v + 8:2, :].rearrange("p k (h d) -> p k h d", h=NH)
                    i = banks(0, 2).rearrange("p (j h d) -> p j h d", j=TILES, h=NH)[:, 8 * v + par:8 * v + 8:2, :, :]
                    r = order[:, v, par, :, :].rearrange("p k (h o) -> p k h o", o=1).to_broadcast([P, 4, NH, HD])
                    last = dve.tensor_tensor(o, i, r, ALU.mult)
            last.then_inc(y_ready, 1)
            dve.wait_ge(wo_summed, 1)
            link(dve.tensor_tensor(flat(x_new), flat(x_tok), banks(4, 2), ALU.add))
            rsqrt_scale(x_new[:], n_twice, 1e-6, twice=True).then_inc(norm_ready, 1)
            dve.wait_ge(norm_ready, 4)
            link(dve.tensor_tensor(x_new[:], x_new[:], h_new[:], ALU.add))

            dve.wait_ge(wh_ready, 2)
            for hi, lo, name in ((w1_h, w1_l, "w1"), (w3_h, w3_l, "w3")):
                dve.tensor_tensor(lo[:], m(name), hi[:].bitcast(F32), ALU.subtract).then_inc(wl_ready, 1)
            for n in range(NCHUNK):
                cols = slice(n * CHUNK * P, (n + 1) * CHUNK * P)
                dve.wait_ge(f_high, n + 1)
                dve.scalar_tensor_tensor(out=f_r[C:, cols], in0=ps[C:, n, :], scalar=w("rms2_w", C, P),
                                         in1=f_r[C:, cols].bitcast(F32), op0=ALU.mult,
                                         op1=ALU.subtract).then_inc(f_ready, 1)

            dve.wait_ge(lg_summed, 1)
            dve.tensor_copy(lg[:].rearrange("p j e -> p (j e)"), ps[:, 4, 0:TILES * NE]).then_inc(lg_ready, 1)
            dve.wait_ge(lg_ready, 1)
            link(dve.tensor_reduce(r_a[:], lg[:], AX.X, ALU.max))
            dve.tensor_tensor(lg[:], lg[:], bcast(r_a[:], NE), ALU.subtract).then_inc(lg_ready, 1)
            dve.wait_ge(lexp_ready, 1)
            link(dve.tensor_reduce(r_a[:], ep[:], AX.X, ALU.add))
            link(dve.reciprocal(r_b[:], r_a[:]))
            link(dve.tensor_tensor(ep[:], ep[:], bcast(r_b[:], NE), ALU.mult))
            expert = w("expert").rearrange("p (j e) -> p j e", e=NE)

            def first_largest(one_hot, largest):
                link(dve.tensor_reduce(largest, ep[:], AX.X, ALU.max))
                link(dve.tensor_tensor(tmp8[:], ep[:], bcast(largest, NE), ALU.is_equal))
                link(dve.tensor_tensor(tmp8[:], tmp8[:], expert, ALU.mult))
                link(dve.tensor_reduce(r_c[:], tmp8[:], AX.X, ALU.min))
                link(dve.tensor_tensor(one_hot[:], expert, bcast(r_c[:], NE), ALU.is_equal))

            first_largest(oh1, r_a[:])
            link(dve.scalar_tensor_tensor(out=ep[:], in0=oh1[:], scalar=-2.0, in1=ep[:], op0=ALU.mult, op1=ALU.add))
            first_largest(oh2, r_b[:])
            link(dve.tensor_tensor(r_c[:], r_a[:], r_b[:], ALU.add))
            link(dve.tensor_scalar(r_c[:], r_c[:], 1e-9, None, ALU.add))
            link(dve.reciprocal(r_d[:], r_c[:]))
            link(dve.tensor_tensor(r_a[:], r_a[:], r_d[:], ALU.mult))
            link(dve.tensor_tensor(r_b[:], r_b[:], r_d[:], ALU.mult))
            link(dve.tensor_tensor(oh1[:], oh1[:], bcast(r_a[:], NE), ALU.mult))
            link(dve.tensor_tensor(oh2[:], oh2[:], bcast(r_b[:], NE), ALU.mult))
            link(dve.tensor_tensor(gate[:], oh1[:], oh2[:], ALU.add))

            def weigh(a):
                dve.wait_ge(eo_summed, a + 1)
                dve.tensor_tensor(eo[:, a % 2, :, :], ps[:, 4 + a % 2, :].rearrange("p (e c) -> p e c", c=C),
                                  bcast(gate[:, a, :], C), ALU.mult).then_inc(eo_weighted, 1)
                dve.wait_ge(eo_weighted, a + 1)
                link(dve.tensor_reduce(n_tok[:, a, :], eo[:, a % 2, :, :].rearrange("p e c -> p c e"),
                                       AX.X, ALU.add))

            dve.wait_ge(f_turned, NCHUNK)
            for n in range(NCHUNK):
                for b in range(NHB):
                    k = n * NHB + b
                    dve.wait_ge(silu_ready, k + 1)
                    dve.wait_ge(e3_summed, k + 1)
                    if n and b == 0:
                        dve.wait_ge(eo_summed, CHUNK * n)
                    dve.tensor_tensor(hh[:, b, :], act_h[:, k % 2, :], ps[0:HB, 2 + k % 2, :],
                                      ALU.mult).then_inc(hh_ready, 1)
                for k in range(CHUNK):
                    weigh(CHUNK * n + k)
            dve.tensor_tensor(y_tok[:], x_new[:], n_tok[:], ALU.add).then_inc(out_ready, 1)


def layout(inputs):
    f = {k: np.asarray(v) for k, v in inputs.items()}
    tok = lambda n: f["L0_tok_" + n]
    at = lambda n: f["L0_attn_" + n]
    fn = lambda n: f["L0_ffn_" + n]
    bn = lambda i, rows: np.concatenate([np.broadcast_to(tok(f"{n}{i}"), (rows, tok(f"{n}{i}").shape[0]))
                                         for n in ("g", "v", "b", "m", "be")], axis=1)

    def pack(parts, where, width):
        out = np.zeros((P, width), np.float32)
        for name, a in parts.items():
            o, n = where[name]
            out[:a.shape[0], o:o + n] = a.reshape(a.shape[0], n)
        return out

    rows = np.arange(PARTS * GROUP) % GROUP
    w0 = np.zeros((PARTS, 4, SF, C1), np.float32)
    w0[:, :CIN] = np.broadcast_to(tok("W0")[None, :, None, :], (PARTS, CIN, SF, C1))
    xt0 = np.zeros((V + 1, STEPS, PARTS, GROUP), np.float32)
    xt0[V, :, :, CIN * SF] = 1.0
    gcn = pack({
        "at": np.concatenate([tok("A").T, np.ones((1, V), np.float32)]),
        "a": tok("A"), "w1": tok("W1"), "w2": tok("W2"), "w0": w0.reshape(PARTS * GROUP, C1),
        "bn0": bn(0, PARTS * GROUP), "bn2": bn(2, P),
        "bn1": np.stack([tok(f"{n}1") for n in ("g", "v", "b", "m", "be")], axis=1),
        "bias_row": (rows == CIN * SF).astype(np.float32)[:, None],
        "own_frame": ((rows[:, None] % SF == np.arange(SF)[None, :])
                      | (rows[:, None] == CIN * SF)).astype(np.float32),
        "xt0": xt0, "ident": np.eye(P, dtype=np.float32),
        "mean_v": np.full((V, P), 1.0 / V, np.float32),
    }, GCN_AT, GCN_N)

    def diag2(a):
        out = np.zeros((2 * a.shape[0], 2 * a.shape[1]), np.float32)
        out[:a.shape[0], :a.shape[1]] = a
        out[a.shape[0]:, a.shape[1]:] = a
        return out

    def twice(a):
        a = a.reshape(C, -1)
        return np.concatenate([a, a])

    swap = np.concatenate([np.arange(HD // 2, HD), np.arange(HD // 2)])
    wq = fn("wq").reshape(NH, HD, C)
    wk = np.repeat(fn("wk").reshape(NKV, HD, C), NH // NKV, axis=0)
    turned = lambda a: np.concatenate([a.reshape(NH * HD, C), a[:, swap].reshape(NH * HD, C)]).T
    inv_freq = 1.0 / 10000.0 ** (np.arange(0, HD, 2, dtype=np.float32) / HD)
    freqs = np.outer(np.arange(T, dtype=np.float32), inv_freq)
    emb = np.concatenate([freqs, freqs], axis=-1)
    sign = np.where(np.arange(HD) < HD // 2, -1.0, 1.0).astype(np.float32)
    cos, sin = np.cos(emb).T, np.sin(emb).T * sign[:, None]
    rope = np.concatenate([np.tile(cos, (NH, 2)), np.tile(sin, (NH, 2))]).astype(np.float32)
    s, t = np.arange(P)[:, None], np.arange(P)[None, :]
    same = s // T == t // T
    eye = np.eye(C, dtype=np.float32)
    tail = pack({
        "bd_xc": diag2(at("in_proj_w")[:C].T), "bd_z": diag2(at("in_proj_w")[C:].T),
        "bd_out": diag2(at("out_proj_w").T),
        "bd_fc1": np.concatenate([diag2(at("fc1_w")[b * C:(b + 1) * C].T) for b in range(FFB)], axis=1),
        "bd_fc2": np.concatenate([diag2(at("fc2_w")[:, b * C:(b + 1) * C].T) for b in range(FFB)], axis=1),
        "bd_wo": diag2(fn("wo").T),
        "wq": twice(turned(wq)), "wk": twice(turned(wk)), "wv": diag2(fn("wv").T),
        "router": twice(fn("router_w").T),
        "fc2_b": np.broadcast_to(at("fc2_b"), (P, C)),
        "ln1_w": twice(at("ln1_w")), "ln1_b": twice(at("ln1_b")), "conv_w": twice(at("conv_w")),
        "conv_b": twice(at("conv_b")), "ssm_b": twice(at("ssm_B")), "ssm_c": twice(at("ssm_C")),
        "ssm_d": twice(at("ssm_D")), "ln2_w": twice(at("ln2_w")), "ln2_b": twice(at("ln2_b")),
        "fc1_b": np.concatenate([at("fc1_b").reshape(FFB, C).T] * 2),
        "rms1_w": twice(fn("ln1_w")), "rms2_w": twice(fn("ln2_w")),
        "tri": (same & (s <= t)).astype(np.float32),
        "causal": np.where(same & (t <= s), 0.0, MASKED).astype(np.float32),
        "rope": rope, "fold": np.block([[eye, eye], [eye, eye]]).astype(np.float32),
        "head": (np.arange(P)[:, None] % (NH * HD) // HD == np.arange(NH)[None, :]).astype(np.float32),
        "expert": np.broadcast_to(np.tile(np.arange(NE) - NE, TILES), (P, TILES * NE)).astype(np.float32),
    }, TAIL_AT, TAIL_N)
    up = lambda a: twice(a.reshape(NHB * HB, C).T)
    moe = pack({
        "w1": up(fn("w1")), "w3": up(fn("w3")),
        "w2": fn("w2").reshape(NE, C, 2, HB).transpose(3, 0, 2, 1),
    }, MOE_AT, MOE_N)
    return {"x": f["x"].reshape(FRAMES, V * CIN), "gcn": gcn, "tail": tail, "moe": moe}


def kernel(**inputs):
    import concourse.bacc as bacc
    from concourse.bass_utils import run_bass_kernel_spmd

    nc = bacc.Bacc("TRN2", target_bir_lowering=False, num_devices=1)
    arrays = layout(inputs)
    args = [nc.dram_tensor(k, a.shape, F32, kind="ExternalInput").ap() for k, a in arrays.items()]
    out = nc.dram_tensor("out", (FRAMES, C), F32, kind="ExternalOutput").ap()
    program(nc, *args, out)
    r = run_bass_kernel_spmd(nc, [arrays], core_ids=[0])
    return r.results[0]["out"].reshape(SEQS, T, C)
```

```python
from contextlib import ExitStack

import numpy as np

import concourse.bass as bass
from concourse import mybir

F32 = mybir.dt.float32
F32R = mybir.dt.float32r
BF16 = mybir.dt.bfloat16
ALU = mybir.AluOpType
ACT = mybir.ActivationFunctionType
AX = mybir.AxisListType

P = 128
SEQS, T, V, CIN, C1, C = 32, 64, 75, 3, 128, 64
FRAMES = SEQS * T
TILES = FRAMES // P
PAIRS = TILES // 2
SF = 12
NSTEP = -(-FRAMES // SF)
SUMS = NSTEP * SF
STEPS = 8
GF = STEPS * SF
GTILES = -(-NSTEP // STEPS)
LOOP = NSTEP // STEPS - 1
REST = NSTEP - LOOP * STEPS
HALF = SF // 2 * V
TRIO = 3 * V
BR = TRIO // 2 + 1
BLOCKS = 2 * SF // 3
PRODUCTS = [(0, 0), (0, 1), (0, 2), (1, 0), (1, 1), (2, 0)]
XR = len(PRODUCTS) * CIN + 3
LOADS = 16 * len(PRODUCTS)
FFB = 4
NH, HD, NKV, NE = 4, 16, 2, 8
HID = int(8 / 3 * C)
NHID = NE * HID
NHB = -(-NHID // P)
MASKED = -1e30
HT, HP, HC = TILES // 2, PAIRS // 2, PAIRS // 2 * P
GT = 4
VW = HD + 1
CHUNK = 2
CT = CHUNK * P
LAG = 3


def offsets(parts):
    at, out = 0, {}
    for name, n in parts:
        out[name] = (at, n)
        at += n
    return out, at


GCN_PARTS = [("at", V), ("w0", C1), ("bn0", 5 * C1), ("bn1", 5), ("bn2", 5 * C), ("bias_row", 1), ("part", 3),
             ("a", V), ("mean_v", P), ("mix", 2 * 2 * V), ("w1", C1), ("w2", C), ("ident", P)]
FIRST = "a"
TAIL_PARTS = [("bd_xc", P), ("bd_z", P), ("bd_out", P), ("bd_fc1", FFB * P), ("bd_fc2", FFB * P),
              ("bd_wo", P), ("wq", P), ("wk", P), ("wv", 2 * NKV * HD), ("router", NE),
              ("fc2_b", C), ("ln1_w", 1), ("ln1_b", 1), ("conv_w", 3), ("conv_b", 1), ("ssm_b", 8),
              ("ssm_c", 8), ("ssm_d", 1), ("ln2_w", 1), ("ln2_b", 1), ("fc1_b", FFB), ("rms1_w", 1),
              ("rms2_w", 1), ("tri", P), ("causal", T), ("rope", P), ("fold", P),
              ("head", NH), ("expert", TILES * NE)]
MOE_PARTS = [("w1", NHID), ("w3", NHID), ("w2", NHB * 2 * C)]


def block_of_hidden(b):
    first, last = b * P, min((b + 1) * P, NHID) - 1
    return last - first + 1, first // HID, last // HID - first // HID + 1


GCN_AT, GCN_N = offsets(GCN_PARTS)
TAIL_AT, TAIL_N = offsets(TAIL_PARTS)
MOE_AT, MOE_N = offsets(MOE_PARTS)


def program(nc, x, gcn, tail, moe, out):
    ctx = ExitStack()
    with ctx:
        def sb(name, shape, dt=F32):
            return ctx.enter_context(nc.sbuf_tensor(name, shape, dt))

        def sem(name):
            return ctx.enter_context(nc.semaphore(name))

        gcn_sb = sb("gcn_sb", [P, GCN_N])
        tail_sb = sb("tail_sb", [P, TAIL_N])
        moe_sb = sb("moe_sb", [P, MOE_N])

        def g(name, rows=P):
            at, n = GCN_AT[name]
            return gcn_sb[0:rows, at:at + n]

        def w(name, r0=0, r1=P):
            at, n = TAIL_AT[name]
            return tail_sb[r0:r1, at:at + n]

        def m(name, rows=P):
            at, n = MOE_AT[name]
            return moe_sb[0:rows, at:at + n]

        x_tile = sb("x_tile", [V, CIN * GF])
        gx_parts = sb("gx_parts", [GF, 3, CIN, V], BF16)
        gx_rest = sb("gx_rest", [GF, CIN * V])
        gx_rows = nc.dram_tensor("gx_rows", (3, CIN, GF, V), BF16).ap()
        buf_s = sb("buf_s", [P, 2, NH * P])
        buf_p = sb("buf_p", [P, 2, NH * T])
        buf_t = sb("buf_t", [P, CHUNK * NE * C])
        buf_ch = sb("buf_ch", [P, 4, PAIRS * P])
        buf_ff = sb("buf_ff", [P, FFB, PAIRS * P])
        gxr = buf_ff[:].rearrange("p a b -> p (a b)").bitcast(BF16)[:, 0:GF * V].rearrange("p (b n) -> p b n", b=2)
        buf_r = sb("buf_r", [P, 8 * HALF], F32R)
        buf_1 = sb("buf_1", [P, 2 * BLOCKS * C1 + 8 * HALF + SUMS])
        w0_b = sb("w0_b", [XR, C1], BF16)
        w0_p = sb("w0_p", [XR, 2, C1], BF16)
        w0_t = sb("w0_t", [XR, 2, C1])
        at = 2 * BLOCKS * C1
        h1 = buf_1[0:BR, 0:at].rearrange("v (b k c) -> v b k c", b=2, c=C1)
        h2, h2w = (buf_1[:, at + n * 4 * HALF:at + (n + 1) * 4 * HALF].rearrange("p (b n) -> p b n", b=2)
                   for n in range(2))
        sums = buf_1[:, at + 8 * HALF:at + 8 * HALF + SUMS]
        gh, gl = (buf_r[:, n * 4 * HALF:(n + 1) * 4 * HALF].rearrange("p (b n) -> p b n", b=2) for n in range(2))
        w1g_h = sb("w1g_h", [P, C1], F32R)
        w1g_l = sb("w1g_l", [P, C1], F32R)
        mean_a = sb("mean_a", [P, V])
        c0 = sb("c0", [XR, C1])
        w0s = sb("w0s", [XR, C1])
        c1 = sb("c1", [P, 1])
        c2 = sb("c2", [P, C])
        bn_e = sb("bn_e", [P, C1 + 1 + C])
        bn_t = sb("bn_t", [P, 2, C1 + 1 + C])

        h_tok = sb("h_tok", [P, TILES, C])
        h_new = sb("h_new", [P, TILES, C])
        x_tok = sb("x_tok", [P, TILES, C])
        x_new = sb("x_new", [P, TILES, C])
        n_tok = sb("n_tok", [P, TILES, C])
        d_tok = sb("d_tok", [P, TILES, C])
        y_tok = sb("y_tok", [P, TILES, C])
        q_tok = y_tok
        row_a = sb("row_a", [P, TILES])
        row_v = sb("row_v", [P, TILES])
        row_t = sb("row_t", [P, 2, TILES])
        n_ch = sb("n_ch", [P, PAIRS * P])
        xc_pad = sb("xc_pad", [P, SEQS // 2, T + 2])
        xc_ch, cv_ch, cw_ch, z_ch = (buf_ch[:, n, :] for n in range(4))
        xc_tok = sb("xc_tok", [P, PAIRS, P])
        bc = sb("bc", [P, 8])
        bcs = sb("bcs", [P, 1])
        ff = buf_ff
        qq, kk = buf_ff[:, 0:2, :], buf_ff[:, 2:4, :]
        kb = buf_ch[:].rearrange("p b n -> p (b n)").rearrange("p (b k q h s) -> p b k q h s", b=2, k=GT, q=2, h=NH)
        vb = buf_1[:, 0:TILES * 4 * 2 * VW]
        n_twice = buf_1[:, NHB * CT:NHB * CT + TILES * 2 * C].rearrange("p (j a c) -> p j a c", j=TILES, a=2)
        sm = buf_s[:, :, 0:NH * T]
        pr = buf_p
        pt = buf_t[:, 0:4 * P].rearrange("p (b n) -> p b n", b=2)
        mx = sb("mx", [P, 2, NH])
        rden = sb("rden", [P, GT * NH])
        f_r = buf_r[:, 0:TILES * P]
        w1_h = sb("w1_h", [P, NHID], F32R)
        w3_h = sb("w3_h", [P, NHID], F32R)
        w1_l = sb("w1_l", [P, NHID], F32R)
        w3_l = sb("w3_l", [P, NHID], F32R)
        lg = sb("lg", [P, TILES, NE])
        ep = sb("ep", [P, TILES, NE])
        oh1 = sb("oh1", [P, TILES, NE])
        oh2 = sb("oh2", [P, TILES, NE])
        tmp8 = sb("tmp8", [P, TILES, NE])
        gate = sb("gate", [P, TILES, NE])
        r_a = sb("r_a", [P, TILES])
        r_b = sb("r_b", [P, TILES])
        r_c = sb("r_c", [P, TILES])
        r_d = sb("r_d", [P, TILES])
        act_h = buf_p
        hh = buf_1[:, 0:NHB * CT].rearrange("p (b n) -> p b n", b=NHB)
        eo = buf_t
        ps = ctx.enter_context(nc.psum_tensor("ps", [P, 8, 512], F32))

        gcn_loaded, tail_loaded, moe_loaded = sem("gcn_loaded"), sem("tail_loaded"), sem("moe_loaded")
        gcn_rest_loaded, x_loaded = sem("gcn_rest_loaded"), sem("x_loaded")
        gx_summed, gx_part0, gx_left, gx_part1, gx_part2 = (
            sem("gx_summed"), sem("gx_part0"), sem("gx_left"), sem("gx_part1"), sem("gx_part2"))
        ones_ready, rows_stored = sem("ones_ready"), sem("rows_stored")
        rows_loaded = [sem("rows_loaded_a"), sem("rows_loaded_b")]
        mean_summed, mean_ready = sem("mean_summed"), sem("mean_ready")
        inverse_ready, guess_ready = sem("inverse_ready"), sem("guess_ready")
        w0_ready, w1g_high, w1g_low, bn1_ready = sem("w0_ready"), sem("w1g_high"), sem("w1g_low"), sem("bn1_ready")
        g_high = sem("g_high")
        h1_summed = sem("h1_summed")
        h1_ready = [sem("h1_ready_a"), sem("h1_ready_b")]
        g_summed, g_ready = sem("g_summed"), sem("g_ready")
        h2_summed, h2_ready = sem("h2_summed"), sem("h2_ready")
        h2_free, h2w_free = sem("h2_free"), sem("h2w_free")
        h_summed = sem("h_summed")
        norm_ready, norm_turned, norm_ch = sem("norm_ready"), sem("norm_turned"), sem("norm_ch")
        pad_zero, xz_summed, xc_copied, conv_ready, xc_silu, z_silu = (
            sem("pad_zero"), sem("xz_summed"), sem("xc_copied"), sem("conv_ready"), sem("xc_silu"),
            sem("z_silu"))
        xc_turned, xc_tok_ready, cum_summed, yz_ready, mix_summed, h_new_ready = (
            sem("xc_turned"), sem("xc_tok_ready"), sem("cum_summed"), sem("yz_ready"),
            sem("mix_summed"), sem("h_new_ready"))
        fc1_summed, gelu_ready, fc2_summed = sem("fc1_summed"), sem("gelu_ready"), sem("fc2_summed")
        q_summed, q_ready, k_summed, k_ready, v_summed, v_ready = (
            sem("q_summed"), sem("q_ready"), sem("k_summed"), sem("k_ready"), sem("v_summed"),
            sem("v_ready"))
        vb_zero, vb_ones = sem("vb_zero"), sem("vb_ones")
        kf_summed, kb_ready, s_summed, s_masked, s_shifted, exp_ready, pt_turned, pt_ready = (
            sem("kf_summed"), sem("kb_ready"), sem("s_summed"), sem("s_masked"), sem("s_shifted"),
            sem("exp_ready"), sem("pt_turned"), sem("pt_ready"))
        pv_summed, y_ready, y_turned, y_ch, wo_summed, x4_ready, resid_ready = (
            sem("pv_summed"), sem("y_ready"), sem("y_turned"), sem("y_ch"), sem("wo_summed"),
            sem("x4_ready"), sem("resid_ready"))
        f_turned, f_high, f_ready, wh_ready, wl_ready = (
            sem("f_turned"), sem("f_high"), sem("f_ready"), sem("wh_ready"), sem("wl_ready"))
        lg_summed, lg_ready, lexp_ready = sem("lg_summed"), sem("lg_ready"), sem("lexp_ready")
        e1_summed, e3_summed, silu_ready, hh_ready, eo_summed, eo_free, out_ready, stored = (
            sem("e1_summed"), sem("e3_summed"), sem("silu_ready"), sem("hh_ready"),
            sem("eo_summed"), sem("eo_free"), sem("out_ready"), sem("stored"))
        chunk_summed = sem("chunk_summed")
        dve_chain = sem("dve_chain")

        h1_ps = ps[0:BR, 0:2, :]
        g_ps = ps[:, 2:4, 0:HALF]
        h2_ps = ps[:, 4:6, 0:HALF]
        gx_ps = ps[0:GF, 7, 0:CIN * V]

        def split(ap, a):
            return ap.rearrange("p (a b) -> p a b", a=a)

        ident = g("ident")
        TURN_Y = 12

        block = ctx.enter_context(nc.Block())

        @block.sync
        def _(sp):
            first = GCN_AT[FIRST][0]
            sp.dma_start(gcn_sb[:, 0:first], gcn[:, 0:first]).then_inc(gcn_loaded, 16)
            sp.dma_start(x_tile[:], x[0:V, :]).then_inc(x_loaded, 16)
            sp.dma_start(gcn_sb[:, first:], gcn[:, first:]).then_inc(gcn_rest_loaded, 16)
            for j in range(GTILES):
                sp.wait_ge(gx_part2, j + 1)
                if j:
                    for half in range(2):
                        sp.wait_ge(rows_loaded[half], LOADS * j)
                sp.dma_start(gx_rows.rearrange("p c f v -> f (p c) v"),
                             gx_parts[:].rearrange("f p c v -> f (p c) v")).then_inc(rows_stored, 16)
                if j == 0:
                    sp.wait_ge(ones_ready, 1)
                if j + 1 < GTILES:
                    sp.wait_ge(gx_summed, j + 1)
                    sp.dma_start(x_tile[:], x[(j + 1) * V:(j + 2) * V, :]).then_inc(x_loaded, 16)
                sp.wait_ge(rows_stored, 16 * (j + 1))
                for half in range(2):
                    if (2 * j + half) * STEPS // 2 >= NSTEP:
                        continue
                    if j:
                        sp.wait_ge(h1_summed, 2 * (STEPS * (j - 1) + STEPS // 2 * (half + 1)))
                    for n, (part, _) in enumerate(PRODUCTS):
                        sp.dma_start(gxr[n * CIN:(n + 1) * CIN, half, :].rearrange("c (f v) -> c f v", v=V),
                                     gx_rows[part, :, half * GF // 2:(half + 1) * GF // 2, :]
                                     ).then_inc(rows_loaded[half], 16)
                if j == 0:
                    sp.dma_start(tail_sb[:], tail).then_inc(tail_loaded, 16)
                    sp.dma_start(moe_sb[:], moe).then_inc(moe_loaded, 16)
            for n in range(TILES // (2 * CHUNK)):
                tiles = slice(2 * CHUNK * n, 2 * CHUNK * (n + 1))
                sp.wait_ge(out_ready, 2 * (n + 1))
                sp.dma_start(out.rearrange("(j p) c -> p j c", p=P)[:, tiles, :],
                             y_tok[:, tiles, :]).then_inc(stored, 16)
            sp.wait_ge(stored, 16 * (TILES // (2 * CHUNK)))

        @block.tensor
        def _(pe):
            def gx_sums(j):
                pe.wait_ge(x_loaded, 16 * (j + 1))
                for c in range(CIN):
                    mm = pe.matmul(gx_ps[:, c * V:(c + 1) * V], x_tile[:, c * GF:(c + 1) * GF], g("at", V),
                                   start=True, stop=True)
                mm.then_inc(gx_summed, 1)

            def layer0(s):
                half, k = divmod(s % STEPS, STEPS // 2)
                for b in range(BLOCKS):
                    at = (k * SF + b // 2 * 3) * V + b % 2 * (BR - 1)
                    mm = pe.matmul(ps[0:BR, 2 * b // BLOCKS, b % (BLOCKS // 2) * C1:(b % (BLOCKS // 2) + 1) * C1],
                                   gxr[0:XR, half, at:at + BR], w0_b[:], start=True, stop=True)
                    if b % (BLOCKS // 2) == BLOCKS // 2 - 1:
                        mm.then_inc(h1_summed, 1)

            def mix(par):
                for b in range(BLOCKS):
                    v, k = divmod(b, BLOCKS // 2)
                    at = k // 2 * TRIO + k % 2 * V
                    mm = pe.matmul(g_ps[:, v, at:at + 2 * V], h1[:, par, b, :],
                                   g("mix", BR)[:, b % 2 * 2 * V:(b % 2 + 1) * 2 * V],
                                   start=(k == 0), stop=(k == BLOCKS // 2 - 1), skip_group_check=True)
                    if k == BLOCKS // 2 - 1:
                        mm.then_inc(g_summed, 1)

            def layer1(par):
                for v in range(2):
                    cols = slice(v * HALF, (v + 1) * HALF)
                    pe.matmul(h2_ps[:, v, :], w1g_h[:], gh[:, par, cols], start=True, stop=False)
                    pe.matmul(h2_ps[:, v, :], w1g_h[:], gl[:, par, cols], start=False, stop=False)
                    mm = pe.matmul(h2_ps[:, v, :], w1g_l[:], gh[:, par, cols], start=False, stop=True)
                mm.then_inc(h2_summed, 1)

            pe.wait_ge(gcn_loaded, 16)
            gx_sums(0)
            pe.wait_ge(gcn_rest_loaded, 16)
            pe.matmul(ps[:, 0, 0:V], g("mean_v", V), g("a", V), start=True, stop=True).then_inc(mean_summed, 1)
            pe.wait_ge(w0_ready, 1)
            pe.wait_ge(mean_ready, 1)
            pe.wait_ge(rows_loaded[0], LOADS)
            layer0(0)
            pe.wait_ge(h1_ready[0], 1)
            pe.wait_ge(h1_ready[1], 1)
            mix(0)
            layer0(1)
            pe.wait_ge(w1g_low, 1)

            def tile(i, steps):
                at = i * STEPS
                for s in range(steps or STEPS):
                    if not steps or s + 1 < steps:
                        pe.wait_ge(h1_ready[0], at + s + 2)
                        pe.wait_ge(h1_ready[1], at + s + 2)
                    if not steps or s + 2 < steps:
                        if (s + 2) % (STEPS // 2) == 0:
                            j, half = divmod((s + 2) // (STEPS // 2), 2)
                            pe.wait_ge(rows_loaded[half], LOADS * (i + j + 1))
                        layer0(s + 2)
                    pe.wait_ge(g_ready, 2 * (at + s + 1))
                    if not steps or s + 1 < steps:
                        mix((s + 1) % 2)
                    pe.wait_ge(h2_ready, at + s)
                    layer1(s % 2)
                    if s == 0:
                        pe.wait_ge(gx_part2, i + 1)
                        gx_sums(i + 1)

            with pe.Fori(0, LOOP) as i:
                tile(i, 0)
            tile(LOOP, REST)

            pe.wait_ge(h2w_free, 2 + NSTEP)
            for d in range(2):
                for k in range(HT):
                    j = HT * d + k
                    mm = pe.matmul(ps[:, d, k * C:(k + 1) * C], sums[:, j * P:(j + 1) * P], g("w2"),
                                   start=True, stop=True)
                mm.then_inc(h_summed, 1)

            def turn_pairs(src, bank, d, done):
                for p in range(HP):
                    j = 2 * (HP * d + p)
                    mm = pe.transpose(ps[:, bank, p * P:(p + 1) * P], src[:, j:j + 2, :], ident)
                mm.then_inc(done, 1)

            def turn_norm(n, bank, d):
                pe.wait_ge(norm_ready, 2 * n + d + 1)
                turn_pairs(n_tok, bank, d, norm_turned)
                pe.wait_ge(norm_ch, 2 * n + d + 1)

            def half(d):
                return slice(HC * d, HC * (d + 1))

            def column(d, p):
                return slice(HC * d + p * P, HC * d + (p + 1) * P)

            pe.wait_ge(tail_loaded, 16)
            pe.wait_ge(g_ready, 2 * NSTEP)
            pe.wait_ge(h2_ready, NSTEP)
            for d in range(2):
                turn_norm(0, 2 + d, d)
                pe.matmul(ps[:, 4 + d, :], w("bd_xc"), n_ch[:, half(d)], start=True, stop=True).then_inc(xz_summed, 1)
                pe.matmul(ps[:, 6 + d, :], w("bd_z"), n_ch[:, half(d)], start=True, stop=True).then_inc(xz_summed, 1)
            for d in range(2):
                pe.wait_ge(xc_silu, d + 1)
                for p in range(HP):
                    mm = pe.transpose(ps[:, 2 + d, p * P:(p + 1) * P], xc_ch[:, column(d, p)], ident)
                mm.then_inc(xc_turned, 1)
                pe.wait_ge(xc_tok_ready, d + 1)
                for p in range(HP):
                    mm = pe.matmul(ps[:, 4 + d, p * P:(p + 1) * P], xc_tok[:, HP * d + p, :], w("tri"),
                                   start=True, stop=True)
                mm.then_inc(cum_summed, 1)
            for d in range(2):
                pe.wait_ge(yz_ready, d + 1)
                for p in range(HP):
                    mm = pe.matmul(ps[:, 2 + d, p * P:(p + 1) * P], cw_ch[:, column(d, p)], w("bd_out"),
                                   start=True, stop=True)
                mm.then_inc(mix_summed, 1)
            for d in range(2):
                turn_norm(1, 6 + d, d)
                for fb in range(FFB):
                    if fb >= 2:
                        pe.wait_ge(gelu_ready, FFB * d + fb - 1)
                    pe.matmul(ps[:, 4 * (fb % 2) + d, :], w("bd_fc1")[:, fb * P:(fb + 1) * P], n_ch[:, half(d)],
                              start=True, stop=True).then_inc(fc1_summed, 1)
            for d in range(2):
                pe.wait_ge(gelu_ready, FFB * (d + 1))
                for p in range(HP):
                    for fb in range(FFB):
                        mm = pe.matmul(ps[:, 2 + d, p * P:(p + 1) * P], ff[:, fb, column(d, p)],
                                       w("bd_fc2")[:, fb * P:(fb + 1) * P],
                                       start=(fb == 0), stop=(fb == FFB - 1))
                mm.then_inc(fc2_summed, 1)

            for d in range(2):
                turn_norm(2, 6 + d, d)
                for par in range(2):
                    if d:
                        pe.wait_ge(q_ready, par + 1)
                        pe.wait_ge(k_ready, par + 1)
                    rows = slice(par * C, (par + 1) * C)
                    pe.matmul(ps[:, par, :], w("wq", par * C, par * C + C), n_ch[rows, half(d)],
                              start=True, stop=True).then_inc(q_summed, 1)
                    pe.matmul(ps[:, 4 + par, :], w("wk", par * C, par * C + C), n_ch[rows, half(d)],
                              start=True, stop=True).then_inc(k_summed, 1)
                pe.wait_ge(h_new_ready, d + 1)
                for p in range(HP):
                    for q in range(2):
                        at = HC * d + p * P + q * T
                        for a in range(2):
                            mm = pe.matmul(ps[a * T:(a + 1) * T, 2 + d, (2 * p + q) * C:(2 * p + q + 1) * C],
                                           n_ch[:, at:at + T], w("wv"), start=True, stop=True)
                mm.then_inc(v_summed, 1)

            def fold_keys(n):
                d, par = divmod(n, 2)
                pe.wait_ge(k_ready, n + 1)
                if n:
                    pe.wait_ge(kb_ready, n)
                pe.matmul(ps[:, 7, :], w("fold"), kk[:, par, half(d)], start=True, stop=True).then_inc(kf_summed, 1)

            def scores(a):
                n, k = divmod(a, GT)
                d, par = divmod(n, 2)
                pe.wait_ge(kb_ready, n + 1)
                if a >= 2:
                    pe.wait_ge(s_masked, a - 1)
                for q in range(2):
                    at = HC * d + k * P + q * T
                    mm = pe.matmul(ps[q * T:(q + 1) * T, 2 + a % 2, 0:NH * T], qq[:, par, at:at + T],
                                   kb[:, n % 2, k, q, :, :].rearrange("p h s -> p (h s)"),
                                   start=True, stop=True)
                mm.then_inc(s_summed, 1)

            def turn_probs(a):
                pe.wait_ge(exp_ready, a + 1)
                if a >= 2:
                    pe.wait_ge(pt_ready, a - 1)
                for kv in range(NKV):
                    mm = pe.transpose(ps[:, 4 + a % 2, kv * P:(kv + 1) * P], pr[:, a % 2, kv * P:(kv + 1) * P], ident)
                mm.then_inc(pt_turned, 1)

            def values(a):
                n, k = divmod(a, GT)
                d, par = divmod(n, 2)
                pe.wait_ge(pt_ready, a + 1)
                if k == 0 and n >= 2:
                    pe.wait_ge(y_ready, n - 1)
                for q in range(2):
                    for kv in range(NKV):
                        at = ((((d * HP + k) * 2 + q) * 2 + par) * NKV + kv) * 2 * VW
                        o = (k * NKV + kv) * 2 * VW
                        mm = pe.matmul(ps[q * T:(q + 1) * T, n % 2, o:o + 2 * VW],
                                       pt[:, a % 2, kv * P + q * T:kv * P + (q + 1) * T], vb[:, at:at + 2 * VW],
                                       start=True, stop=True)
                mm.then_inc(pv_summed, 1)

            def turn_y(d):
                pe.wait_ge(y_ready, 2 * (d + 1))
                turn_pairs(y_tok, 6, d, y_turned)

            def project_y(d):
                pe.wait_ge(y_ch, d + 1)
                for p in range(HP):
                    mm = pe.matmul(ps[:, 6, p * P:(p + 1) * P], n_ch[:, column(d, p)], w("bd_wo"),
                                   start=True, stop=True)
                mm.then_inc(wo_summed, 1)

            pe.wait_ge(v_ready, 4)
            fold_keys(0)
            for a in range(TILES + 2):
                if a == TURN_Y:
                    turn_y(0)
                if a == TURN_Y + 1:
                    project_y(0)
                if a < TILES:
                    if a % GT == 0 and a // GT + 1 < TILES // GT:
                        fold_keys(a // GT + 1)
                    scores(a)
                if 1 <= a <= TILES:
                    turn_probs(a - 1)
                if a >= 2:
                    values(a - 2)
            pe.wait_ge(x4_ready, 1)
            turn_y(1)
            project_y(1)

            for n in range(TILES // GT):
                pe.wait_ge(norm_ready, 6 + n // 2 + 1)
                for k in range(GT):
                    mm = pe.transpose(ps[:, 2 + n, k * P:(k + 1) * P],
                                      n_twice[:, GT * n + k, :, :].rearrange("p a c -> p (a c)"), ident)
                mm.then_inc(f_turned, 1)
            pe.wait_ge(f_ready, TILES // GT)
            pe.wait_ge(x4_ready, 2)
            for j in range(TILES):
                mm = pe.matmul(ps[:, 6, j * NE:(j + 1) * NE], f_r[:, j * P:(j + 1) * P].bitcast(F32),
                               w("router"), start=True, stop=True)
            mm.then_inc(lg_summed, 1)
            pe.wait_ge(wl_ready, 2)
            pe.wait_ge(lg_ready, 1)

            def up(k, step, cols):
                b = step % NHB
                rows = block_of_hidden(b)[0]
                for bank, hi, lo, done, free in ((0, w1_h, w1_l, e1_summed, silu_ready),
                                                 (2, w3_h, w3_l, e3_summed, hh_ready)):
                    if free is not None and step >= 2:
                        pe.wait_ge(free, k - 1)
                    o = ps[0:rows, bank + step % 2, 0:CT]
                    part = slice(b * P, b * P + rows)
                    pe.matmul(o, hi[:, part], f_r[:, cols], start=True, stop=False)
                    pe.matmul(o, lo[:, part], f_r[:, cols], start=False, stop=True).then_inc(done, 1)

            def down(k, step, i):
                c, b = divmod(step, NHB)
                rows, e, ne = block_of_hidden(b)
                pe.wait_ge(hh_ready, k + 1)
                if b == 0:
                    pe.wait_ge(eo_free, 2 * (i * 2 + c + 1))
                for t in range(CHUNK):
                    mm = pe.matmul(ps[:, 4 + CHUNK * c + t, e * C:(e + ne) * C], hh[0:rows, b, t * P:(t + 1) * P],
                                   m("w2", rows)[:, b * 2 * C:(b * 2 + ne) * C], start=(b == 0),
                                   stop=(b == NHB - 1), skip_group_check=True)
                if b == NHB - 1:
                    mm.then_inc(eo_summed, 1)

            for k in range(LAG):
                up(k, k, slice(0, CT))

            def two_chunks(i, last):
                for step in range(2 * NHB):
                    ahead = step + LAG
                    if not (last and ahead >= 2 * NHB):
                        at = (i * 2 + ahead // NHB) * CT
                        up(i * 2 * NHB + ahead, ahead, slice(at, at + CT) if last else bass.ds(at, CT))
                    down(i * 2 * NHB + step, step, i)

            with pe.Fori(0, TILES // (2 * CHUNK) - 1) as i:
                two_chunks(i, False)
            two_chunks(TILES // (2 * CHUNK) - 1, True)

        @block.scalar
        def _(act):
            def gx_copy(j):
                act.wait_ge(gx_summed, j + 1)
                act.activation(gx_parts[:, 0, :, :].rearrange("f c v -> f (c v)"), gx_ps,
                               ACT.Copy).then_inc(gx_part0, 1)

            def g_copy(k, par):
                for v in range(2):
                    act.wait_ge(g_summed, 2 * k + v + 1)
                    act.activation(gh[:, par, v * HALF:(v + 1) * HALF], g_ps[:, v, :], ACT.Copy).then_inc(g_high, 1)

            def h1_relu(k, par):
                act.wait_ge(h1_summed, 2 * k + 1)
                act.activation(h1[:, par, 0:BLOCKS // 2, :].rearrange("v k c -> v (k c)"), h1_ps[:, 0, :],
                               ACT.Relu).then_inc(h1_ready[0], 1)

            def h2_relu(k, par):
                act.wait_ge(h2_summed, k + 1)
                act.wait_ge(h2_free, k + 1)
                act.activation(split(h2[:, par, :], 2), h2_ps, ACT.Relu, bias=c1[:, 0:1],
                               scale=bn_t[:, 1, C1:C1 + 1]).then_inc(h2_ready, 1)

            guesses = [0]

            def rsqrt_guess(t):
                guesses[0] += 1
                act.wait_ge(inverse_ready, guesses[0])
                act.activation(t, t, ACT.Sqrt).then_inc(guess_ready, 1)

            gx_copy(0)
            rsqrt_guess(bn_t[:, 0, :])
            act.wait_ge(gcn_rest_loaded, 16)
            act.activation(w1g_h[:], g("w1"), ACT.Copy).then_inc(w1g_high, 1)
            h1_relu(0, 0)
            g_copy(0, 0)
            h1_relu(1, 1)
            act.wait_ge(bn1_ready, 1)

            def tile(i, steps):
                at = i * STEPS
                for s in range(steps or STEPS):
                    if not steps or s + 2 < steps:
                        h1_relu(at + s + 2, s % 2)
                    if not steps or s + 1 < steps:
                        g_copy(at + s + 1, (s + 1) % 2)
                    h2_relu(at + s, s % 2)
                    if s == 0:
                        act.wait_ge(rows_stored, 16 * (i + 1))
                        gx_copy(i + 1)

            with act.Fori(0, LOOP) as i:
                tile(i, 0)
            tile(LOOP, REST)

            def half(d):
                return slice(HC * d, HC * (d + 1))

            def norm_scale(n, bank, d, scale, bias=None):
                act.wait_ge(norm_turned, 2 * n + d + 1)
                if bias is None:
                    act.activation(n_ch[:, half(d)], ps[:, bank, :], ACT.Copy, scale=scale).then_inc(norm_ch, 1)
                else:
                    act.activation(n_ch[:, half(d)], ps[:, bank, :], ACT.Identity, bias=bias,
                                   scale=scale).then_inc(norm_ch, 1)

            def row_guess(d):
                rsqrt_guess(row_t[:, 0, HT * d:HT * (d + 1)])

            def copy_xc(d):
                act.wait_ge(xz_summed, 2 * d + 1)
                act.activation(xc_pad[:, HT * d:HT * (d + 1), 2:T + 2],
                               ps[:, 4 + d, :].rearrange("p (q t) -> p q t", t=T), ACT.Copy).then_inc(xc_copied, 1)

            act.wait_ge(moe_loaded, 16)
            act.activation(w1_h[:], m("w1"), ACT.Copy).then_inc(wh_ready, 1)
            act.activation(w3_h[:], m("w3"), ACT.Copy).then_inc(wh_ready, 1)
            act.wait_ge(tail_loaded, 16)
            row_guess(0)
            row_guess(0)
            norm_scale(0, 2, 0, w("ln1_w"), w("ln1_b"))
            row_guess(1)
            act.wait_ge(pad_zero, 1)
            copy_xc(0)
            row_guess(1)
            norm_scale(0, 3, 1, w("ln1_w"), w("ln1_b"))
            copy_xc(1)
            for d in range(2):
                act.wait_ge(xz_summed, 2 * d + 2)
                act.activation(z_ch[:, half(d)], ps[:, 6 + d, :], ACT.Silu).then_inc(z_silu, 1)
            for d in range(2):
                act.wait_ge(conv_ready, d + 1)
                act.activation(xc_ch[:, half(d)], cv_ch[:, half(d)], ACT.Silu).then_inc(xc_silu, 1)
            for d in range(2):
                act.wait_ge(xc_turned, d + 1)
                act.activation(xc_tok[:, HP * d:HP * (d + 1), :].rearrange("p a b -> p (a b)"), ps[:, 2 + d, :],
                               ACT.Copy).then_inc(xc_tok_ready, 1)
            row_guess(0)
            norm_scale(1, 6, 0, w("ln2_w"), w("ln2_b"))
            row_guess(1)

            def gelus(d):
                for fb in range(FFB):
                    act.wait_ge(fc1_summed, FFB * d + fb + 1)
                    act.activation(ff[:, fb, half(d)], ps[:, 4 * (fb % 2) + d, :], ACT.Gelu,
                                   bias=w("fc1_b")[:, fb:fb + 1]).then_inc(gelu_ready, 1)

            gelus(0)
            norm_scale(1, 7, 1, w("ln2_w"), w("ln2_b"))
            gelus(1)
            for d in range(2):
                row_guess(d)
                row_guess(d)
                norm_scale(2, 6 + d, d, w("rms1_w"))
            act.wait_ge(vb_ones, 2)
            spread = vb.rearrange("p (n e v) -> p n e v", e=2, v=VW)
            for d in range(2):
                act.wait_ge(v_summed, d + 1)
                for a in range(2):
                    rows = slice(a * T, (a + 1) * T)
                    n = HP * 2 * 2 * NKV
                    act.activation(spread[rows, n * d:n * (d + 1), a, 0:HD],
                                   ps[rows, 2 + d, :].rearrange("p (n v) -> p n v", v=HD),
                                   ACT.Copy).then_inc(v_ready, 1)

            def key_blocks(n):
                act.wait_ge(kf_summed, n + 1)
                if n >= 2:
                    act.wait_ge(s_summed, GT * (n - 1))
                for h in range(NH):
                    a = act.activation(kb[:, n % 2, :, :, h, :].rearrange("p k q s -> p (k q) s"),
                                       split(ps[:, 7, :], 2 * GT), ACT.Copy, scale=w("head")[:, h:h + 1])
                a.then_inc(kb_ready, 1)

            def y_copy(d):
                act.wait_ge(y_turned, d + 1)
                act.activation(n_ch[:, half(d)], ps[:, 6, :], ACT.Copy).then_inc(y_ch, 1)

            key_blocks(0)
            for a in range(TILES + 1):
                if a == TURN_Y + 1:
                    y_copy(0)
                if a < TILES:
                    act.wait_ge(s_shifted, a + 1)
                    if a >= 2:
                        act.wait_ge(pt_turned, a - 1)
                    act.activation(pr[:, a % 2, :], sm[:, a % 2, :], ACT.Exp, scale=HD ** -0.5).then_inc(exp_ready, 1)
                if a >= 1:
                    act.wait_ge(pt_turned, a)
                    if a >= 3:
                        act.wait_ge(pv_summed, a - 2)
                    act.activation(pt[:, (a - 1) % 2, :], ps[:, 4 + (a - 1) % 2, 0:2 * P],
                                   ACT.Copy).then_inc(pt_ready, 1)
                if a % GT == 1 and a // GT + 1 < TILES // GT:
                    key_blocks(a // GT + 1)
            row_guess(0)
            y_copy(1)
            row_guess(1)
            for n in range(TILES // GT):
                act.wait_ge(f_turned, n + 1)
                act.activation(f_r[:, n * GT * P:(n + 1) * GT * P], ps[:, 2 + n, :], ACT.Copy,
                               scale=w("rms2_w")).then_inc(f_high, 1)
            act.wait_ge(lg_ready, 2)
            act.activation(ep[:], lg[:], ACT.Exp).then_inc(lexp_ready, 1)

            def silu(k, step):
                rows = block_of_hidden(step % NHB)[0]
                act.wait_ge(e1_summed, k + 1)
                if step >= 2:
                    act.wait_ge(hh_ready, k - 1)
                act.activation(act_h[0:rows, step % 2, :], ps[0:rows, step % 2, 0:CT], ACT.Silu).then_inc(silu_ready, 1)

            for k in range(LAG):
                silu(k, k)

            def two_chunks(i, last):
                for ahead in range(LAG, 2 * NHB + (0 if last else LAG)):
                    silu(i * 2 * NHB + ahead, ahead)

            with act.Fori(0, TILES // (2 * CHUNK) - 1) as i:
                two_chunks(i, False)
            two_chunks(TILES // (2 * CHUNK) - 1, True)

        @block.gpsimd
        def _(pool):
            pool.memset(gxr[0:32, :, :], 1.0).then_inc(ones_ready, 1)
            pool.memset(xc_pad[:, :, 0:2], 0.0).then_inc(pad_zero, 1)

            def tile(i, steps):
                for s in range(steps):
                    k = i * STEPS + s
                    pool.wait_ge(h2_ready, k + 1)
                    pool.wait_ge(h2w_free, k + 1)
                    pool.tensor_tensor(split(h2w[:, s % 2, :], SF), split(h2[:, s % 2, :], SF),
                                       mean_a[:].rearrange("p (a v) -> p a v", a=1).to_broadcast([P, SF, V]),
                                       ALU.mult).then_inc(h2_free, 1)

            pool.wait_ge(mean_ready, 1)
            pool.nop().then_inc(h2_free, 2)
            with pool.Fori(0, LOOP) as i:
                tile(i, STEPS)
            tile(LOOP, REST)

            spread = vb.rearrange("p (n e v) -> p n e v", e=2, v=VW)
            pool.wait_ge(h_summed, 2)
            pool.memset(vb, 0.0).then_inc(vb_zero, 1)
            pool.wait_ge(vb_zero, 1)
            for a in range(2):
                pool.memset(spread[a * T:(a + 1) * T, :, a, HD:VW], 1.0).then_inc(vb_ones, 1)
            pool.wait_ge(vb_ones, 2)

            for n, (hi, lo, name) in enumerate(((w1_h, w1_l, "w1"), (w3_h, w3_l, "w3"))):
                pool.wait_ge(wh_ready, n + 1)
                pool.tensor_tensor(lo[:], m(name), hi[:].bitcast(F32), ALU.subtract).then_inc(wl_ready, 1)

            for d in range(2):
                tiles = slice(HT * d, HT * (d + 1))
                pool.wait_ge(x4_ready, d + 1)
                pool.tensor_tensor(h_tok[:, tiles, :], x_new[:, tiles, :], h_new[:, tiles, :],
                                   ALU.add).then_inc(resid_ready, 1)

        @block.vector
        def _(dve):
            chain = [0]

            def link(ins):
                chain[0] += 1
                ins.then_inc(dve_chain, 1)
                dve.wait_ge(dve_chain, chain[0])

            def bcast(ap, n):
                return ap.rearrange("p (a o) -> p a o", o=1).to_broadcast([ap.shape[0], ap.shape[1], n])

            def gx_left_parts(j):
                dve.wait_ge(gx_part0, j + 1)
                part = [gx_parts[:, n, :, :].rearrange("f c v -> f (c v)") for n in range(3)]
                dve.tensor_tensor(gx_rest[:], gx_ps, part[0], ALU.subtract).then_inc(gx_left, 1)
                dve.wait_ge(gx_left, j + 1)
                dve.tensor_copy(part[1], gx_rest[:]).then_inc(gx_part1, 1)
                dve.wait_ge(gx_part1, j + 1)
                dve.tensor_tensor(part[2], gx_rest[:], part[1], ALU.subtract).then_inc(gx_part2, 1)

            dve.wait_ge(gcn_loaded, 16)
            bn0, bn1, bn2 = g("bn0", XR), g("bn1"), g("bn2")
            dve.tensor_scalar(bn_e[:, 0:C1], g("bn0")[:, C1:2 * C1], 1e-5, None, ALU.add)
            dve.tensor_scalar(bn_e[:, C1:C1 + 1], bn1[:, 1:2], 1e-5, None, ALU.add)
            link(dve.tensor_scalar(bn_e[:, C1 + 1:], bn2[:, C:2 * C], 1e-5, None, ALU.add))

            guesses = [0]

            def rsqrt(e, t, invert=True):
                guesses[0] += 1
                if invert:
                    dve.reciprocal(t[:, 0, :], e).then_inc(inverse_ready, 1)
                dve.wait_ge(guess_ready, guesses[0])
                link(dve.tensor_tensor(t[:, 1, :], t[:, 0, :], t[:, 0, :], ALU.mult))
                link(dve.scalar_tensor_tensor(out=t[:, 1, :], in0=t[:, 1, :], scalar=-0.5, in1=e,
                                              op0=ALU.mult, op1=ALU.mult))
                link(dve.scalar_tensor_tensor(out=t[:, 1, :], in0=t[:, 1, :], scalar=1.5, in1=t[:, 0, :],
                                              op0=ALU.add, op1=ALU.mult))

            dve.reciprocal(bn_t[:, 0, :], bn_e[:]).then_inc(inverse_ready, 1)
            gx_left_parts(0)
            rsqrt(bn_e[:], bn_t, False)
            s0, s1, s2 = bn_t[0:XR, 1, 0:C1], bn_t[:, 1, C1:C1 + 1], bn_t[:, 1, C1 + 1:]

            def bn_shift(s, c, bn, n):
                link(dve.tensor_tensor(s, s, bn[:, 0:n], ALU.mult))
                link(dve.tensor_tensor(c, bn[:, 2 * n:3 * n], bn[:, 3 * n:4 * n], ALU.subtract))
                link(dve.tensor_tensor(c, c, s, ALU.mult))
                return dve.tensor_tensor(c, c, bn[:, 4 * n:5 * n], ALU.add)

            link(bn_shift(s0, c0[:], bn0, C1))
            link(dve.tensor_tensor(w0s[:], g("w0", XR), s0, ALU.mult))
            link(dve.scalar_tensor_tensor(out=w0s[:], in0=c0[:], scalar=g("bias_row", XR), in1=w0s[:],
                                          op0=ALU.mult, op1=ALU.add))
            part = g("part", XR)
            left = w0s[:]
            for n in range(2):
                link(dve.tensor_copy(w0_p[:, n, :], left))
                link(dve.tensor_tensor(w0_t[:, n, :], left, w0_p[:, n, :], ALU.subtract))
                left = w0_t[:, n, :]
            link(dve.tensor_scalar(left, left, part[:, 2:3], None, ALU.mult))
            link(dve.scalar_tensor_tensor(out=left, in0=w0_p[:, 1, :], scalar=part[:, 1:2], in1=left,
                                          op0=ALU.mult, op1=ALU.add))
            dve.scalar_tensor_tensor(out=w0_b[:], in0=w0_p[:, 0, :], scalar=part[:, 0:1], in1=left,
                                     op0=ALU.mult, op1=ALU.add).then_inc(w0_ready, 1)
            bn_shift(s1, c1[:], bn1, 1).then_inc(bn1_ready, 1)
            link(bn_shift(s2, c2[:], bn2, C))
            dve.wait_ge(w1g_high, 1)
            dve.tensor_tensor(w1g_l[:], g("w1"), w1g_h[:].bitcast(F32), ALU.subtract).then_inc(w1g_low, 1)
            dve.wait_ge(mean_summed, 1)
            dve.tensor_copy(mean_a[:], ps[:, 0, 0:V]).then_inc(mean_ready, 1)
            dve.nop().then_inc(h2w_free, 2)

            def g_low_part(k, par):
                for v in range(2):
                    cols = slice(v * HALF, (v + 1) * HALF)
                    dve.wait_ge(g_high, 2 * k + v + 1)
                    dve.tensor_tensor(gl[:, par, cols], g_ps[:, v, :], gh[:, par, cols].bitcast(F32),
                                      ALU.subtract).then_inc(g_ready, 1)

            def h1_relu(k, par):
                dve.wait_ge(h1_summed, 2 * k + 2)
                dve.tensor_scalar(h1[:, par, BLOCKS // 2:, :].rearrange("v k c -> v (k c)"), h1_ps[:, 1, :],
                                  0.0, None, ALU.max).then_inc(h1_ready[1], 1)

            def vertex_sum(k, par, col):
                dve.wait_ge(h2_free, k + 3)
                dve.tensor_reduce(sums[:, col], split(h2w[:, par, :], SF), AX.X, ALU.add).then_inc(h2w_free, 1)

            for k in range(4):
                h1_relu(k, k % 2)
                if k:
                    g_low_part(k - 1, (k - 1) % 2)

            def tile(i, steps):
                at = i * STEPS
                for s in range(steps or STEPS):
                    if not steps or s + 4 < steps:
                        h1_relu(at + s + 4, s % 2)
                    col = bass.ds(i * GF + s * SF, SF) if not steps else slice(i * GF + s * SF, i * GF + (s + 1) * SF)
                    vertex_sum(at + s, s % 2, col)
                    if not steps or s + 3 < steps:
                        g_low_part(at + s + 3, (s + 3) % 2)
                    if s == 0:
                        gx_left_parts(i + 1)

            with dve.Fori(0, LOOP) as i:
                tile(i, 0)
            tile(LOOP, REST)

            def tiles(t, d):
                return t[:, HT * d:HT * (d + 1), :]

            def tile_cols(t, d):
                return tiles(t, d).rearrange("p j c -> p (j c)")

            def half(t, d):
                return t[:, HC * d:HC * (d + 1)]

            def row(ap):
                return ap.rearrange("p (a c) -> p a c", a=1).to_broadcast([P, HT, C])

            def mean_square(src, d, eps):
                rows = slice(HT * d, HT * (d + 1))
                link(dve.tensor_tensor(tiles(q_tok, d), src, src, ALU.mult))
                link(dve.tensor_reduce(row_v[:, rows], tiles(q_tok, d), AX.X, ALU.add))
                link(dve.tensor_scalar(row_v[:, rows], row_v[:, rows], 1.0 / C, eps, ALU.mult, ALU.add))

            def scale_rows(src, dst, d, twice=False):
                rows = slice(HT * d, HT * (d + 1))
                rsqrt(row_v[:, rows], row_t[:, :, rows])
                r = row_t[:, 1, rows]
                if twice:
                    return dve.tensor_tensor(dst, src.rearrange("p j (a c) -> p j a c", a=1)
                                             .to_broadcast([P, HT, 2, C]),
                                             r.rearrange("p (j a c) -> p j a c", a=1, c=1)
                                             .to_broadcast([P, HT, 2, C]), ALU.mult)
                return dve.tensor_tensor(dst, src, bcast(r, C), ALU.mult)

            def rms_norm(src, dst, d, eps=1e-6):
                mean_square(src, d, eps)
                return scale_rows(src, dst, d)

            def layer_norm(src, dst, d):
                mean = row_a[:, HT * d:HT * (d + 1)]
                link(dve.tensor_reduce(mean, src, AX.X, ALU.add))
                link(dve.tensor_scalar(mean, mean, -1.0 / C, None, ALU.mult))
                link(dve.tensor_tensor(tiles(d_tok, d), src, bcast(mean, C), ALU.add))
                return rms_norm(tiles(d_tok, d), dst, d, 1e-5)

            dve.wait_ge(tail_loaded, 16)
            for d in range(2):
                h = tiles(h_tok, d)
                dve.wait_ge(h_summed, d + 1)
                link(dve.tensor_tensor(h, ps[:, d, :].rearrange("p (j c) -> p j c", c=C), row(s2), ALU.mult))
                link(dve.tensor_tensor(h, h, row(c2[:]), ALU.add))
                link(layer_norm(h, tiles(x_tok, d), d))
                layer_norm(tiles(x_tok, d), tiles(n_tok, d), d).then_inc(norm_ready, 1)
            link(dve.tensor_tensor(bc[:], w("ssm_b"), w("ssm_c"), ALU.mult))
            link(dve.tensor_reduce(bcs[:], bc[:], AX.X, ALU.add))
            cw = w("conv_w")
            for d in range(2):
                pad = xc_pad[:, HT * d:HT * (d + 1), :]
                cv, c2nd = (half(t, d).rearrange("p (q t) -> p q t", t=T) for t in (cv_ch, cw_ch))
                dve.wait_ge(xc_copied, d + 1)
                link(dve.tensor_scalar(cv, pad[:, :, 2:T + 2], cw[:, 2:3], w("conv_b"), ALU.mult, ALU.add))
                link(dve.scalar_tensor_tensor(out=c2nd, in0=pad[:, :, 1:T + 1], scalar=cw[:, 1:2], in1=cv,
                                              op0=ALU.mult, op1=ALU.add))
                dve.scalar_tensor_tensor(out=cv, in0=pad[:, :, 0:T], scalar=cw[:, 0:1], in1=c2nd,
                                         op0=ALU.mult, op1=ALU.add).then_inc(conv_ready, 1)
            for d in range(2):
                link(dve.tensor_tensor(tiles(h_tok, d), tiles(h_tok, d), row(w("fc2_b")), ALU.add))
            for d in range(2):
                dve.wait_ge(xc_silu, d + 1)
                link(dve.tensor_scalar(half(cv_ch, d), half(xc_ch, d), w("ssm_d"), None, ALU.mult))
            for d in range(2):
                dve.wait_ge(cum_summed, d + 1)
                link(dve.scalar_tensor_tensor(out=half(cv_ch, d), in0=ps[:, 4 + d, :], scalar=bcs[:, 0:1],
                                              in1=half(cv_ch, d), op0=ALU.mult, op1=ALU.add))
                dve.wait_ge(z_silu, d + 1)
                dve.tensor_tensor(half(cw_ch, d), half(cv_ch, d), half(z_ch, d), ALU.mult).then_inc(yz_ready, 1)
            for d in range(2):
                dve.wait_ge(mix_summed, d + 1)
                link(dve.tensor_tensor(tile_cols(x_new, d), tile_cols(x_tok, d), ps[:, 2 + d, :], ALU.add))
                layer_norm(tiles(x_new, d), tiles(n_tok, d), d).then_inc(norm_ready, 1)
            for d in range(2):
                link(dve.tensor_tensor(tiles(h_tok, d), tiles(h_tok, d), tiles(x_new, d), ALU.add))
            for d in range(2):
                dve.wait_ge(fc2_summed, d + 1)
                dve.tensor_tensor(tile_cols(h_new, d), tile_cols(h_tok, d), ps[:, 2 + d, :],
                                  ALU.add).then_inc(h_new_ready, 1)
                dve.wait_ge(h_new_ready, d + 1)

                link(layer_norm(tiles(h_new, d), tiles(x_tok, d), d))
                rms_norm(tiles(x_tok, d), tiles(n_tok, d), d).then_inc(norm_ready, 1)
            rope = w("rope").rearrange("p (a t) -> p a t", a=1).to_broadcast([P, HP, P])
            for d in range(2):
                for par in range(2):
                    n = 2 * d + par + 1
                    for bank, o, summed, ready in ((par, qq, q_summed, q_ready), (4 + par, kk, k_summed, k_ready)):
                        dve.wait_ge(summed, n)
                        dve.tensor_tensor(split(o[:, par, HC * d:HC * (d + 1)], HP), split(ps[:, bank, :], HP), rope,
                                          ALU.mult).then_inc(ready, 1)

            def divide(n):
                d, par = divmod(n, 2)
                dve.wait_ge(pv_summed, GT * (n + 1))
                o = ps[:, n % 2, 0:GT * NH * VW].rearrange("p (k h v) -> p k h v", k=GT, h=NH)
                r = rden[:].rearrange("p (k h v) -> p k h v", k=GT, v=1)
                link(dve.reciprocal(r, o[:, :, :, HD:VW]))
                dve.tensor_tensor(y_tok[:, HT * d + par:HT * (d + 1):2, :].rearrange("p k (h v) -> p k h v", h=NH),
                                  o[:, :, :, 0:HD], r.to_broadcast([P, GT, NH, HD]), ALU.mult).then_inc(y_ready, 1)

            def add_attention(d):
                dve.wait_ge(wo_summed, d + 1)
                dve.tensor_tensor(tile_cols(x_new, d), tile_cols(x_tok, d), ps[:, 6, :], ALU.add).then_inc(x4_ready, 1)
                dve.wait_ge(x4_ready, d + 1)
                mean_square(tiles(x_new, d), d, 1e-6)

            causal = w("causal").rearrange("p (a s) -> p a s", a=1).to_broadcast([P, NH, T])
            for a in range(TILES):
                s = split(sm[:, a % 2, :], NH)
                dve.wait_ge(s_summed, a + 1)
                if a >= 2:
                    dve.wait_ge(exp_ready, a - 1)
                dve.tensor_tensor(s, split(ps[:, 2 + a % 2, 0:NH * T], NH), causal, ALU.add).then_inc(s_masked, 1)
                dve.wait_ge(s_masked, a + 1)
                link(dve.tensor_reduce(mx[:, a % 2, :], s, AX.X, ALU.max))
                dve.tensor_tensor(s, s, bcast(mx[:, a % 2, :], T), ALU.subtract).then_inc(s_shifted, 1)
                if a >= GT and a % GT == 2:
                    divide(a // GT - 1)
                if a == TURN_Y + 2:
                    add_attention(0)
            divide(TILES // GT - 1)
            scale_rows(tiles(x_new, 0), n_twice[:, 0:HT, :, :], 0, twice=True).then_inc(norm_ready, 1)
            add_attention(1)
            scale_rows(tiles(x_new, 1), n_twice[:, HT:, :, :], 1, twice=True).then_inc(norm_ready, 1)

            for n in range(TILES // GT):
                cols = slice(n * GT * P, (n + 1) * GT * P)
                dve.wait_ge(f_high, n + 1)
                dve.scalar_tensor_tensor(out=f_r[C:, cols], in0=ps[C:, 2 + n, :], scalar=w("rms2_w", C, P),
                                         in1=f_r[C:, cols].bitcast(F32), op0=ALU.mult,
                                         op1=ALU.subtract).then_inc(f_ready, 1)
            dve.nop().then_inc(eo_free, 4)

            def hidden(k, step):
                b = step % NHB
                rows = block_of_hidden(b)[0]
                dve.wait_ge(silu_ready, k + 1)
                dve.wait_ge(e3_summed, k + 1)
                dve.tensor_tensor(hh[0:rows, b, :], act_h[0:rows, step % 2, :], ps[0:rows, 2 + step % 2, 0:CT],
                                  ALU.mult).then_inc(hh_ready, 1)

            dve.wait_ge(lg_summed, 1)
            dve.tensor_copy(lg[:].rearrange("p j e -> p (j e)"), ps[:, 6, 0:TILES * NE]).then_inc(lg_ready, 1)
            dve.wait_ge(lg_ready, 1)
            link(dve.tensor_reduce(r_a[:], lg[:], AX.X, ALU.max))
            dve.tensor_tensor(lg[:], lg[:], bcast(r_a[:], NE), ALU.subtract).then_inc(lg_ready, 1)
            for k in range(LAG):
                hidden(k, k)
            dve.wait_ge(lexp_ready, 1)
            link(dve.tensor_reduce(r_a[:], ep[:], AX.X, ALU.add))
            link(dve.reciprocal(r_b[:], r_a[:]))
            link(dve.tensor_tensor(ep[:], ep[:], bcast(r_b[:], NE), ALU.mult))
            expert = w("expert").rearrange("p (j e) -> p j e", e=NE)

            def first_largest(one_hot, largest):
                link(dve.tensor_reduce(largest, ep[:], AX.X, ALU.max))
                link(dve.tensor_tensor(tmp8[:], ep[:], bcast(largest, NE), ALU.is_equal))
                link(dve.tensor_tensor(tmp8[:], tmp8[:], expert, ALU.mult))
                link(dve.tensor_reduce(r_c[:], tmp8[:], AX.X, ALU.min))
                link(dve.tensor_tensor(one_hot[:], expert, bcast(r_c[:], NE), ALU.is_equal))

            first_largest(oh1, r_a[:])
            link(dve.scalar_tensor_tensor(out=ep[:], in0=oh1[:], scalar=-2.0, in1=ep[:], op0=ALU.mult, op1=ALU.add))
            first_largest(oh2, r_b[:])
            link(dve.tensor_tensor(r_c[:], r_a[:], r_b[:], ALU.add))
            link(dve.tensor_scalar(r_c[:], r_c[:], 1e-9, None, ALU.add))
            link(dve.reciprocal(r_d[:], r_c[:]))
            link(dve.tensor_tensor(r_a[:], r_a[:], r_d[:], ALU.mult))
            link(dve.tensor_tensor(r_b[:], r_b[:], r_d[:], ALU.mult))
            link(dve.tensor_tensor(oh1[:], oh1[:], bcast(r_a[:], NE), ALU.mult))
            link(dve.tensor_tensor(oh2[:], oh2[:], bcast(r_b[:], NE), ALU.mult))
            link(dve.tensor_tensor(gate[:], oh1[:], oh2[:], ALU.add))
            dve.wait_ge(resid_ready, 2)

            def weigh(i, c, last):
                n = i * 2 + c
                at = n * CHUNK
                two = slice(at, at + CHUNK) if last else bass.ds(at, CHUNK)
                dve.wait_ge(eo_summed, n + 1)
                dve.tensor_tensor(eo[:].rearrange("p (t e c) -> p t e c", t=CHUNK, e=NE),
                                  ps[:, 4 + CHUNK * c:4 + CHUNK * (c + 1), :].rearrange("p t (e c) -> p t e c", e=NE),
                                  gate[:, two, :].rearrange("p t (e c) -> p t e c", c=1)
                                  .to_broadcast([P, CHUNK, NE, C]), ALU.mult).then_inc(eo_free, 2)
                dve.wait_ge(eo_free, 4 + 2 * (n + 1))
                dve.tensor_reduce(n_tok[:, CHUNK * c:CHUNK * (c + 1), :],
                                  eo[:].rearrange("p (t e c) -> p t c e", t=CHUNK, e=NE), AX.X,
                                  ALU.add).then_inc(chunk_summed, 1)
                dve.wait_ge(chunk_summed, n + 1)
                dve.tensor_tensor(y_tok[:, two, :], n_tok[:, CHUNK * c:CHUNK * (c + 1), :], h_tok[:, two, :],
                                  ALU.add).then_inc(out_ready, 1)

            def two_chunks(i, last):
                for step in range(2 * NHB):
                    ahead = step + LAG
                    if not (last and ahead >= 2 * NHB):
                        hidden(i * 2 * NHB + ahead, ahead)
                    if step % NHB == NHB - 1:
                        weigh(i, step // NHB, last)

            with dve.Fori(0, TILES // (2 * CHUNK) - 1) as i:
                two_chunks(i, False)
            two_chunks(TILES // (2 * CHUNK) - 1, True)


def layout(inputs):
    f = {k: np.asarray(v) for k, v in inputs.items()}
    tok = lambda n: f["L0_tok_" + n]
    at = lambda n: f["L0_attn_" + n]
    fn = lambda n: f["L0_ffn_" + n]
    bn = lambda i, rows: np.concatenate([np.broadcast_to(tok(f"{n}{i}"), (rows, tok(f"{n}{i}").shape[0]))
                                         for n in ("g", "v", "b", "m", "be")], axis=1)

    def pack(parts, where, width):
        out = np.zeros((P, width), np.float32)
        for name, a in parts.items():
            o, n = where[name]
            out[:a.shape[0], o:o + n] = a.reshape(a.shape[0], n)
        return out

    w0 = np.zeros((XR, C1), np.float32)
    w0[:XR - 3] = np.tile(tok("W0"), (len(PRODUCTS), 1))
    takes = np.concatenate([np.repeat([part for _, part in PRODUCTS], CIN), np.arange(3)])
    mix = np.zeros((BR, 2, 2 * V), np.float32)
    for b in range(2):
        for r in range(b, BR):
            frame, v = divmod(b * (BR - 1) + r, V)
            mix[r, b, (frame - b) * V:(frame - b + 1) * V] = tok("A")[:, v]
    gcn = pack({
        "at": tok("A").T, "a": tok("A"), "w1": tok("W1"), "w2": tok("W2"), "w0": w0,
        "bn0": bn(0, P), "bn2": bn(2, P),
        "bn1": np.stack([tok(f"{n}1") for n in ("g", "v", "b", "m", "be")], axis=1),
        "bias_row": (np.arange(XR) >= XR - 3).astype(np.float32)[:, None],
        "part": (takes[:, None] == np.arange(3)[None, :]).astype(np.float32),
        "mix": mix, "ident": np.eye(P, dtype=np.float32), "mean_v": np.full((V, P), 1.0 / V, np.float32),
    }, GCN_AT, GCN_N)
    x = np.zeros((GTILES * GF, V, CIN), np.float32)
    x[:FRAMES] = f["x"].reshape(FRAMES, V, CIN)
    x = x.reshape(GTILES, GF, V, CIN).transpose(0, 2, 3, 1).reshape(GTILES * V, CIN * GF)

    def diag2(a):
        out = np.zeros((2 * a.shape[0], 2 * a.shape[1]), np.float32)
        out[:a.shape[0], :a.shape[1]] = a
        out[a.shape[0]:, a.shape[1]:] = a
        return out

    def twice(a):
        a = a.reshape(C, -1)
        return np.concatenate([a, a])

    swap = np.concatenate([np.arange(HD // 2, HD), np.arange(HD // 2)])
    wq = fn("wq").reshape(NH, HD, C)
    wk = np.repeat(fn("wk").reshape(NKV, HD, C), NH // NKV, axis=0)
    turned = lambda a: np.concatenate([a.reshape(NH * HD, C), a[:, swap].reshape(NH * HD, C)]).T
    inv_freq = 1.0 / 10000.0 ** (np.arange(0, HD, 2, dtype=np.float32) / HD)
    freqs = np.outer(np.arange(T, dtype=np.float32), inv_freq)
    emb = np.concatenate([freqs, freqs], axis=-1)
    sign = np.where(np.arange(HD) < HD // 2, -1.0, 1.0).astype(np.float32)
    cos, sin = np.cos(emb).T, np.sin(emb).T * sign[:, None]
    rope = np.concatenate([np.tile(cos, (NH, 2)), np.tile(sin, (NH, 2))]).astype(np.float32)
    s, t = np.arange(P)[:, None], np.arange(P)[None, :]
    same = s // T == t // T
    eye = np.eye(C, dtype=np.float32)
    tail = pack({
        "bd_xc": diag2(at("in_proj_w")[:C].T), "bd_z": diag2(at("in_proj_w")[C:].T),
        "bd_out": diag2(at("out_proj_w").T),
        "bd_fc1": np.concatenate([diag2(at("fc1_w")[b * C:(b + 1) * C].T) for b in range(FFB)], axis=1),
        "bd_fc2": np.concatenate([diag2(at("fc2_w")[:, b * C:(b + 1) * C].T) for b in range(FFB)], axis=1),
        "bd_wo": diag2(fn("wo").T),
        "wq": twice(turned(wq)), "wk": twice(turned(wk)), "wv": diag2(fn("wv").T),
        "router": twice(fn("router_w").T),
        "fc2_b": np.broadcast_to(at("fc2_b"), (P, C)),
        "ln1_w": twice(at("ln1_w")), "ln1_b": twice(at("ln1_b")), "conv_w": twice(at("conv_w")),
        "conv_b": twice(at("conv_b")), "ssm_b": twice(at("ssm_B")), "ssm_c": twice(at("ssm_C")),
        "ssm_d": twice(at("ssm_D")), "ln2_w": twice(at("ln2_w")), "ln2_b": twice(at("ln2_b")),
        "fc1_b": np.concatenate([at("fc1_b").reshape(FFB, C).T] * 2),
        "rms1_w": twice(fn("ln1_w")), "rms2_w": twice(fn("ln2_w")),
        "tri": (same & (s <= t)).astype(np.float32),
        "causal": np.where(np.arange(T)[None, :] <= s % T, 0.0, MASKED).astype(np.float32),
        "rope": rope, "fold": np.block([[eye, eye], [eye, eye]]).astype(np.float32),
        "head": (np.arange(P)[:, None] % (NH * HD) // HD == np.arange(NH)[None, :]).astype(np.float32),
        "expert": np.broadcast_to(np.tile(np.arange(NE) - NE, TILES), (P, TILES * NE)).astype(np.float32),
    }, TAIL_AT, TAIL_N)
    up = lambda a: twice(a.reshape(NHID, C).T)
    w2 = np.zeros((P, NHB, 2, C), np.float32)
    for b in range(NHB):
        rows, e, _ = block_of_hidden(b)
        for r in range(rows):
            expert, k = divmod(b * P + r, HID)
            w2[r, b, expert - e] = fn("w2")[expert, :, k]
    moe = pack({
        "w1": up(fn("w1")), "w3": up(fn("w3")),
        "w2": w2,
    }, MOE_AT, MOE_N)
    return {"x": x, "gcn": gcn, "tail": tail, "moe": moe}


def kernel(**inputs):
    import concourse.bacc as bacc
    from concourse.bass_utils import run_bass_kernel_spmd

    nc = bacc.Bacc("TRN2", target_bir_lowering=False, num_devices=1)
    arrays = layout(inputs)
    args = [nc.dram_tensor(k, a.shape, F32, kind="ExternalInput").ap() for k, a in arrays.items()]
    out = nc.dram_tensor("out", (FRAMES, C), F32, kind="ExternalOutput").ap()
    program(nc, *args, out)
    r = run_bass_kernel_spmd(nc, [arrays], core_ids=[0])
    return r.results[0]["out"].reshape(SEQS, T, C)
```

```python
from contextlib import ExitStack

import numpy as np

import concourse.bass as bass
from concourse import mybir

F32 = mybir.dt.float32
F32R = mybir.dt.float32r
BF16 = mybir.dt.bfloat16
ALU = mybir.AluOpType
ACT = mybir.ActivationFunctionType
AX = mybir.AxisListType

P = 128
SEQS, T, V, CIN, C1, C = 32, 64, 75, 3, 128, 64
FRAMES = SEQS * T
TILES = FRAMES // P
PAIRS = TILES // 2
SF = 12
NSTEP = -(-FRAMES // SF)
SUMS = NSTEP * SF
STEPS = 8
GF = STEPS * SF
GTILES = -(-NSTEP // STEPS)
LOOP = NSTEP // STEPS - 4
REST = NSTEP - LOOP * STEPS
HALF = SF // 2 * V
TRIO = 3 * V
BR = TRIO // 2 + 1
BLOCKS = 2 * SF // 3
PRODUCTS = [(0, 0), (0, 1), (0, 2), (1, 0), (1, 1), (2, 0)]
XR = len(PRODUCTS) * CIN + 3
GROUP = 32
LOADS = 16 * 3
FFB = 4
NH, HD, NKV, NE = 4, 16, 2, 8
HID = int(8 / 3 * C)
NHID = NE * HID
NHB = -(-NHID // P)
MASKED = -1e30
HT, HP, HC = TILES // 2, PAIRS // 2, PAIRS // 2 * P
GT = 4
VW = HD + 1
CHUNK = 2
CT = CHUNK * P
WARM_START = 4
WARM = (16, 16, 20)
LAG = 3
WEIGH_LAG = LAG + 4


def offsets(parts):
    at, out = 0, {}
    for name, n in parts:
        out[name] = (at, n)
        at += n
    return out, at


GCN_PARTS = [("at", V), ("w0", C1), ("bn0", 5 * C1), ("bn1", 5), ("bn2", 5 * C), ("bias_row", 1), ("part", 3),
             ("a", V), ("mean_v", P), ("mix", 2 * 2 * V), ("w1", C1), ("w2", C), ("ident", P)]
FIRST = "a"
TAIL_PARTS = [("bd_xc", P), ("bd_z", P), ("bd_out", P), ("bd_fc1", FFB * P), ("bd_fc2", FFB * P),
              ("bd_wo", P), ("wq", P), ("wk", P), ("wv", 2 * NKV * HD), ("router", NE),
              ("fc2_b", C), ("ln1_w", 1), ("ln1_b", 1), ("conv_w", 3), ("conv_b", 1), ("ssm_b", 8),
              ("ssm_c", 8), ("ssm_d", 1), ("ln2_w", 1), ("ln2_b", 1), ("fc1_b", FFB), ("rms1_w", 1),
              ("rms2_w", 1), ("tri", P), ("causal", T), ("rope", P), ("fold", P),
              ("head", NH), ("expert", TILES * NE)]
MOE_PARTS = [("w1", NHID), ("w3", NHID), ("w2", NHB * 2 * C)]


def block_of_hidden(b):
    first, last = b * P, min((b + 1) * P, NHID) - 1
    return last - first + 1, first // HID, last // HID - first // HID + 1


GCN_AT, GCN_N = offsets(GCN_PARTS)
TAIL_AT, TAIL_N = offsets(TAIL_PARTS)
MOE_AT, MOE_N = offsets(MOE_PARTS)


def program(nc, x, gcn, tail, moe, out):
    ctx = ExitStack()
    with ctx:
        def sb(name, shape, dt=F32):
            return ctx.enter_context(nc.sbuf_tensor(name, shape, dt))

        def sem(name):
            return ctx.enter_context(nc.semaphore(name))

        gcn_sb = sb("gcn_sb", [P, GCN_N])
        tail_sb = sb("tail_sb", [P, TAIL_N])
        moe_sb = sb("moe_sb", [P, MOE_N])

        def g(name, rows=P):
            at, n = GCN_AT[name]
            return gcn_sb[0:rows, at:at + n]

        def w(name, r0=0, r1=P):
            at, n = TAIL_AT[name]
            return tail_sb[r0:r1, at:at + n]

        def m(name, rows=P):
            at, n = MOE_AT[name]
            return moe_sb[0:rows, at:at + n]

        x_tile = sb("x_tile", [V, CIN * GF])
        gx_parts = sb("gx_parts", [GF, 3, CIN, V], BF16)
        gx_rest = sb("gx_rest", [GF, CIN * V])
        gx_rows = nc.dram_tensor("gx_rows", (3, CIN, GF, V), BF16).ap()
        buf_s = sb("buf_s", [P, 2, NH * T])
        buf_p = sb("buf_p", [P, 2, NH * T])
        buf_t = sb("buf_t", [P, CHUNK * NE * C])
        buf_ch = sb("buf_ch", [P, 4, PAIRS * P])
        buf_ff = sb("buf_ff", [P, FFB, PAIRS * P])
        buf_g = sb("buf_g", [P, GF * V // 2])
        gxr = buf_g[0:GROUP, :].bitcast(BF16).rearrange("p (b n) -> p b n", b=2)
        buf_r = sb("buf_r", [P, 8 * HALF], F32R)
        buf_1 = sb("buf_1", [P, 2 * BLOCKS * C1 + 8 * HALF + SUMS])
        w0_b = sb("w0_b", [XR, C1], BF16)
        w0_p = sb("w0_p", [XR, 2, C1], BF16)
        w0_t = sb("w0_t", [XR, 2, C1])
        at = 2 * BLOCKS * C1
        h1 = buf_1[0:BR, 0:at].rearrange("v (b k c) -> v b k c", b=2, c=C1)
        h2, h2w = (buf_1[:, at + n * 4 * HALF:at + (n + 1) * 4 * HALF].rearrange("p (b n) -> p b n", b=2)
                   for n in range(2))
        sums = buf_1[:, at + 8 * HALF:at + 8 * HALF + SUMS]
        gh, gl = (buf_r[:, n * 4 * HALF:(n + 1) * 4 * HALF].rearrange("p (b n) -> p b n", b=2) for n in range(2))
        w1g_h = sb("w1g_h", [P, C1], F32R)
        w1g_l = sb("w1g_l", [P, C1], F32R)
        mean_a = sb("mean_a", [P, V])
        c0 = sb("c0", [XR, C1])
        w0s = sb("w0s", [XR, C1])
        c1 = sb("c1", [P, 1])
        c2 = sb("c2", [P, 2, C])
        c2_b = sb("c2_b", [P, C])
        w2s = sb("w2s", [P, 2, C])
        w2m = sb("w2m", [P, 2])
        bn_e = sb("bn_e", [P, C1 + 1 + C])
        bn_t = sb("bn_t", [P, 2, C1 + 1 + C])

        h_tok = sb("h_tok", [P, TILES, C])
        h_new = sb("h_new", [P, TILES, C])
        x_tok = sb("x_tok", [P, TILES, C])
        x_new = sb("x_new", [P, TILES, C])
        n_tok = sb("n_tok", [P, TILES, C])
        d_tok = sb("d_tok", [P, TILES, C])
        y_tok = sb("y_tok", [P, TILES, C])
        q_tok = y_tok
        row_a = sb("row_a", [P, TILES])
        row_s = sb("row_s", [P, TILES])
        row_v = sb("row_v", [P, 2, TILES])
        row_t = sb("row_t", [P, 2, 2, TILES])
        n_ch = sb("n_ch", [P, PAIRS * P])
        xc_pad = sb("xc_pad", [P, SEQS // 2, T + 2])
        xc_ch, cv_ch, cw_ch, z_ch = (buf_ch[:, n, :] for n in range(4))
        xc_tok = sb("xc_tok", [P, PAIRS, P])
        bc = sb("bc", [P, 8])
        bcs = sb("bcs", [P, 1])
        ff = buf_ff
        qq, kk = buf_ff[:, 0:2, :], buf_ff[:, 2:4, :]
        n_kb = GT * 2 * NH * T
        at = NHB * CT + TILES * 2 * C
        kb = [t.rearrange("p (k q h s) -> p k q h s", k=GT, q=2, h=NH)
              for t in (buf_g[:, 0:n_kb], buf_1[:, at:at + n_kb])]
        vb = buf_1[:, 0:TILES * 4 * 2 * VW]
        n_twice = buf_1[:, NHB * CT:NHB * CT + TILES * 2 * C].rearrange("p (j a c) -> p j a c", j=TILES, a=2)
        sm = buf_s
        pr = buf_p
        pt = buf_t[:, 0:4 * P].rearrange("p (b n) -> p b n", b=2)
        mx = sb("mx", [P, 2, NH])
        rden = sb("rden", [P, GT * NH])
        f_r = buf_r[:, 0:TILES * P]
        w1_h = sb("w1_h", [P, NHID], F32R)
        w3_h = sb("w3_h", [P, NHID], F32R)
        w1_l = sb("w1_l", [P, NHID], F32R)
        w3_l = sb("w3_l", [P, NHID], F32R)
        lg, ep, oh1, oh2, tmp8, gate = (
            d_tok[:].rearrange("p j c -> p (j c)")[:, n * TILES * NE:(n + 1) * TILES * NE]
            .rearrange("p (j e) -> p j e", e=NE) for n in range(6))
        r_a = sb("r_a", [P, TILES])
        r_b = sb("r_b", [P, TILES])
        r_c = sb("r_c", [P, TILES])
        r_d = sb("r_d", [P, TILES])
        act_h = buf_p
        hh = buf_1[:, 0:NHB * CT].rearrange("p (b n) -> p b n", b=NHB)
        eo = buf_t
        ps = ctx.enter_context(nc.psum_tensor("ps", [P, 8, 512], F32))

        gcn_loaded, tail_loaded, moe_loaded = sem("gcn_loaded"), sem("tail_loaded"), sem("moe_loaded")
        gcn_rest_loaded, x_loaded = sem("gcn_rest_loaded"), sem("x_loaded")
        gx_summed, gx_part0, gx_left, gx_part1, gx_part2 = (
            sem("gx_summed"), sem("gx_part0"), sem("gx_left"), sem("gx_part1"), sem("gx_part2"))
        ones_ready, rows_stored = sem("ones_ready"), sem("rows_stored")
        rows_loaded = [sem("rows_loaded_a"), sem("rows_loaded_b")]
        mean_summed, mean_ready = sem("mean_summed"), sem("mean_ready")
        inverse_ready, guess_ready = sem("inverse_ready"), sem("guess_ready")
        w0_ready, w1g_high, w1g_low, bn1_ready, w2_ready = (
            sem("w0_ready"), sem("w1g_high"), sem("w1g_low"), sem("bn1_ready"), sem("w2_ready"))
        g_high = sem("g_high")
        h1_summed = sem("h1_summed")
        h1_ready = [sem("h1_ready_a"), sem("h1_ready_b")]
        g_summed, g_ready = sem("g_summed"), sem("g_ready")
        h2_summed, h2_ready = sem("h2_summed"), sem("h2_ready")
        h2_free, h2w_free = sem("h2_free"), sem("h2w_free")
        h_summed = sem("h_summed")
        norm_ready, norm_turned, norm_ch = sem("norm_ready"), sem("norm_turned"), sem("norm_ch")
        pad_zero, xz_summed, xc_copied, conv_ready, xc_silu, z_silu = (
            sem("pad_zero"), sem("xz_summed"), sem("xc_copied"), sem("conv_ready"), sem("xc_silu"),
            sem("z_silu"))
        xc_turned, xc_tok_ready, cum_summed, yz_ready, mix_summed, h_new_ready = (
            sem("xc_turned"), sem("xc_tok_ready"), sem("cum_summed"), sem("yz_ready"),
            sem("mix_summed"), sem("h_new_ready"))
        fc1_summed, gelu_ready, fc2_summed = sem("fc1_summed"), sem("gelu_ready"), sem("fc2_summed")
        q_summed, q_ready, k_summed, k_ready, v_summed, v_ready = (
            sem("q_summed"), sem("q_ready"), sem("k_summed"), sem("k_ready"), sem("v_summed"),
            sem("v_ready"))
        vb_zero, vb_ones = sem("vb_zero"), sem("vb_ones")
        kf_summed, kb_ready, s_summed, s_masked, s_shifted, exp_ready, pt_turned, pt_ready = (
            sem("kf_summed"), sem("kb_ready"), sem("s_summed"), sem("s_masked"), sem("s_shifted"),
            sem("exp_ready"), sem("pt_turned"), sem("pt_ready"))
        pv_summed, y_ready, y_turned, y_ch, wo_summed, x4_ready, resid_ready = (
            sem("pv_summed"), sem("y_ready"), sem("y_turned"), sem("y_ch"), sem("wo_summed"),
            sem("x4_ready"), sem("resid_ready"))
        f_turned, f_high, f_ready, wh_ready, wl_ready = (
            sem("f_turned"), sem("f_high"), sem("f_ready"), sem("wh_ready"), sem("wl_ready"))
        lg_summed, lg_ready, lexp_ready = sem("lg_summed"), sem("lg_ready"), sem("lexp_ready")
        e1_summed, e3_summed, silu_ready, hh_ready, eo_summed, eo_free, out_ready, stored = (
            sem("e1_summed"), sem("e3_summed"), sem("silu_ready"), sem("hh_ready"),
            sem("eo_summed"), sem("eo_free"), sem("out_ready"), sem("stored"))
        chunk_summed = sem("chunk_summed")
        dve_chain = sem("dve_chain")

        h1_ps = ps[0:BR, 0:2, :]
        g_ps = ps[:, 2:4, 0:HALF]
        h2_ps = ps[:, 4:6, 0:HALF]
        gx_ps = ps[0:GF, 7, 0:CIN * V]

        def split(ap, a):
            return ap.rearrange("p (a b) -> p a b", a=a)

        ident = g("ident")

        block = ctx.enter_context(nc.Block())

        @block.sync
        def _(sp):
            first = GCN_AT[FIRST][0]
            sp.dma_start(gcn_sb[:, 0:first], gcn[:, 0:first]).then_inc(gcn_loaded, 16)
            sp.dma_start(x_tile[:], x[0:V, :]).then_inc(x_loaded, 16)
            sp.dma_start(gcn_sb[:, first:], gcn[:, first:]).then_inc(gcn_rest_loaded, 16)
            for j in range(GTILES):
                sp.wait_ge(gx_part2, j + 1)
                if j:
                    for half in range(2):
                        sp.wait_ge(rows_loaded[half], LOADS * j)
                sp.dma_start(gx_rows.rearrange("p c f v -> f (p c) v"),
                             gx_parts[:].rearrange("f p c v -> f (p c) v")).then_inc(rows_stored, 16)
                if j == 0:
                    sp.wait_ge(ones_ready, 1)
                if j + 1 < GTILES:
                    sp.wait_ge(gx_summed, j + 1)
                    sp.dma_start(x_tile[:], x[(j + 1) * V:(j + 2) * V, :]).then_inc(x_loaded, 16)
                sp.wait_ge(rows_stored, 16 * (j + 1))
                for half in range(2):
                    if (2 * j + half) * STEPS // 2 >= NSTEP:
                        continue
                    if j:
                        sp.wait_ge(h1_summed, 2 * (STEPS * (j - 1) + STEPS // 2 * (half + 1)))
                    row = 0
                    for part in range(3):
                        n = 3 - part
                        sp.dma_start(gxr[row:row + n * CIN, half, :],
                                     gx_rows[part:part + 1, :, half * GF // 2:(half + 1) * GF // 2, :]
                                     .rearrange("p c f v -> p c (f v)").to_broadcast([n, CIN, GF // 2 * V])
                                     ).then_inc(rows_loaded[half], 16)
                        row += n * CIN
                if j == 0:
                    sp.dma_start(tail_sb[:], tail).then_inc(tail_loaded, 16)
                    sp.dma_start(moe_sb[:], moe).then_inc(moe_loaded, 16)
            for n in range(TILES // (2 * CHUNK)):
                tiles = slice(2 * CHUNK * n, 2 * CHUNK * (n + 1))
                sp.wait_ge(out_ready, 2 * (n + 1))
                sp.dma_start(out.rearrange("(j p) c -> p j c", p=P)[:, tiles, :],
                             y_tok[:, tiles, :]).then_inc(stored, 16)
            sp.wait_ge(stored, 16 * (TILES // (2 * CHUNK)))

        @block.tensor
        def _(pe):
            def gx_sums(j):
                pe.wait_ge(x_loaded, 16 * (j + 1))
                for c in range(CIN):
                    mm = pe.matmul(gx_ps[:, c * V:(c + 1) * V], x_tile[:, c * GF:(c + 1) * GF], g("at", V),
                                   start=True, stop=True)
                mm.then_inc(gx_summed, 1)

            def layer0(s):
                half, k = divmod(s % STEPS, STEPS // 2)
                for b in range(BLOCKS):
                    at = (k * SF + b // 2 * 3) * V + b % 2 * (BR - 1)
                    mm = pe.matmul(ps[0:BR, 2 * b // BLOCKS, b % (BLOCKS // 2) * C1:(b % (BLOCKS // 2) + 1) * C1],
                                   gxr[0:XR, half, at:at + BR], w0_b[:], start=True, stop=True)
                    if b % (BLOCKS // 2) == BLOCKS // 2 - 1:
                        mm.then_inc(h1_summed, 1)

            def mix(par):
                for b in range(BLOCKS):
                    v, k = divmod(b, BLOCKS // 2)
                    at = k // 2 * TRIO + k % 2 * V
                    mm = pe.matmul(g_ps[:, v, at:at + 2 * V], h1[:, par, b, :],
                                   g("mix", BR)[:, b % 2 * 2 * V:(b % 2 + 1) * 2 * V],
                                   start=(k == 0), stop=(k == BLOCKS // 2 - 1), skip_group_check=True)
                    if k == BLOCKS // 2 - 1:
                        mm.then_inc(g_summed, 1)

            def layer1(par):
                for v in range(2):
                    cols = slice(v * HALF, (v + 1) * HALF)
                    pe.matmul(h2_ps[:, v, :], w1g_h[:], gh[:, par, cols], start=True, stop=False)
                    pe.matmul(h2_ps[:, v, :], w1g_h[:], gl[:, par, cols], start=False, stop=False)
                    mm = pe.matmul(h2_ps[:, v, :], w1g_l[:], gh[:, par, cols], start=False, stop=True)
                mm.then_inc(h2_summed, 1)

            pe.wait_ge(gcn_loaded, 16)
            gx_sums(0)
            pe.wait_ge(gcn_rest_loaded, 16)
            pe.matmul(ps[:, 0, 0:V], g("mean_v", V), g("a", V), start=True, stop=True).then_inc(mean_summed, 1)
            for _ in range(WARM_START):
                pe.matmul(ps[:, 6, :], g("w0"), g("bn0")[:, 0:512], start=True, stop=True)
            pe.wait_ge(w0_ready, 1)
            pe.wait_ge(mean_ready, 1)
            pe.wait_ge(rows_loaded[0], LOADS)
            layer0(0)
            pe.wait_ge(h1_ready[0], 1)
            pe.wait_ge(h1_ready[1], 1)
            mix(0)
            layer0(1)
            pe.wait_ge(w1g_low, 1)

            def tile(i, steps):
                at = i * STEPS
                for s in range(steps or STEPS):
                    if not steps or s + 1 < steps:
                        pe.wait_ge(h1_ready[0], at + s + 2)
                        pe.wait_ge(h1_ready[1], at + s + 2)
                    if not steps or s + 2 < steps:
                        if (s + 2) % (STEPS // 2) == 0:
                            j, half = divmod((s + 2) // (STEPS // 2), 2)
                            pe.wait_ge(rows_loaded[half], LOADS * (i + j + 1))
                        layer0(s + 2)
                    pe.wait_ge(g_ready, 2 * (at + s + 1))
                    if not steps or s + 1 < steps:
                        mix((s + 1) % 2)
                    pe.wait_ge(h2_ready, at + s + 1)
                    layer1(s % 2)
                    if s % STEPS == 0 and not (steps and s + STEPS > steps):
                        pe.wait_ge(gx_part2, i + s // STEPS + 1)
                        if s == 3 * STEPS:
                            pe.wait_ge(h_new_ready, 1)
                        gx_sums(i + s // STEPS + 1)
                    if steps:
                        beside(s)

            def half(d):
                return slice(HC * d, HC * (d + 1))

            def column(d, p):
                return slice(HC * d + p * P, HC * d + (p + 1) * P)

            def turn_pairs(src, bank, d, done):
                for p in range(HP):
                    j = 2 * (HP * d + p)
                    mm = pe.transpose(ps[:, bank, p * P:(p + 1) * P], src[:, j:j + 2, :], ident)
                mm.then_inc(done, 1)

            def last_layer(d, first, tiles):
                for k in tiles:
                    j = HT * d + k
                    bank, at = divmod(k, HT // 2)
                    mm = pe.matmul(ps[:, first + bank, at * 2 * C:(at + 1) * 2 * C], sums[:, j * P:(j + 1) * P],
                                   w2s[:].rearrange("p a c -> p (a c)"), start=True, stop=True)
                if tiles[-1] == HT - 1:
                    mm.then_inc(h_summed, 1)

            def turn_norm(n, d):
                pe.wait_ge(norm_ready, n + 3 * d + 1)
                turn_pairs(n_tok, 6, d, norm_turned)

            def mixer_xc(d):
                pe.wait_ge(norm_ch, 3 * d + 1)
                pe.matmul(ps[:, 6, :], w("bd_xc"), n_ch[:, half(d)], start=True, stop=True).then_inc(xz_summed, 1)

            def mixer_z(d):
                pe.wait_ge(xc_copied, d + 1)
                pe.matmul(ps[:, 6, :], w("bd_z"), n_ch[:, half(d)], start=True, stop=True).then_inc(xz_summed, 1)

            def turn_xc(d):
                pe.wait_ge(xc_silu, d + 1)
                for p in range(HP):
                    mm = pe.transpose(ps[:, 6, p * P:(p + 1) * P], xc_ch[:, column(d, p)], ident)
                mm.then_inc(xc_turned, 1)

            def running_sums(d):
                pe.wait_ge(xc_tok_ready, d + 1)
                for p in range(HP):
                    mm = pe.matmul(ps[:, 7, p * P:(p + 1) * P], xc_tok[:, HP * d + p, :], w("tri"),
                                   start=True, stop=True)
                mm.then_inc(cum_summed, 1)

            def mixer_out(d):
                pe.wait_ge(yz_ready, d + 1)
                for p in range(HP):
                    mm = pe.matmul(ps[:, 6, p * P:(p + 1) * P], cw_ch[:, column(d, p)], w("bd_out"),
                                   start=True, stop=True)
                mm.then_inc(mix_summed, 1)

            def fc1(d, fb):
                if fb == 0:
                    pe.wait_ge(norm_ch, 3 * d + 2)
                if fb >= 2:
                    pe.wait_ge(gelu_ready, FFB * d + fb - 1)
                pe.matmul(ps[:, 7 - fb % 2, :], w("bd_fc1")[:, fb * P:(fb + 1) * P], n_ch[:, half(d)],
                          start=True, stop=True).then_inc(fc1_summed, 1)

            def fc2(d):
                pe.wait_ge(gelu_ready, FFB * (d + 1))
                for p in range(HP):
                    for fb in range(FFB):
                        mm = pe.matmul(ps[:, 7, p * P:(p + 1) * P], ff[:, fb, column(d, p)],
                                       w("bd_fc2")[:, fb * P:(fb + 1) * P],
                                       start=(fb == 0), stop=(fb == FFB - 1))
                mm.then_inc(fc2_summed, 1)

            def queries(d, par, bank):
                if par == 0:
                    pe.wait_ge(norm_ch, 3 * (d + 1))
                rows = slice(par * C, (par + 1) * C)
                pe.matmul(ps[:, bank, :], w("wq", par * C, par * C + C), n_ch[rows, half(d)],
                          start=True, stop=True).then_inc(q_summed, 1)

            def keys(d, par, bank):
                rows = slice(par * C, (par + 1) * C)
                pe.matmul(ps[:, bank, :], w("wk", par * C, par * C + C), n_ch[rows, half(d)],
                          start=True, stop=True).then_inc(k_summed, 1)

            def fold_keys(n, bank):
                d, par = divmod(n, 2)
                pe.wait_ge(k_ready, n + 1)
                pe.matmul(ps[:, bank, :], w("fold"), kk[:, par, half(d)], start=True, stop=True).then_inc(kf_summed, 1)

            def make_values(d):
                if d:
                    pe.wait_ge(s_masked, HT)
                for p in range(HP):
                    for q in range(2):
                        at = HC * d + p * P + q * T
                        for a in range(2):
                            mm = pe.matmul(ps[a * T:(a + 1) * T, 2, (2 * p + q) * C:(2 * p + q + 1) * C],
                                           n_ch[:, at:at + T], w("wv"), start=True, stop=True)
                mm.then_inc(v_summed, 1)

            def beside(s):
                if s == 3:
                    pe.wait_ge(tail_loaded, 16)
                    pe.wait_ge(w2_ready, 1)
                    pe.wait_ge(gx_part2, LOOP + 2)
                    last_layer(0, 6, range(HT))
                if s == 7:
                    turn_norm(0, 0)
                if s == 8:
                    mixer_xc(0)
                if s == 9:
                    mixer_z(0)
                if s == 11:
                    turn_xc(0)
                if s == 12:
                    pe.wait_ge(gx_part2, LOOP + 3)
                    running_sums(0)
                if s == 14:
                    mixer_out(0)
                if s == 18:
                    turn_norm(1, 0)
                if s == 19:
                    pe.wait_ge(gx_part2, LOOP + 4)
                    fc1(0, 0)
                if s == 20:
                    fc1(0, 1)
                    fc1(0, 2)
                if s == 21:
                    fc1(0, 3)
                if s == 22:
                    fc2(0)
                if s == 26:
                    turn_norm(2, 0)
                if s == 27:
                    queries(0, 0, 6)
                if s == 28:
                    pe.wait_ge(gx_part2, GTILES)
                    keys(0, 0, 7)
                if s == 29:
                    pe.wait_ge(q_ready, 1)
                    queries(0, 1, 6)
                if s == 30:
                    pe.wait_ge(k_ready, 1)
                    keys(0, 1, 7)
                if s == 32:
                    fold_keys(0, 6)

            with pe.Fori(0, LOOP) as i:
                tile(i, 0)
            tile(LOOP, REST)

            def stay_warm(bank, n):
                for _ in range(n):
                    pe.matmul(ps[:, bank, :], w1g_h[:], w1_h[:, 0:512], start=True, stop=True)

            pe.wait_ge(h2w_free, 2 + (TILES - 1) * P // SF)
            last_layer(1, 0, range(HT - 1))
            fold_keys(1, 3)
            make_values(0)
            pe.wait_ge(h2w_free, 2 + NSTEP)
            last_layer(1, 0, range(HT - 1, HT))
            pe.wait_ge(kb_ready, 1)
            pe.wait_ge(h2_ready, NSTEP + 1)
            def scores(a):
                n, k = divmod(a, GT)
                d, par = divmod(n, 2)
                pe.wait_ge(kb_ready, n + 1)
                pe.wait_ge(v_ready, 2 * (d + 1))
                if a >= 2:
                    pe.wait_ge(s_masked, a - 1)
                for q in range(2):
                    at = HC * d + k * P + q * T
                    mm = pe.matmul(ps[q * T:(q + 1) * T, 2 + a % 2, 0:NH * T], qq[:, par, at:at + T],
                                   kb[n % 2][:, k, q, :, :].rearrange("p h s -> p (h s)"),
                                   start=True, stop=True)
                mm.then_inc(s_summed, 1)

            def turn_probs(a):
                pe.wait_ge(exp_ready, a + 1)
                if a >= 2:
                    pe.wait_ge(pt_ready, a - 1)
                for kv in range(NKV):
                    mm = pe.transpose(ps[:, 4 + a % 2, kv * P:(kv + 1) * P], pr[:, a % 2, kv * P:(kv + 1) * P], ident)
                mm.then_inc(pt_turned, 1)

            def values(a):
                n, k = divmod(a, GT)
                d, par = divmod(n, 2)
                pe.wait_ge(pt_ready, a + 1)
                for q in range(2):
                    for kv in range(NKV):
                        at = ((((d * HP + k) * 2 + q) * 2 + par) * NKV + kv) * 2 * VW
                        o = (k * NKV + kv) * 2 * VW
                        mm = pe.matmul(ps[q * T:(q + 1) * T, par, o:o + 2 * VW],
                                       pt[:, a % 2, kv * P + q * T:kv * P + (q + 1) * T], vb[:, at:at + 2 * VW],
                                       start=True, stop=True)
                mm.then_inc(pv_summed, 1)

            def attend(d, k):
                a = HT * d + k
                if k < HT:
                    scores(a)
                if 2 <= k <= HT + 1:
                    turn_probs(a - 2)
                if k >= 3:
                    values(a - 3)

            def turn_y(d):
                if d == 0:
                    pe.wait_ge(h_new_ready, 2)
                pe.wait_ge(y_ready, 2 * (d + 1))
                turn_pairs(y_tok, 7, d, y_turned)

            def project_y(d):
                pe.wait_ge(y_ch, d + 1)
                for p in range(HP):
                    mm = pe.matmul(ps[:, 7, p * P:(p + 1) * P], n_ch[:, column(d, p)], w("bd_wo"),
                                   start=True, stop=True)
                mm.then_inc(wo_summed, 1)

            pe.wait_ge(wh_ready, 1)
            stay_warm(6, WARM[0])
            turn_norm(0, 1)
            mixer_xc(1)
            mixer_z(1)
            attend(0, 0)
            turn_xc(1)
            attend(0, 1)
            running_sums(1)
            attend(0, 2)
            mixer_out(1)
            attend(0, 3)
            attend(0, 4)
            stay_warm(7, WARM[1])
            turn_norm(1, 1)
            attend(0, 5)
            fc1(1, 0)
            fc1(1, 1)
            fc1(1, 2)
            fc1(1, 3)
            attend(0, 6)
            attend(0, 7)
            fc2(1)
            attend(0, 8)
            attend(0, 9)
            attend(0, 10)
            stay_warm(6, WARM[2])
            turn_norm(2, 1)
            turn_y(0)
            pe.wait_ge(pt_ready, HT)
            for par in range(2):
                queries(1, par, par)
                keys(1, par, 4 + par)
            fold_keys(2, 0)
            make_values(1)
            fold_keys(3, 1)
            project_y(0)
            def turn_tokens(n):
                pe.wait_ge(norm_ready, 6 + n // 2 + 1)
                if n:
                    pe.wait_ge(f_ready, n)
                if n == 2:
                    pe.wait_ge(lg_ready, 1)
                for k in range(GT):
                    mm = pe.transpose(ps[:, 6, k * P:(k + 1) * P],
                                      n_twice[:, GT * n + k, :, :].rearrange("p a c -> p (a c)"), ident)
                mm.then_inc(f_turned, 1)

            def router(d):
                pe.wait_ge(f_ready, 2 * (d + 1))
                for j in range(HT * d, HT * (d + 1)):
                    mm = pe.matmul(ps[:, 6, j * NE:(j + 1) * NE], f_r[:, j * P:(j + 1) * P].bitcast(F32),
                                   w("router"), start=True, stop=True)
                mm.then_inc(lg_summed, 1)

            def up(k, step, cols):
                b = step % NHB
                rows = block_of_hidden(b)[0]
                for bank, hi, lo, done, free in ((0, w1_h, w1_l, e1_summed, silu_ready),
                                                 (2, w3_h, w3_l, e3_summed, hh_ready)):
                    if free is not None and step >= 2:
                        pe.wait_ge(free, k - 1)
                    o = ps[0:rows, bank + step % 2, 0:CT]
                    part = slice(b * P, b * P + rows)
                    pe.matmul(o, hi[:, part], f_r[:, cols], start=True, stop=False)
                    pe.matmul(o, lo[:, part], f_r[:, cols], start=False, stop=True).then_inc(done, 1)

            def down(k, step, i):
                c, b = divmod(step, NHB)
                rows, e, ne = block_of_hidden(b)
                pe.wait_ge(hh_ready, k + 1)
                if b == 0:
                    pe.wait_ge(eo_free, 2 * (i * 2 + c + 1))
                for t in range(CHUNK):
                    mm = pe.matmul(ps[:, 4 + CHUNK * c + t, e * C:(e + ne) * C], hh[0:rows, b, t * P:(t + 1) * P],
                                   m("w2", rows)[:, b * 2 * C:(b * 2 + ne) * C], start=(b == 0),
                                   stop=(b == NHB - 1), skip_group_check=True)
                if b == NHB - 1:
                    mm.then_inc(eo_summed, 1)

            for k in range(HT + 3):
                attend(1, k)
                if k == 3:
                    turn_tokens(0)
                if k == 5:
                    turn_tokens(1)
                if k == 7:
                    router(0)
            pe.wait_ge(x4_ready, 1)
            turn_y(1)
            pe.wait_ge(wl_ready, 2)
            up(0, 0, slice(0, CT))
            up(1, 1, slice(0, CT))
            project_y(1)
            up(2, 2, slice(0, CT))

            def beside_experts(s):
                if s == 2:
                    turn_tokens(2)
                if s == 4:
                    turn_tokens(3)
                if s == 7:
                    router(1)
                if s == NHB - 1:
                    pe.wait_ge(lg_ready, 3)
                    pe.wait_ge(x4_ready, 2)

            def two_chunks(i, last, first=False):
                for step in range(2 * NHB):
                    ahead = step + LAG
                    if not (last and ahead >= 2 * NHB):
                        at = (i * 2 + ahead // NHB) * CT
                        up(i * 2 * NHB + ahead, ahead, slice(at, at + CT) if last else bass.ds(at, CT))
                    down(i * 2 * NHB + step, step, i)
                    if first:
                        beside_experts(step)

            two_chunks(0, False, True)
            with pe.Fori(1, TILES // (2 * CHUNK) - 1) as i:
                two_chunks(i, False)
            two_chunks(TILES // (2 * CHUNK) - 1, True)

        @block.scalar
        def _(act):
            def gx_copy(j):
                act.wait_ge(gx_summed, j + 1)
                act.activation(gx_parts[:, 0, :, :].rearrange("f c v -> f (c v)"), gx_ps,
                               ACT.Copy).then_inc(gx_part0, 1)

            def g_copy(k, par):
                for v in range(2):
                    act.wait_ge(g_summed, 2 * k + v + 1)
                    act.activation(gh[:, par, v * HALF:(v + 1) * HALF], g_ps[:, v, :], ACT.Copy).then_inc(g_high, 1)

            def h1_relu(k, par):
                act.wait_ge(h1_summed, 2 * k + 1)
                act.activation(h1[:, par, 0:BLOCKS // 2, :].rearrange("v k c -> v (k c)"), h1_ps[:, 0, :],
                               ACT.Relu).then_inc(h1_ready[0], 1)

            def h1_relu_rest(k, par):
                act.wait_ge(h1_summed, 2 * k + 2)
                act.activation(h1[:, par, BLOCKS // 2:, :].rearrange("v k c -> v (k c)"), h1_ps[:, 1, :],
                               ACT.Relu).then_inc(h1_ready[1], 1)

            def h2_relu(k, par):
                act.wait_ge(h2_summed, k + 1)
                act.wait_ge(h2_free, k + 1)
                act.activation(split(h2[:, par, :], 2), h2_ps, ACT.Relu, bias=c1[:, 0:1],
                               scale=bn_t[:, 1, C1:C1 + 1]).then_inc(h2_ready, 1)

            guesses = [0]

            def rsqrt_guess(t):
                guesses[0] += 1
                act.wait_ge(inverse_ready, guesses[0])
                act.activation(t, t, ACT.Sqrt).then_inc(guess_ready, 1)

            gx_copy(0)
            rsqrt_guess(bn_t[:, 0, :])
            act.wait_ge(gcn_rest_loaded, 16)
            act.activation(w1g_h[:], g("w1"), ACT.Copy).then_inc(w1g_high, 1)
            h1_relu(0, 0)
            g_copy(0, 0)
            h1_relu(1, 1)
            act.wait_ge(bn1_ready, 1)

            def tile(i, steps):
                at = i * STEPS
                for s in range(steps or STEPS):
                    if not steps or s + 2 < steps:
                        h1_relu(at + s + 2, s % 2)
                        if steps and s + 2 >= 4:
                            h1_relu_rest(at + s + 2, s % 2)
                    if not steps or s + 1 < steps:
                        g_copy(at + s + 1, (s + 1) % 2)
                    if steps and s:
                        beside(s - 1)
                    h2_relu(at + s, s % 2)
                    if s % STEPS == 0 and not (steps and s + STEPS > steps):
                        act.wait_ge(rows_stored, 16 * (i + s // STEPS + 1))
                        gx_copy(i + s // STEPS + 1)

            def half(d):
                return slice(HC * d, HC * (d + 1))

            def norm_scale(n, d, scale, bias=None):
                act.wait_ge(norm_turned, n + 3 * d + 1)
                if bias is None:
                    act.activation(n_ch[:, half(d)], ps[:, 6, :], ACT.Copy, scale=scale).then_inc(norm_ch, 1)
                else:
                    act.activation(n_ch[:, half(d)], ps[:, 6, :], ACT.Identity, bias=bias,
                                   scale=scale).then_inc(norm_ch, 1)

            def row_guess(d, norms=1):
                rsqrt_guess(row_t[:, 0, 0:norms, HT * d:HT * (d + 1)])

            def copy_xc(d):
                act.wait_ge(xz_summed, 2 * d + 1)
                act.activation(xc_pad[:, HT * d:HT * (d + 1), 2:T + 2],
                               ps[:, 6, :].rearrange("p (q t) -> p q t", t=T), ACT.Copy).then_inc(xc_copied, 1)

            def silu_z(d):
                act.wait_ge(xz_summed, 2 * d + 2)
                act.activation(z_ch[:, half(d)], ps[:, 6, :], ACT.Silu).then_inc(z_silu, 1)

            def silu_xc(d):
                act.wait_ge(conv_ready, d + 1)
                act.activation(xc_ch[:, half(d)], cv_ch[:, half(d)], ACT.Silu).then_inc(xc_silu, 1)

            def copy_xc_tok(d):
                act.wait_ge(xc_turned, d + 1)
                act.activation(xc_tok[:, HP * d:HP * (d + 1), :].rearrange("p a b -> p (a b)"), ps[:, 6, :],
                               ACT.Copy).then_inc(xc_tok_ready, 1)

            def gelu(d, fb):
                act.wait_ge(fc1_summed, FFB * d + fb + 1)
                act.activation(ff[:, fb, half(d)], ps[:, 7 - fb % 2, :], ACT.Gelu,
                               bias=w("fc1_b")[:, fb:fb + 1]).then_inc(gelu_ready, 1)

            def key_blocks(n, bank):
                act.wait_ge(kf_summed, n + 1)
                if n >= 2:
                    act.wait_ge(s_summed, GT * (n - 1))
                for h in range(NH):
                    a = act.activation(kb[n % 2][:, :, :, h, :].rearrange("p k q s -> p (k q) s"),
                                       split(ps[:, bank, :], 2 * GT), ACT.Copy, scale=w("head")[:, h:h + 1])
                a.then_inc(kb_ready, 1)

            def beside(s):
                if s == 0:
                    act.wait_ge(moe_loaded, 16)
                    act.activation(w1_h[:], m("w1"), ACT.Copy).then_inc(wh_ready, 1)
                if s == 1:
                    act.activation(w3_h[:], m("w3"), ACT.Copy).then_inc(wh_ready, 1)
                    act.wait_ge(tail_loaded, 16)
                if s == 5:
                    row_guess(0, 2)
                if s == 7:
                    norm_scale(0, 0, w("ln1_w"), w("ln1_b"))
                if s == 8:
                    act.wait_ge(pad_zero, 1)
                    copy_xc(0)
                if s == 9:
                    silu_z(0)
                if s == 10:
                    silu_xc(0)
                if s == 11:
                    copy_xc_tok(0)
                if s == 16:
                    row_guess(0)
                if s == 18:
                    norm_scale(1, 0, w("ln2_w"), w("ln2_b"))
                if s == 19:
                    gelu(0, 0)
                if s == 20:
                    gelu(0, 1)
                    gelu(0, 2)
                if s == 21:
                    gelu(0, 3)
                if s == 24:
                    row_guess(0, 2)
                if s == 26:
                    norm_scale(2, 0, w("rms1_w"))
                if s == 34:
                    key_blocks(0, 6)

            with act.Fori(0, LOOP) as i:
                tile(i, 0)
            tile(LOOP, REST)
            beside(REST - 1)

            spread = vb.rearrange("p (n e v) -> p n e v", e=2, v=VW)

            def copy_values(d):
                act.wait_ge(vb_ones, 2)
                act.wait_ge(v_summed, d + 1)
                for a in range(2):
                    rows = slice(a * T, (a + 1) * T)
                    n = HP * 2 * 2 * NKV
                    act.activation(spread[rows, n * d:n * (d + 1), a, 0:HD],
                                   ps[rows, 2, :].rearrange("p (n v) -> p n v", v=HD),
                                   ACT.Copy).then_inc(v_ready, 1)

            def y_copy(d):
                act.wait_ge(y_turned, d + 1)
                act.activation(n_ch[:, half(d)], ps[:, 7, :], ACT.Copy).then_inc(y_ch, 1)

            def attend(d, k):
                a = HT * d + k
                if k < HT:
                    act.wait_ge(s_shifted, a + 1)
                    if a >= 2:
                        act.wait_ge(pt_turned, a - 1)
                    act.activation(pr[:, a % 2, :], sm[:, a % 2, :], ACT.Exp, scale=HD ** -0.5).then_inc(exp_ready, 1)
                if k >= 2:
                    act.wait_ge(pt_turned, a - 1)
                    if a >= 4:
                        act.wait_ge(pv_summed, a - 3)
                    act.activation(pt[:, a % 2, :], ps[:, 4 + a % 2, 0:2 * P], ACT.Copy).then_inc(pt_ready, 1)

            row_guess(1, 2)
            norm_scale(0, 1, w("ln1_w"), w("ln1_b"))
            copy_xc(1)
            key_blocks(1, 3)
            copy_values(0)
            silu_z(1)
            silu_xc(1)
            attend(0, 0)
            copy_xc_tok(1)
            attend(0, 1)
            attend(0, 2)
            attend(0, 3)
            row_guess(1)
            attend(0, 4)
            norm_scale(1, 1, w("ln2_w"), w("ln2_b"))
            attend(0, 5)
            gelu(1, 0)
            gelu(1, 1)
            gelu(1, 2)
            gelu(1, 3)
            attend(0, 6)
            attend(0, 7)
            attend(0, 8)
            attend(0, 9)
            row_guess(1, 2)
            norm_scale(2, 1, w("rms1_w"))
            y_copy(0)
            key_blocks(2, 0)
            copy_values(1)

            def tokens_high(n):
                act.wait_ge(f_turned, n + 1)
                act.activation(f_r[:, n * GT * P:(n + 1) * GT * P], ps[:, 6, :], ACT.Copy,
                               scale=w("rms2_w")).then_inc(f_high, 1)

            def router_exp(d):
                act.wait_ge(lg_ready, 2 * (d + 1))
                act.activation(ep[:, HT * d:HT * (d + 1), :], lg[:, HT * d:HT * (d + 1), :],
                               ACT.Exp).then_inc(lexp_ready, 1)

            for k in range(HT + 2):
                attend(1, k)
                if k == 0:
                    row_guess(0)
                    key_blocks(3, 1)
                if k == 3:
                    tokens_high(0)
                if k == 5:
                    tokens_high(1)
            router_exp(0)
            y_copy(1)

            def silu(k, step):
                rows = block_of_hidden(step % NHB)[0]
                act.wait_ge(e1_summed, k + 1)
                if step >= 2:
                    act.wait_ge(hh_ready, k - 1)
                act.activation(act_h[0:rows, step % 2, :], ps[0:rows, step % 2, 0:CT], ACT.Silu).then_inc(silu_ready, 1)

            silu(0, 0)
            silu(1, 1)
            row_guess(1)
            silu(2, 2)

            def two_chunks(i, last, first=False):
                for ahead in range(LAG, 2 * NHB + (0 if last else LAG)):
                    silu(i * 2 * NHB + ahead, ahead)
                    if first:
                        if ahead == 6:
                            tokens_high(2)
                        if ahead == 8:
                            tokens_high(3)
                        if ahead == 11:
                            router_exp(1)

            two_chunks(0, False, True)
            with act.Fori(1, TILES // (2 * CHUNK) - 1) as i:
                two_chunks(i, False)
            two_chunks(TILES // (2 * CHUNK) - 1, True)

        @block.gpsimd
        def _(pool):
            pool.memset(gxr, 1.0).then_inc(ones_ready, 1)
            pool.memset(xc_pad[:, :, 0:2], 0.0).then_inc(pad_zero, 1)

            def tile(i, steps):
                for s in range(steps):
                    k = i * STEPS + s
                    pool.wait_ge(h2_ready, k + 2)
                    pool.wait_ge(h2w_free, k + 1)
                    pool.tensor_tensor(split(h2w[:, s % 2, :], SF), split(h2[:, s % 2, :], SF),
                                       mean_a[:].rearrange("p (a v) -> p a v", a=1).to_broadcast([P, SF, V]),
                                       ALU.mult).then_inc(h2_free, 1)

            pool.wait_ge(mean_ready, 1)
            pool.nop().then_inc(h2_free, 2)
            pool.nop().then_inc(h2_ready, 1)
            with pool.Fori(0, LOOP) as i:
                tile(i, STEPS)
            tile(LOOP, REST - 1)

            spread = vb.rearrange("p (n e v) -> p n e v", e=2, v=VW)
            pool.wait_ge(h_summed, 2)
            pool.memset(vb, 0.0).then_inc(vb_zero, 1)
            pool.wait_ge(vb_zero, 1)
            for a in range(2):
                pool.memset(spread[a * T:(a + 1) * T, :, a, HD:VW], 1.0).then_inc(vb_ones, 1)
            pool.wait_ge(vb_ones, 2)

            for n, (hi, lo, name) in enumerate(((w1_h, w1_l, "w1"), (w3_h, w3_l, "w3"))):
                pool.wait_ge(wh_ready, n + 1)
                pool.tensor_tensor(lo[:], m(name), hi[:].bitcast(F32), ALU.subtract).then_inc(wl_ready, 1)

            for d in range(2):
                tiles = slice(HT * d, HT * (d + 1))
                pool.wait_ge(x4_ready, d + 1)
                pool.tensor_tensor(h_tok[:, tiles, :], x_new[:, tiles, :], h_new[:, tiles, :],
                                   ALU.add).then_inc(resid_ready, 1)

        @block.vector
        def _(dve):
            chain = [0]

            def link(ins):
                chain[0] += 1
                ins.then_inc(dve_chain, 1)
                dve.wait_ge(dve_chain, chain[0])

            def bcast(ap, n):
                return ap.rearrange("p (a o) -> p a o", o=1).to_broadcast([ap.shape[0], ap.shape[1], n])

            def gx_left_parts(j):
                dve.wait_ge(gx_part0, j + 1)
                part = [gx_parts[:, n, :, :].rearrange("f c v -> f (c v)") for n in range(3)]
                dve.tensor_tensor(gx_rest[:], gx_ps, part[0], ALU.subtract).then_inc(gx_left, 1)
                dve.wait_ge(gx_left, j + 1)
                dve.tensor_copy(part[1], gx_rest[:]).then_inc(gx_part1, 1)
                dve.wait_ge(gx_part1, j + 1)
                dve.tensor_tensor(part[2], gx_rest[:], part[1], ALU.subtract).then_inc(gx_part2, 1)

            dve.wait_ge(gcn_loaded, 16)
            bn0, bn1, bn2 = g("bn0", XR), g("bn1"), g("bn2")
            dve.tensor_scalar(bn_e[:, 0:C1], g("bn0")[:, C1:2 * C1], 1e-5, None, ALU.add)
            dve.tensor_scalar(bn_e[:, C1:C1 + 1], bn1[:, 1:2], 1e-5, None, ALU.add)
            link(dve.tensor_scalar(bn_e[:, C1 + 1:], bn2[:, C:2 * C], 1e-5, None, ALU.add))

            guesses = [0]

            def rsqrt(e, t, invert=True):
                guesses[0] += 1
                if invert:
                    dve.reciprocal(t[:, 0, :], e).then_inc(inverse_ready, 1)
                dve.wait_ge(guess_ready, guesses[0])
                link(dve.tensor_tensor(t[:, 1, :], t[:, 0, :], t[:, 0, :], ALU.mult))
                link(dve.scalar_tensor_tensor(out=t[:, 1, :], in0=t[:, 1, :], scalar=-0.5, in1=e,
                                              op0=ALU.mult, op1=ALU.mult))
                link(dve.scalar_tensor_tensor(out=t[:, 1, :], in0=t[:, 1, :], scalar=1.5, in1=t[:, 0, :],
                                              op0=ALU.add, op1=ALU.mult))

            dve.reciprocal(bn_t[:, 0, :], bn_e[:]).then_inc(inverse_ready, 1)
            gx_left_parts(0)
            rsqrt(bn_e[:], bn_t, False)
            s0, s1, s2 = bn_t[0:XR, 1, 0:C1], bn_t[:, 1, C1:C1 + 1], bn_t[:, 1, C1 + 1:]

            def bn_shift(s, c, bn, n):
                link(dve.tensor_tensor(s, s, bn[:, 0:n], ALU.mult))
                link(dve.tensor_tensor(c, bn[:, 2 * n:3 * n], bn[:, 3 * n:4 * n], ALU.subtract))
                link(dve.tensor_tensor(c, c, s, ALU.mult))
                return dve.tensor_tensor(c, c, bn[:, 4 * n:5 * n], ALU.add)

            link(bn_shift(s0, c0[:], bn0, C1))
            link(dve.tensor_tensor(w0s[:], g("w0", XR), s0, ALU.mult))
            link(dve.scalar_tensor_tensor(out=w0s[:], in0=c0[:], scalar=g("bias_row", XR), in1=w0s[:],
                                          op0=ALU.mult, op1=ALU.add))
            part = g("part", XR)
            left = w0s[:]
            for n in range(2):
                link(dve.tensor_copy(w0_p[:, n, :], left))
                link(dve.tensor_tensor(w0_t[:, n, :], left, w0_p[:, n, :], ALU.subtract))
                left = w0_t[:, n, :]
            link(dve.tensor_scalar(left, left, part[:, 2:3], None, ALU.mult))
            link(dve.scalar_tensor_tensor(out=left, in0=w0_p[:, 1, :], scalar=part[:, 1:2], in1=left,
                                          op0=ALU.mult, op1=ALU.add))
            dve.scalar_tensor_tensor(out=w0_b[:], in0=w0_p[:, 0, :], scalar=part[:, 0:1], in1=left,
                                     op0=ALU.mult, op1=ALU.add).then_inc(w0_ready, 1)
            dve.wait_ge(mean_summed, 1)
            dve.tensor_copy(mean_a[:], ps[:, 0, 0:V]).then_inc(mean_ready, 1)
            bn_shift(s1, c1[:], bn1, 1).then_inc(bn1_ready, 1)
            dve.wait_ge(gcn_rest_loaded, 16)
            dve.wait_ge(w1g_high, 1)
            dve.tensor_tensor(w1g_l[:], g("w1"), w1g_h[:].bitcast(F32), ALU.subtract).then_inc(w1g_low, 1)
            dve.nop().then_inc(h2w_free, 2)

            def g_low_part(k, par):
                for v in range(2):
                    cols = slice(v * HALF, (v + 1) * HALF)
                    dve.wait_ge(g_high, 2 * k + v + 1)
                    dve.tensor_tensor(gl[:, par, cols], g_ps[:, v, :], gh[:, par, cols].bitcast(F32),
                                      ALU.subtract).then_inc(g_ready, 1)

            def h1_relu(k, par):
                dve.wait_ge(h1_summed, 2 * k + 2)
                dve.tensor_scalar(h1[:, par, BLOCKS // 2:, :].rearrange("v k c -> v (k c)"), h1_ps[:, 1, :],
                                  0.0, None, ALU.max).then_inc(h1_ready[1], 1)

            def weigh_last(k, par):
                dve.wait_ge(h2_ready, k + 2)
                dve.wait_ge(h2w_free, k + 1)
                dve.tensor_tensor(split(h2w[:, par, :], SF), split(h2[:, par, :], SF),
                                  mean_a[:].rearrange("p (a v) -> p a v", a=1).to_broadcast([P, SF, V]),
                                  ALU.mult).then_inc(h2_free, 1)

            def vertex_sum(k, par, col):
                dve.wait_ge(h2_free, k + 3)
                dve.tensor_reduce(sums[:, col], split(h2w[:, par, :], SF), AX.X, ALU.add).then_inc(h2w_free, 1)

            for k in range(4):
                h1_relu(k, k % 2)
                if k:
                    g_low_part(k - 1, (k - 1) % 2)

            def tile(i, steps):
                at = i * STEPS
                for s in range(steps or STEPS):
                    if not steps:
                        h1_relu(at + s + 4, s % 2)
                    col = bass.ds(i * GF + s * SF, SF) if not steps else slice(i * GF + s * SF, i * GF + (s + 1) * SF)
                    if s + 1 == steps:
                        weigh_last(at + s, s % 2)
                    vertex_sum(at + s, s % 2, col)
                    if not steps or s + 3 < steps:
                        g_low_part(at + s + 3, (s + 3) % 2)
                    if s == 0:
                        gx_left_parts(i + 1)
                    if steps:
                        beside(s)

            def tiles(t, d):
                return t[:, HT * d:HT * (d + 1), :]

            def tile_cols(t, d):
                return tiles(t, d).rearrange("p j c -> p (j c)")

            def half(t, d):
                return t[:, HC * d:HC * (d + 1)]

            def row(ap):
                return ap.rearrange("p (a c) -> p a c", a=1).to_broadcast([P, HT, C])

            def mean_square(src, d, eps, then=None):
                rows = slice(HT * d, HT * (d + 1))
                link(dve.tensor_tensor(tiles(q_tok, d), src, src, ALU.mult))
                link(dve.tensor_reduce(row_s[:, rows], tiles(q_tok, d), AX.X, ALU.add))
                if then is not None:
                    dve.tensor_scalar(row_v[:, 1, rows], row_s[:, rows], (1.0 + then) / C, eps * then,
                                      ALU.mult, ALU.add)
                link(dve.tensor_scalar(row_v[:, 0, rows], row_s[:, rows], 1.0 / C, eps, ALU.mult, ALU.add))

            def row_rsqrt(d, norms=1, invert=True):
                rows = slice(HT * d, HT * (d + 1))
                rsqrt(row_v[:, 0:norms, rows], row_t[:, :, 0:norms, rows], invert)

            def row_inverse(d, norms=1):
                rows = slice(HT * d, HT * (d + 1))
                dve.reciprocal(row_t[:, 0, 0:norms, rows], row_v[:, 0:norms, rows]).then_inc(inverse_ready, 1)

            def times_row(src, dst, d, norm=0):
                return dve.tensor_tensor(dst, src, bcast(row_t[:, 1, norm, HT * d:HT * (d + 1)], C), ALU.mult)

            def centre(src, d):
                mean = row_a[:, HT * d:HT * (d + 1)]
                link(dve.tensor_reduce(mean, src, AX.X, ALU.add))
                link(dve.tensor_scalar(mean, mean, -1.0 / C, None, ALU.mult))
                link(dve.tensor_tensor(tiles(d_tok, d), src, bcast(mean, C), ALU.add))

            def h_tokens(d, first):
                both = ps[:, first:first + 2, :].rearrange("p b (j a c) -> p (b j) a c", a=2, c=C)
                dve.wait_ge(h_summed, d + 1)
                link(dve.tensor_tensor(tiles(d_tok, d), both[:, :, 1, :], row(c2[:, 1, :]), ALU.add))

            def h_residual(d, first):
                both = ps[:, first:first + 2, :].rearrange("p b (j a c) -> p (b j) a c", a=2, c=C)
                link(dve.tensor_tensor(tiles(h_tok, d), both[:, :, 0, :], row(c2_b[:]), ALU.add))

            def measure(d, eps, then=None):
                mean_square(tiles(d_tok, d), d, eps, then)
                row_inverse(d, 1 if then is None else 2)

            def normalise(d, norms=1):
                row_rsqrt(d, norms, False)
                times_row(tiles(d_tok, d), tiles(n_tok, d), d, norms - 1).then_inc(norm_ready, 1)

            def layer_norm_x(d):
                link(times_row(tiles(d_tok, d), tiles(x_tok, d), d))

            cw = w("conv_w")

            def convolve(d):
                pad = xc_pad[:, HT * d:HT * (d + 1), :]
                cv, c2nd = (half(t, d).rearrange("p (q t) -> p q t", t=T) for t in (cv_ch, cw_ch))
                dve.wait_ge(xc_copied, d + 1)
                link(dve.tensor_scalar(cv, pad[:, :, 2:T + 2], cw[:, 2:3], w("conv_b"), ALU.mult, ALU.add))
                link(dve.scalar_tensor_tensor(out=c2nd, in0=pad[:, :, 1:T + 1], scalar=cw[:, 1:2], in1=cv,
                                              op0=ALU.mult, op1=ALU.add))
                dve.scalar_tensor_tensor(out=cv, in0=pad[:, :, 0:T], scalar=cw[:, 0:1], in1=c2nd,
                                         op0=ALU.mult, op1=ALU.add).then_inc(conv_ready, 1)

            def skip(d):
                dve.wait_ge(xc_silu, d + 1)
                link(dve.tensor_scalar(half(cv_ch, d), half(xc_ch, d), w("ssm_d"), None, ALU.mult))

            def gate_y(d):
                dve.wait_ge(cum_summed, d + 1)
                link(dve.scalar_tensor_tensor(out=half(cv_ch, d), in0=ps[:, 7, :], scalar=bcs[:, 0:1],
                                              in1=half(cv_ch, d), op0=ALU.mult, op1=ALU.add))
                dve.wait_ge(z_silu, d + 1)
                dve.tensor_tensor(half(cw_ch, d), half(cv_ch, d), half(z_ch, d), ALU.mult).then_inc(yz_ready, 1)

            def add_mixer(d):
                dve.wait_ge(mix_summed, d + 1)
                link(dve.tensor_tensor(tile_cols(x_new, d), tile_cols(x_tok, d), ps[:, 6, :], ALU.add))
                centre(tiles(x_new, d), d)

            def add_x(d):
                link(dve.tensor_tensor(tiles(h_tok, d), tiles(h_tok, d), tiles(x_new, d), ALU.add))

            def add_mlp(d):
                dve.wait_ge(fc2_summed, d + 1)
                dve.tensor_tensor(tile_cols(h_new, d), tile_cols(h_tok, d), ps[:, 7, :],
                                  ALU.add).then_inc(h_new_ready, 1)
                dve.wait_ge(h_new_ready, d + 1)
                centre(tiles(h_new, d), d)

            rope = w("rope").rearrange("p (a t) -> p a t", a=1).to_broadcast([P, HP, P])

            def rotate(d, par, keys, bank):
                o, summed, ready = (kk, k_summed, k_ready) if keys else (qq, q_summed, q_ready)
                dve.wait_ge(summed, 2 * d + par + 1)
                dve.tensor_tensor(split(o[:, par, HC * d:HC * (d + 1)], HP), split(ps[:, bank, :], HP), rope,
                                  ALU.mult).then_inc(ready, 1)

            def beside(s):
                if s in (7, 16, 24):
                    gx_left_parts(LOOP + 1 + -(-s // STEPS))
                if s == 0:
                    link(bn_shift(s2, c2[:, 0, :], bn2, C))
                    link(dve.tensor_tensor(w2s[:, 0, :], g("w2"), s2, ALU.mult))
                    for n, t in enumerate((w2s, c2)):
                        link(dve.tensor_reduce(w2m[:, n:n + 1], t[:, 0, :], AX.X, ALU.add))
                        link(dve.scalar_tensor_tensor(out=t[:, 1, :], in0=w2m[:, n:n + 1].to_broadcast([P, C]), scalar=-1.0 / C,
                                                      in1=t[:, 0, :], op0=ALU.mult, op1=ALU.add))
                    dve.nop().then_inc(w2_ready, 1)
                    dve.wait_ge(tail_loaded, 16)
                    link(dve.tensor_tensor(c2_b[:], c2[:, 0, :], w("fc2_b"), ALU.add))
                    link(dve.tensor_tensor(bc[:], w("ssm_b"), w("ssm_c"), ALU.mult))
                    link(dve.tensor_reduce(bcs[:], bc[:], AX.X, ALU.add))
                if s == 2:
                    h_tokens(0, 6)
                    h_residual(0, 6)
                if s == 3:
                    measure(0, 1e-5, 1e-5)
                if s == 4:
                    normalise(0, 2)
                if s == 5:
                    layer_norm_x(0)
                if s == 8:
                    convolve(0)
                if s == 9:
                    skip(0)
                if s == 11:
                    gate_y(0)
                if s == 13:
                    add_mixer(0)
                if s == 14:
                    measure(0, 1e-5)
                if s == 15:
                    normalise(0)
                if s == 17:
                    add_x(0)
                if s == 21:
                    add_mlp(0)
                if s == 22:
                    measure(0, 1e-5, 1e-6)
                if s == 23:
                    normalise(0, 2)
                if s == 24:
                    layer_norm_x(0)
                if 26 <= s < 30:
                    rotate(0, (s - 26) // 2, s % 2, 6 + s % 2)

            with dve.Fori(0, LOOP) as i:
                tile(i, 0)
            tile(LOOP, REST)

            causal = w("causal").rearrange("p (a s) -> p a s", a=1).to_broadcast([P, NH, T])

            def shift(a):
                s = split(sm[:, a % 2, :], NH)
                dve.wait_ge(s_summed, a + 1)
                if a >= 2:
                    dve.wait_ge(exp_ready, a - 1)
                dve.tensor_tensor(s, split(ps[:, 2 + a % 2, 0:NH * T], NH), causal, ALU.add).then_inc(s_masked, 1)
                dve.wait_ge(s_masked, a + 1)
                link(dve.tensor_reduce(mx[:, a % 2, :], s, AX.X, ALU.max))
                dve.tensor_tensor(s, s, bcast(mx[:, a % 2, :], T), ALU.subtract).then_inc(s_shifted, 1)

            def divide(n):
                d, par = divmod(n, 2)
                dve.wait_ge(pv_summed, GT * (n + 1))
                o = ps[:, n % 2, 0:GT * NH * VW].rearrange("p (k h v) -> p k h v", k=GT, h=NH)
                r = rden[:].rearrange("p (k h v) -> p k h v", k=GT, v=1)
                link(dve.reciprocal(r, o[:, :, :, HD:VW]))
                dve.tensor_tensor(y_tok[:, HT * d + par:HT * (d + 1):2, :].rearrange("p k (h v) -> p k h v", h=NH),
                                  o[:, :, :, 0:HD], r.to_broadcast([P, GT, NH, HD]), ALU.mult).then_inc(y_ready, 1)

            def add_attention(d):
                dve.wait_ge(wo_summed, d + 1)
                dve.tensor_tensor(tile_cols(x_new, d), tile_cols(x_tok, d), ps[:, 7, :], ALU.add).then_inc(x4_ready, 1)
                dve.wait_ge(x4_ready, d + 1)
                mean_square(tiles(x_new, d), d, 1e-6)

            def scale_twice(d, invert=True):
                row_rsqrt(d, 1, invert)
                dve.tensor_tensor(n_twice[:, HT * d:HT * (d + 1), :, :],
                                  tiles(x_new, d).rearrange("p j (a c) -> p j a c", a=1).to_broadcast([P, HT, 2, C]),
                                  row_t[:, 1, 0, HT * d:HT * (d + 1)].rearrange("p (j a c) -> p j a c", a=1, c=1)
                                  .to_broadcast([P, HT, 2, C]), ALU.mult).then_inc(norm_ready, 1)

            h_tokens(1, 0)
            measure(1, 1e-5, 1e-5)
            h_residual(1, 0)
            normalise(1, 2)
            layer_norm_x(1)
            convolve(1)
            shift(0)
            skip(1)
            shift(1)
            gate_y(1)
            shift(2)
            add_mixer(1)
            measure(1, 1e-5)
            shift(3)
            shift(4)
            normalise(1)
            shift(5)
            add_x(1)
            shift(6)
            divide(0)
            shift(7)
            add_mlp(1)
            measure(1, 1e-5, 1e-6)
            divide(1)
            normalise(1, 2)
            layer_norm_x(1)
            for par in range(2):
                rotate(1, par, False, par)
                rotate(1, par, True, 4 + par)
            def hidden(k, step):
                b = step % NHB
                rows = block_of_hidden(b)[0]
                dve.wait_ge(silu_ready, k + 1)
                dve.wait_ge(e3_summed, k + 1)
                dve.tensor_tensor(hh[0:rows, b, :], act_h[0:rows, step % 2, :], ps[0:rows, 2 + step % 2, 0:CT],
                                  ALU.mult).then_inc(hh_ready, 1)

            def tokens_low(n):
                cols = slice(n * GT * P, (n + 1) * GT * P)
                dve.wait_ge(f_high, n + 1)
                dve.scalar_tensor_tensor(out=f_r[C:, cols], in0=ps[C:, 6, :], scalar=w("rms2_w", C, P),
                                         in1=f_r[C:, cols].bitcast(F32), op0=ALU.mult,
                                         op1=ALU.subtract).then_inc(f_ready, 1)

            all_expert = w("expert").rearrange("p (j e) -> p j e", e=NE)

            def router_logits(d):
                l, (largest,) = tiles(lg, d), (r_a[:, HT * d:HT * (d + 1)],)
                dve.wait_ge(lg_summed, d + 1)
                dve.tensor_copy(l, ps[:, 6, HT * d * NE:HT * (d + 1) * NE].rearrange("p (j e) -> p j e", e=NE)
                                ).then_inc(lg_ready, 1)
                dve.wait_ge(lg_ready, 2 * d + 1)
                link(dve.tensor_reduce(largest, l, AX.X, ALU.max))
                dve.tensor_tensor(l, l, bcast(largest, NE), ALU.subtract).then_inc(lg_ready, 1)

            def router_softmax(d):
                e = tiles(ep, d)
                a, b = (t[:, HT * d:HT * (d + 1)] for t in (r_a, r_b))
                dve.wait_ge(lexp_ready, d + 1)
                link(dve.tensor_reduce(a, e, AX.X, ALU.add))
                link(dve.reciprocal(b, a))
                link(dve.tensor_tensor(e, e, bcast(b, NE), ALU.mult))

            def first_largest(d, one_hots, values):
                e, t, x = tiles(ep, d), tiles(tmp8, d), tiles(all_expert, d)
                largest, index = (r[:, HT * d:HT * (d + 1)] for r in (values, r_c))
                link(dve.tensor_reduce(largest, e, AX.X, ALU.max))
                link(dve.tensor_tensor(t, e, bcast(largest, NE), ALU.is_equal))
                link(dve.tensor_tensor(t, t, x, ALU.mult))
                link(dve.tensor_reduce(index, t, AX.X, ALU.min))
                link(dve.tensor_tensor(tiles(one_hots, d), x, bcast(index, NE), ALU.is_equal))

            def router_first(d):
                first_largest(d, oh1, r_a)
                link(dve.scalar_tensor_tensor(out=tiles(ep, d), in0=tiles(oh1, d), scalar=-2.0, in1=tiles(ep, d),
                                              op0=ALU.mult, op1=ALU.add))

            def router_second(d):
                first_largest(d, oh2, r_b)

            def router_gates(d):
                a, b, c, e = (t[:, HT * d:HT * (d + 1)] for t in (r_a, r_b, r_c, r_d))
                link(dve.tensor_tensor(c, a, b, ALU.add))
                link(dve.tensor_scalar(c, c, 1e-9, None, ALU.add))
                link(dve.reciprocal(e, c))
                link(dve.tensor_tensor(a, a, e, ALU.mult))
                link(dve.tensor_tensor(b, b, e, ALU.mult))
                o1, o2 = tiles(oh1, d), tiles(oh2, d)
                link(dve.tensor_tensor(o1, o1, bcast(a, NE), ALU.mult))
                link(dve.tensor_tensor(o2, o2, bcast(b, NE), ALU.mult))
                link(dve.tensor_tensor(tiles(gate, d), o1, o2, ALU.add))

            for k in range(HT):
                shift(HT + k)
                if k == 0:
                    add_attention(0)
                    row_inverse(0)
                if k == 1:
                    scale_twice(0, False)
                if k == 3:
                    tokens_low(0)
                if k == 5:
                    tokens_low(1)
                if k == GT + 3:
                    divide(2)
            router_logits(0)
            divide(3)
            router_softmax(0)
            router_first(0)
            router_second(0)
            dve.nop().then_inc(eo_free, 4)
            add_attention(1)
            row_inverse(1)
            hidden(0, 0)
            hidden(1, 1)
            scale_twice(1, False)
            hidden(2, 2)
            hidden(3, 3)
            hidden(4, 4)
            router_gates(0)
            hidden(5, 5)
            tokens_low(2)
            hidden(6, 6)
            dve.wait_ge(resid_ready, 2)

            def weigh(i, c, piece, last):
                n = i * 2 + c
                at = n * CHUNK
                t = piece % CHUNK
                if piece < CHUNK:
                    one = slice(at + t, at + t + 1) if last else bass.ds(at + t, 1)
                    if t == 0:
                        dve.wait_ge(eo_summed, n + 1)
                    dve.tensor_tensor(eo[:, t * NE * C:(t + 1) * NE * C].rearrange("p (t e c) -> p t e c", t=1, e=NE),
                                      ps[:, 4 + CHUNK * c + t:5 + CHUNK * c + t, :].rearrange("p t (e c) -> p t e c", e=NE),
                                      gate[:, one, :].rearrange("p t (e c) -> p t e c", c=1)
                                      .to_broadcast([P, 1, NE, C]), ALU.mult).then_inc(eo_free, 1)
                else:
                    dve.wait_ge(eo_free, 4 + 2 * n + t + 1)
                    dve.tensor_reduce(n_tok[:, CHUNK * c + t:CHUNK * c + t + 1, :],
                                      eo[:, t * NE * C:(t + 1) * NE * C].rearrange("p (t e c) -> p t c e", t=1, e=NE),
                                      AX.X, ALU.add).then_inc(chunk_summed, 1)
                    if t == CHUNK - 1:
                        two = slice(at, at + CHUNK) if last else bass.ds(at, CHUNK)
                        dve.wait_ge(chunk_summed, CHUNK * (n + 1))
                        dve.tensor_tensor(y_tok[:, two, :], n_tok[:, CHUNK * c:CHUNK * (c + 1), :], h_tok[:, two, :],
                                          ALU.add).then_inc(out_ready, 1)

            def two_chunks(i, last, first=False):
                for step in range(2 * NHB):
                    ahead = step + WEIGH_LAG
                    if not (last and ahead >= 2 * NHB):
                        hidden(i * 2 * NHB + ahead, ahead)
                    c, piece = divmod(step - (NHB - 2 * CHUNK), NHB)
                    if 0 <= piece < 2 * CHUNK and c >= 0:
                        weigh(i, c, piece, last)
                    if first:
                        if step == 1:
                            tokens_low(3)
                        if step == 3:
                            router_logits(1)
                        if step == 6:
                            router_softmax(1)
                        if step == 12:
                            router_first(1)
                        if step == 14:
                            router_second(1)
                        if step == 16:
                            router_gates(1)

            two_chunks(0, False, True)
            with dve.Fori(1, TILES // (2 * CHUNK) - 1) as i:
                two_chunks(i, False)
            two_chunks(TILES // (2 * CHUNK) - 1, True)


def layout(inputs):
    f = {k: np.asarray(v) for k, v in inputs.items()}
    tok = lambda n: f["L0_tok_" + n]
    at = lambda n: f["L0_attn_" + n]
    fn = lambda n: f["L0_ffn_" + n]
    bn = lambda i, rows: np.concatenate([np.broadcast_to(tok(f"{n}{i}"), (rows, tok(f"{n}{i}").shape[0]))
                                         for n in ("g", "v", "b", "m", "be")], axis=1)

    def pack(parts, where, width):
        out = np.zeros((P, width), np.float32)
        for name, a in parts.items():
            o, n = where[name]
            out[:a.shape[0], o:o + n] = a.reshape(a.shape[0], n)
        return out

    w0 = np.zeros((XR, C1), np.float32)
    w0[:XR - 3] = np.tile(tok("W0"), (len(PRODUCTS), 1))
    takes = np.concatenate([np.repeat([part for _, part in PRODUCTS], CIN), np.arange(3)])
    mix = np.zeros((BR, 2, 2 * V), np.float32)
    for b in range(2):
        for r in range(b, BR):
            frame, v = divmod(b * (BR - 1) + r, V)
            mix[r, b, (frame - b) * V:(frame - b + 1) * V] = tok("A")[:, v]
    gcn = pack({
        "at": tok("A").T, "a": tok("A"), "w1": tok("W1"), "w2": tok("W2"), "w0": w0,
        "bn0": bn(0, P), "bn2": bn(2, P),
        "bn1": np.stack([tok(f"{n}1") for n in ("g", "v", "b", "m", "be")], axis=1),
        "bias_row": (np.arange(XR) >= XR - 3).astype(np.float32)[:, None],
        "part": (takes[:, None] == np.arange(3)[None, :]).astype(np.float32),
        "mix": mix, "ident": np.eye(P, dtype=np.float32), "mean_v": np.full((V, P), 1.0 / V, np.float32),
    }, GCN_AT, GCN_N)
    x = np.zeros((GTILES * GF, V, CIN), np.float32)
    x[:FRAMES] = f["x"].reshape(FRAMES, V, CIN)
    x = x.reshape(GTILES, GF, V, CIN).transpose(0, 2, 3, 1).reshape(GTILES * V, CIN * GF)

    def diag2(a):
        out = np.zeros((2 * a.shape[0], 2 * a.shape[1]), np.float32)
        out[:a.shape[0], :a.shape[1]] = a
        out[a.shape[0]:, a.shape[1]:] = a
        return out

    def twice(a):
        a = a.reshape(C, -1)
        return np.concatenate([a, a])

    swap = np.concatenate([np.arange(HD // 2, HD), np.arange(HD // 2)])
    wq = fn("wq").reshape(NH, HD, C)
    wk = np.repeat(fn("wk").reshape(NKV, HD, C), NH // NKV, axis=0)
    turned = lambda a: np.concatenate([a.reshape(NH * HD, C), a[:, swap].reshape(NH * HD, C)]).T
    inv_freq = 1.0 / 10000.0 ** (np.arange(0, HD, 2, dtype=np.float32) / HD)
    freqs = np.outer(np.arange(T, dtype=np.float32), inv_freq)
    emb = np.concatenate([freqs, freqs], axis=-1)
    sign = np.where(np.arange(HD) < HD // 2, -1.0, 1.0).astype(np.float32)
    cos, sin = np.cos(emb).T, np.sin(emb).T * sign[:, None]
    rope = np.concatenate([np.tile(cos, (NH, 2)), np.tile(sin, (NH, 2))]).astype(np.float32)
    s, t = np.arange(P)[:, None], np.arange(P)[None, :]
    same = s // T == t // T
    eye = np.eye(C, dtype=np.float32)
    tail = pack({
        "bd_xc": diag2(at("in_proj_w")[:C].T), "bd_z": diag2(at("in_proj_w")[C:].T),
        "bd_out": diag2(at("out_proj_w").T),
        "bd_fc1": np.concatenate([diag2(at("fc1_w")[b * C:(b + 1) * C].T) for b in range(FFB)], axis=1),
        "bd_fc2": np.concatenate([diag2(at("fc2_w")[:, b * C:(b + 1) * C].T) for b in range(FFB)], axis=1),
        "bd_wo": diag2(fn("wo").T),
        "wq": twice(turned(wq)), "wk": twice(turned(wk)), "wv": diag2(fn("wv").T),
        "router": twice(fn("router_w").T),
        "fc2_b": np.broadcast_to(at("fc2_b"), (P, C)),
        "ln1_w": twice(at("ln1_w")), "ln1_b": twice(at("ln1_b")), "conv_w": twice(at("conv_w")),
        "conv_b": twice(at("conv_b")), "ssm_b": twice(at("ssm_B")), "ssm_c": twice(at("ssm_C")),
        "ssm_d": twice(at("ssm_D")), "ln2_w": twice(at("ln2_w")), "ln2_b": twice(at("ln2_b")),
        "fc1_b": np.concatenate([at("fc1_b").reshape(FFB, C).T] * 2),
        "rms1_w": twice(fn("ln1_w")), "rms2_w": twice(fn("ln2_w")),
        "tri": (same & (s <= t)).astype(np.float32),
        "causal": np.where(np.arange(T)[None, :] <= s % T, 0.0, MASKED).astype(np.float32),
        "rope": rope, "fold": np.block([[eye, eye], [eye, eye]]).astype(np.float32),
        "head": (np.arange(P)[:, None] % (NH * HD) // HD == np.arange(NH)[None, :]).astype(np.float32),
        "expert": np.broadcast_to(np.tile(np.arange(NE) - NE, TILES), (P, TILES * NE)).astype(np.float32),
    }, TAIL_AT, TAIL_N)
    up = lambda a: twice(a.reshape(NHID, C).T)
    w2 = np.zeros((P, NHB, 2, C), np.float32)
    for b in range(NHB):
        rows, e, _ = block_of_hidden(b)
        for r in range(rows):
            expert, k = divmod(b * P + r, HID)
            w2[r, b, expert - e] = fn("w2")[expert, :, k]
    moe = pack({
        "w1": up(fn("w1")), "w3": up(fn("w3")),
        "w2": w2,
    }, MOE_AT, MOE_N)
    return {"x": x, "gcn": gcn, "tail": tail, "moe": moe}


def kernel(**inputs):
    import concourse.bacc as bacc
    from concourse.bass_utils import run_bass_kernel_spmd

    nc = bacc.Bacc("TRN2", target_bir_lowering=False, num_devices=1)
    arrays = layout(inputs)
    args = [nc.dram_tensor(k, a.shape, F32, kind="ExternalInput").ap() for k, a in arrays.items()]
    out = nc.dram_tensor("out", (FRAMES, C), F32, kind="ExternalOutput").ap()
    program(nc, *args, out)
    r = run_bass_kernel_spmd(nc, [arrays], core_ids=[0])
    return r.results[0]["out"].reshape(SEQS, T, C)
```
